# Optimizing a Trainium2 kernel written in Bass

```python
import numpy as np
import jax
import jax.numpy as jnp

def _softmax(x, axis=-1):
    return jax.nn.softmax(x, axis=axis)

def _gelu(x):
    return jax.nn.gelu(x, approximate=True)

def _silu(x):
    return jax.nn.silu(x)

def _sigmoid(x):
    return jax.nn.sigmoid(x)

def _layernorm(x, axis=-1, eps=1e-05):
    m = jnp.mean(x, axis=axis, keepdims=True)
    v = jnp.var(x, axis=axis, keepdims=True)
    return (x - m) / jnp.sqrt(v + eps)

def _scatter_add(tgt, idx, src, axis=0):
    return tgt.at[idx].add(src)

def _segment_sum(src, seg, n):
    return jax.ops.segment_sum(src, seg, n)
kernel_name = 'mk_prb_d2_jaxref_r8_ae8c75'

def setup_inputs(seed: int=0):
    np.random.seed(seed)
    _w = jnp.asarray

    def _L0_attn_setup():
        import jax, jax.numpy as jnp
        import numpy as np
        key = jax.random.key(seed)
        ks = jax.random.split(key, 5)
        B, S, D = (1, 512, 256)
        H, Dh = (16, 128)
        scale = 1.0 / np.sqrt(D).astype(np.float32)
        return {'x': jax.random.normal(ks[0], (B, S, D), dtype=jnp.float32), 'W_K': jax.random.normal(ks[1], (H, Dh, D), dtype=jnp.float32) * scale, 'W_Q': jax.random.normal(ks[2], (H, Dh, D), dtype=jnp.float32) * scale, 'W_V': jax.random.normal(ks[3], (H, Dh, D), dtype=jnp.float32) * scale, 'W_O': jax.random.normal(ks[4], (D, H * Dh), dtype=jnp.float32) * scale}
    _L0_attn_in = _L0_attn_setup()

    def _L0_ffn_setup():
        import jax, jax.numpy as jnp
        import numpy as np
        EPS = 1e-06
        Q_B = 128.0

        def layer_norm(x):
            mean = jnp.mean(x, axis=-1, keepdims=True)
            var = jnp.var(x, axis=-1, keepdims=True)
            return (x - mean) / jnp.sqrt(var + EPS)

        def absmax_quant(x):
            gamma = jnp.max(jnp.abs(x), axis=-1, keepdims=True)
            x_hat = jnp.clip(x * Q_B / gamma, -Q_B + EPS, Q_B - EPS)
            return x_hat * gamma / Q_B

        def ternarize_weights(w):
            gamma = jnp.mean(jnp.abs(w))
            return jnp.sign(jnp.round(w / (gamma + EPS))) * gamma

        def bitlinear(x, w):
            xn = layer_norm(x)
            x_hat = xn + jax.lax.stop_gradient(absmax_quant(xn) - xn)
            w_hat = w + jax.lax.stop_gradient(ternarize_weights(w) - w)
            return jnp.einsum('bsd,od->bso', x_hat, w_hat)
        key = jax.random.key(seed)
        k1, k2, k3 = jax.random.split(key, 3)
        B, S, D = (4, 256, 256)
        x = jax.random.normal(k1, (B, S, D), dtype=jnp.float32)
        w_fc = jax.random.normal(k2, (4 * D, D), dtype=jnp.float32) / np.sqrt(D)
        w_proj = jax.random.normal(k3, (D, 4 * D), dtype=jnp.float32) / np.sqrt(4 * D)
        return {'x': x, 'w_fc': w_fc, 'w_proj': w_proj}
    _L0_ffn_in = _L0_ffn_setup()

    def _L1_attn_setup():
        import jax, jax.numpy as jnp
        import numpy as np
        DIM = 256
        HEADS = 16
        HEAD_DIM = DIM // HEADS
        CHUNK = 128
        B, N = (4, 256)

        def _rmsnorm(x, w, eps):
            return x * jax.lax.rsqrt(jnp.mean(x * x, axis=-1, keepdims=True) + eps) * w

        def _weight_quant(w):
            scale = 1.0 / jnp.clip(jnp.mean(jnp.abs(w)), 1e-05, None)
            q = jnp.clip(jnp.round(w * scale), -1.0, 1.0) / scale
            return w + jax.lax.stop_gradient(q - w)

        def _forward(x, qkv_w, qkv_norm_w, proj_w, proj_norm_w, norm_w, s):
            Bb, Nn, C = x.shape
            H, D, T = (HEADS, HEAD_DIM, CHUNK)
            nc = Nn // T
            eps = jnp.finfo(x.dtype).eps
            scale = D ** (-0.5)
            h = _rmsnorm(x, qkv_norm_w, eps)
            qkv = h @ _weight_quant(qkv_w).T
            qkv = qkv.reshape(Bb, Nn, 3, H, D)
            q, k, v = (qkv[:, :, 0], qkv[:, :, 1], qkv[:, :, 2])

            def chunks(t):
                return t.reshape(Bb, nc, T, H, D).transpose(1, 0, 3, 2, 4)
            qc, kc, vc = (chunks(q), chunks(k), chunks(v))
            tt = jnp.arange(T, dtype=x.dtype)
            lam_t = jnp.exp(-s[:, None] * tt)
            lam_rev = jnp.exp(-s[:, None] * (T - tt))
            diff = tt[:, None] - tt[None, :]
            mask = jnp.where(diff >= 0, jnp.exp(-s[:, None, None] * diff), 0.0)
            lam_T = jnp.exp(-s * T)[:, None, None]

            def step(S, qkv_c):
                qi, ki, vi = qkv_c
                scores = jnp.einsum('bhtd,bhsd,hts->bhts', qi, ki, mask)
                intra = jnp.einsum('bhts,bhsd->bhtd', scores, vi)
                cross = jnp.einsum('bhtd,ht,bhde->bhte', qi, lam_t, S)
                o = scale * (intra + cross)
                kv = jnp.einsum('bhtd,ht,bhte->bhde', ki, lam_rev, vi)
                return (lam_T * S + kv, o)
            S0 = jnp.zeros((Bb, H, D, D), x.dtype)
            _, outs = jax.lax.scan(step, S0, (qc, kc, vc))
            out = outs.transpose(1, 0, 3, 2, 4).reshape(Bb, Nn, C)
            out = _rmsnorm(out, norm_w, 1e-06)
            out = _rmsnorm(out, proj_norm_w, eps) @ _weight_quant(proj_w).T
            return out
        key = jax.random.key(seed)
        ks = jax.random.split(key, 3)
        x = jax.random.normal(ks[0], (B, N, DIM), jnp.float32)
        bound = float(1.0 / np.sqrt(DIM))
        qkv_w = jax.random.uniform(ks[1], (3 * DIM, DIM), jnp.float32, -bound, bound)
        proj_w = jax.random.uniform(ks[2], (DIM, DIM), jnp.float32, -bound, bound)
        return {'x': x, 'qkv_w': qkv_w, 'qkv_norm_w': jnp.ones((DIM,), jnp.float32), 'proj_w': proj_w, 'proj_norm_w': jnp.ones((DIM,), jnp.float32), 'norm_w': jnp.ones((DIM,), jnp.float32), 's': jnp.full((HEADS,), 0.02, jnp.float32)}
    _L1_attn_in = _L1_attn_setup()

    def _L1_ffn_setup():
        import jax, jax.numpy as jnp
        import numpy as np
        TOP_K = 8
        NUM_GROUPS = 8
        key = jax.random.key(seed)
        ks = jax.random.split(key, 6)
        T_B, T_S, H, I, E, G = (1, 256, 256, 96, 32, NUM_GROUPS)
        hidden_states = jax.random.normal(ks[0], (T_B, T_S, H), dtype=jnp.float32)
        gate_weight = jax.random.normal(ks[1], (E, H), dtype=jnp.float32) * 0.02
        gate_up_proj = jax.random.normal(ks[2], (E, 2 * I, H), dtype=jnp.float32) * 0.02
        down_proj = jax.random.normal(ks[3], (E, H, I), dtype=jnp.float32) * 0.02
        merge_groups = jax.random.randint(ks[4], (E,), 0, G, dtype=jnp.int64)
        merge_groups = merge_groups.at[:G].set(jnp.arange(G, dtype=jnp.int64))
        dominant_experts = jax.random.randint(ks[5], (G,), 0, E, dtype=jnp.int64)
        return {'hidden_states': hidden_states, 'gate_weight': gate_weight, 'gate_up_proj': gate_up_proj, 'down_proj': down_proj, 'merge_groups': merge_groups, 'dominant_experts': dominant_experts}
    _L1_ffn_in = _L1_ffn_setup()
    _d = {'L0_attn_x': _L0_attn_in['x'], 'L0_attn_W_K': _L0_attn_in['W_K'], 'L0_attn_W_Q': _L0_attn_in['W_Q'], 'L0_attn_W_V': _L0_attn_in['W_V'], 'L0_attn_W_O': _L0_attn_in['W_O'], 'L0_ffn_w_fc': _L0_ffn_in['w_fc'], 'L0_ffn_w_proj': _L0_ffn_in['w_proj'], 'L1_attn_qkv_w': _L1_attn_in['qkv_w'], 'L1_attn_qkv_norm_w': _L1_attn_in['qkv_norm_w'], 'L1_attn_proj_w': _L1_attn_in['proj_w'], 'L1_attn_proj_norm_w': _L1_attn_in['proj_norm_w'], 'L1_attn_norm_w': _L1_attn_in['norm_w'], 'L1_attn_s': _L1_attn_in['s'], 'L1_ffn_gate_weight': _L1_ffn_in['gate_weight'], 'L1_ffn_gate_up_proj': _L1_ffn_in['gate_up_proj'], 'L1_ffn_down_proj': _L1_ffn_in['down_proj'], 'L1_ffn_merge_groups': _L1_ffn_in['merge_groups'], 'L1_ffn_dominant_experts': _L1_ffn_in['dominant_experts']}
    _x0 = _d['L0_attn_x']
    _d['L0_attn_x'] = jax.random.normal(jax.random.fold_in(jax.random.key(seed), 1), (1, 1024, 256), dtype=_x0.dtype)
    del _x0
    return _d

def reference(L0_attn_x, L0_attn_W_K, L0_attn_W_Q, L0_attn_W_V, L0_attn_W_O, L0_ffn_w_fc, L0_ffn_w_proj, L1_attn_qkv_w, L1_attn_qkv_norm_w, L1_attn_proj_w, L1_attn_proj_norm_w, L1_attn_norm_w, L1_attn_s, L1_ffn_gate_weight, L1_ffn_gate_up_proj, L1_ffn_down_proj, L1_ffn_merge_groups, L1_ffn_dominant_experts):

    def _L0_attn_ref(x, W_K, W_Q, W_V, W_O):
        import jax, jax.numpy as jnp
        import numpy as np
        b, pos, d_model = x.shape
        d_head = W_K.shape[1]
        k = jnp.einsum('ihd,bpd->biph', W_K, x)
        q = jnp.einsum('ihd,bpd->biph', W_Q, x)
        v = jnp.einsum('ihd,bpd->biph', W_V, x)
        scores = jnp.einsum('biph,biqh->biqp', k, q)
        mask = jnp.tril(jnp.ones((pos, pos), dtype=x.dtype))
        masked = scores * mask - jnp.float32(10000000000.0) * (1.0 - mask)
        attn = jax.nn.softmax(masked / jnp.sqrt(jnp.float32(d_head)), axis=-1)
        z = jnp.einsum('biqp,biph->biqh', attn, v)
        z_flat = jnp.transpose(z, (0, 2, 1, 3)).reshape(b, pos, -1)
        out = jnp.einsum('df,bqf->bqd', W_O, z_flat)
        return out

    def _L0_ffn_ref(x, w_fc, w_proj):
        import jax, jax.numpy as jnp
        import numpy as np
        EPS = 1e-06
        Q_B = 128.0

        def layer_norm(x):
            mean = jnp.mean(x, axis=-1, keepdims=True)
            var = jnp.var(x, axis=-1, keepdims=True)
            return (x - mean) / jnp.sqrt(var + EPS)

        def absmax_quant(x):
            gamma = jnp.max(jnp.abs(x), axis=-1, keepdims=True)
            x_hat = jnp.clip(x * Q_B / gamma, -Q_B + EPS, Q_B - EPS)
            return x_hat * gamma / Q_B

        def ternarize_weights(w):
            gamma = jnp.mean(jnp.abs(w))
            return jnp.sign(jnp.round(w / (gamma + EPS))) * gamma

        def bitlinear(x, w):
            xn = layer_norm(x)
            x_hat = xn + jax.lax.stop_gradient(absmax_quant(xn) - xn)
            w_hat = w + jax.lax.stop_gradient(ternarize_weights(w) - w)
            return jnp.einsum('bsd,od->bso', x_hat, w_hat)
        h = bitlinear(x, w_fc)
        h = jax.nn.gelu(h, approximate=False)
        return bitlinear(h, w_proj)

    def _L1_attn_ref(x, qkv_w, qkv_norm_w, proj_w, proj_norm_w, norm_w, s):
        import jax, jax.numpy as jnp
        import numpy as np
        DIM = 256
        HEADS = 16
        HEAD_DIM = DIM // HEADS
        CHUNK = 128
        B, N = (4, 256)

        def _rmsnorm(x, w, eps):
            return x * jax.lax.rsqrt(jnp.mean(x * x, axis=-1, keepdims=True) + eps) * w

        def _weight_quant(w):
            scale = 1.0 / jnp.clip(jnp.mean(jnp.abs(w)), 1e-05, None)
            q = jnp.clip(jnp.round(w * scale), -1.0, 1.0) / scale
            return w + jax.lax.stop_gradient(q - w)

        def _forward(x, qkv_w, qkv_norm_w, proj_w, proj_norm_w, norm_w, s):
            Bb, Nn, C = x.shape
            H, D, T = (HEADS, HEAD_DIM, CHUNK)
            nc = Nn // T
            eps = jnp.finfo(x.dtype).eps
            scale = D ** (-0.5)
            h = _rmsnorm(x, qkv_norm_w, eps)
            qkv = h @ _weight_quant(qkv_w).T
            qkv = qkv.reshape(Bb, Nn, 3, H, D)
            q, k, v = (qkv[:, :, 0], qkv[:, :, 1], qkv[:, :, 2])

            def chunks(t):
                return t.reshape(Bb, nc, T, H, D).transpose(1, 0, 3, 2, 4)
            qc, kc, vc = (chunks(q), chunks(k), chunks(v))
            tt = jnp.arange(T, dtype=x.dtype)
            lam_t = jnp.exp(-s[:, None] * tt)
            lam_rev = jnp.exp(-s[:, None] * (T - tt))
            diff = tt[:, None] - tt[None, :]
            mask = jnp.where(diff >= 0, jnp.exp(-s[:, None, None] * diff), 0.0)
            lam_T = jnp.exp(-s * T)[:, None, None]

            def step(S, qkv_c):
                qi, ki, vi = qkv_c
                scores = jnp.einsum('bhtd,bhsd,hts->bhts', qi, ki, mask)
                intra = jnp.einsum('bhts,bhsd->bhtd', scores, vi)
                cross = jnp.einsum('bhtd,ht,bhde->bhte', qi, lam_t, S)
                o = scale * (intra + cross)
                kv = jnp.einsum('bhtd,ht,bhte->bhde', ki, lam_rev, vi)
                return (lam_T * S + kv, o)
            S0 = jnp.zeros((Bb, H, D, D), x.dtype)
            _, outs = jax.lax.scan(step, S0, (qc, kc, vc))
            out = outs.transpose(1, 0, 3, 2, 4).reshape(Bb, Nn, C)
            out = _rmsnorm(out, norm_w, 1e-06)
            out = _rmsnorm(out, proj_norm_w, eps) @ _weight_quant(proj_w).T
            return out
        return _forward(x, qkv_w, qkv_norm_w, proj_w, proj_norm_w, norm_w, s)

    def _L1_ffn_ref(hidden_states, gate_weight, gate_up_proj, down_proj, merge_groups, dominant_experts):
        import jax, jax.numpy as jnp
        import numpy as np
        TOP_K = 8
        NUM_GROUPS = 8
        B, S, H = hidden_states.shape
        G = dominant_experts.shape[0]
        x = hidden_states.reshape(-1, H)
        logits = jnp.einsum('th,eh->te', x, gate_weight)
        probs = jax.nn.softmax(logits.astype(jnp.float32), axis=-1).astype(logits.dtype)
        top_val, top_idx = jax.lax.top_k(probs, TOP_K)
        top_val = top_val / jnp.sum(top_val, axis=-1, keepdims=True)
        sel_group = merge_groups[top_idx]
        onehot = jax.nn.one_hot(sel_group, G, dtype=top_val.dtype)
        w_tg = jnp.einsum('tk,tkg->tg', top_val, onehot)
        gu = gate_up_proj[dominant_experts]
        dn = down_proj[dominant_experts]
        h = jnp.einsum('th,goh->tgo', x, gu)
        gate, up = jnp.split(h, 2, axis=-1)
        act = jax.nn.silu(gate) * up
        y = jnp.einsum('tgi,ghi->tgh', act, dn)
        out = jnp.einsum('tg,tgh->th', w_tg, y)
        return out.reshape(B, S, H)
    x = L0_attn_x
    xn = _layernorm(x, axis=-1)
    x = x + _L0_attn_ref(xn, L0_attn_W_K, L0_attn_W_Q, L0_attn_W_V, L0_attn_W_O) + _L0_ffn_ref(xn, L0_ffn_w_fc, L0_ffn_w_proj)
    xn = _layernorm(x, axis=-1)
    x = x + _L1_attn_ref(xn, L1_attn_qkv_w, L1_attn_qkv_norm_w, L1_attn_proj_w, L1_attn_proj_norm_w, L1_attn_norm_w, L1_attn_s) + _L1_ffn_ref(xn, L1_ffn_gate_weight, L1_ffn_gate_up_proj, L1_ffn_down_proj, L1_ffn_merge_groups, L1_ffn_dominant_experts)
    return x

_drawn_inputs = setup_inputs


def setup_inputs(seed=0):
    import zlib

    import numpy as np

    out = dict(_drawn_inputs(seed))
    spreads = {'L1_attn_qkv_norm_w': (1.0, 0.2),
     'L1_attn_proj_norm_w': (1.0, 0.6),
     'L1_attn_norm_w': (1.0, 0.6),
     'L1_attn_s': (0.019999999552965164, 0.6)}
    factors = {'L1_ffn_gate_weight': 8.0, 'L1_ffn_gate_up_proj': 8.0, 'L1_ffn_down_proj': 8.0}
    for name, (base, spread) in spreads.items():
        noise = np.random.default_rng([zlib.crc32(name.encode()), seed]).standard_normal(out[name].shape)
        drawn = base * np.exp(spread * noise) if base else spread * noise
        out[name] = jnp.asarray(drawn.astype(out[name].dtype))
    for name, factor in factors.items():
        out[name] = (out[name] * factor).astype(out[name].dtype)
    return out
```

```python
from contextlib import ExitStack

import numpy as np

import concourse.bass as bass
from concourse import mybir

F32 = mybir.dt.float32
F32R = mybir.dt.float32r
BF16 = mybir.dt.bfloat16
I32 = mybir.dt.int32
ALU = mybir.AluOpType
ACT = mybir.ActivationFunctionType
AX = mybir.AxisListType

P = 128


class Order:

    def __init__(self, names, act, dve):
        self.names, self.at, self.act, self.dve, a, d = names, {}, {}, {}, 0, 0
        for n, name in enumerate(names):
            a += any(name.startswith(x) for x in act)
            d += any(name.startswith(x) for x in dve)
            self.at[name], self.act[name], self.dve[name] = n, a, d
        self.read_by_dve = {name for name in names if any(name.startswith(x) for x in dve)}
        self.read_by_act = {name for name in names if any(name.startswith(x) for x in act)}
        self.n, self.na, self.nd = len(names), a, d


class Round:

    def __init__(self, order, banks, offset, g, a, d):
        self.order, self.banks, self.offset, self.g, self.a, self.d = order, banks, offset, g, a, d

    def bank(self, name):
        return self.banks[(self.offset + self.order.at[name]) % len(self.banks)]

    def ready(self, name):
        return self.g + self.order.at[name] + 1

    def acted(self, name):
        return self.a + self.order.act[name]

    def read(self, name):
        return self.d + self.order.dve[name]



class Memory:

    def __init__(self, nc, first, last):
        self.nc, self.next, self.last = nc, first, last

    def take(self, name, shape, dt=F32):
        size = 1
        for n in shape[1:]:
            size *= n
        size = (size * (2 if dt == BF16 else 4) + 31) // 32 * 32
        at, self.next = self.next, self.next + size
        assert self.next <= self.last, (name, self.next, self.last)
        return self.nc.alloc_sbuf_tensor_at(name, shape, dt, offset=at)


def transformer_kernel(nc, x, w_k, w_q, w_v, w_o, w_fc, w_proj, qkv_w, qkv_norm_w, proj_w, proj_norm_w, norm_w, decay,
                       gate_w, gate_up, down, merge, dominant, out, dbg=None):
    _, TOK, D = x.shape
    H, DH, _ = w_q.shape
    NT, KT = TOK // P, D // P
    PAIRS = H // 2
    F = w_fc.shape[0]
    FT_ = F // P
    CH = 512
    NCH = TOK // CH
    SCALE = float(DH) ** -0.5
    EPS_LN, EPS_BIT, EPS_F32, EPS_OUT = 1e-5, 1e-6, float(np.finfo(np.float32).eps), 1e-6
    QB = 128.0
    H1, D1 = decay.shape[0], D // decay.shape[0]
    E, I2, _ = gate_up.shape
    I = I2 // 2
    G = dominant.shape[0]
    HALF = H1 // 2

    ctx = ExitStack()
    with ctx:
        def sem(name):
            return ctx.enter_context(nc.semaphore(name))

        first, last_byte = (nc.sbuf_base + 31) // 32 * 32, nc.sbuf_usable_end
        always = Memory(nc, first, last_byte)
        ident = always.take("ident", [P, P])
        ident_b = always.take("ident_b", [P, P], BF16)
        mask_b = always.take("mask_b", [P, P], BF16)
        half = always.take("half", [P, NT])
        ones = always.take("ones", [P, P])
        acc = always.take("acc", [P, NT, D])
        stats = always.take("stats", [P, NT, 6])
        mv = always.take("mv", [P, NT, 2])
        rstd = always.take("rstd", [P, NT])
        rows = always.take("rows", [P, 4, NT])
        absum = always.take("absum", [P, 4])
        gamma = always.take("gamma", [P, 4])
        thr = always.take("thr", [P, 4])
        nthr = always.take("nthr", [P, 4])
        ngamma = always.take("ngamma", [P, 4])
        shared = always.next

        m = Memory(nc, shared, last_byte)
        xnT = [m.take(f"xnT{n}", [P, KT, TOK], F32R) for n in "hl"]
        wraw = {w: m.take(f"raw_{w}", [P, 2, D]) for w in "qkv"}
        wT = {w: [m.take(f"wT_{w}{n}", [P, 2, 2 * P], F32R) for n in "hl"] for w in "qkvo"}
        qT = [[m.take(f"qT{a}{n}", [P, TOK], F32R) for n in "hl"] for a in range(2)]
        kT = [[m.take(f"kT{a}{n}", [P, TOK], F32R) for n in "hl"] for a in range(2)]
        vv = [m.take(f"v{n}", [P, NT, 2 * DH], F32R) for n in "hl"]
        prob = [m.take(f"prob{n}", [P, (NT - n) * P]) for n in range(4)]
        nmax = m.take("nmax", [P, 4])
        rsum = m.take("rsum", [P, 4])
        rinv = m.take("rinv", [P, 4])
        xq_tile = m.take("xq_tile", [P, D])
        fxT = [m.take(f"fxT{n}", [P, KT, P], F32R) for n in "hl"]
        fcT = m.take("fcT", [P, KT, F], F32R)
        prT = m.take("prT", [P, FT_, D], F32R)
        h_place = m.next
        h = m.take("h", [P, F])
        junk = nc.alloc_sbuf_tensor_at("junk", [P, 2 * F], BF16, offset=h_place)
        hT = [m.take(f"hT{n}", [P, FT_, P], F32R) for n in "hl"]
        hstats = m.take("hstats", [P, 2, 6])
        hmv = m.take("hmv", [P, 2])
        hrow = m.take("hrow", [P, 8])
        late = m.next
        pT = [[m.take(f"pT{c}{n}", [P, 4 * (c + 1), CH], F32R) for n in "hl"] for c in range(2)]
        zT = [[m.take(f"zT{a}{n}", [P, TOK], F32R) for n in "hl"] for a in range(2)]
        m0 = Memory(nc, late, m.next)
        xn = m0.take("xn", [P, NT, D])
        xq = m0.take("xq", [P, NT, D])
        raw_fc = m0.take("raw_fc", [P, F // P, D])
        raw_pr = m0.take("raw_pr", [P, KT, F])
        raw_l1 = m0.take("raw_l1", [P, 8, D])
        above = m0.take("above", [P, 2 * F], BF16)
        tern_fc = m0.take("tern_fc", [P, F // P, D], BF16)
        tern_pr = m0.take("tern_pr", [P, KT, F], BF16)
        tern_l1 = m0.take("tern_l1", [P, 8, D], BF16)

        m = Memory(nc, shared, last_byte)
        tern1 = m.take("tern1", [P, 8, D], BF16)
        x2 = m.take("x2", [P, NT, D])
        hq = m.take("hq", [P, NT, D])
        x2T = [m.take(f"x2T{n}", [P, KT, TOK], F32R) for n in "hl"]
        nT = [m.take(f"nT{n}", [P, KT, TOK], F32R) for n in "hl"]
        qkvT = m.take("qkvT", [P, KT, 3 * D], F32R)
        p1T = m.take("p1T", [P, KT, D], F32R)
        q1T = m.take("q1T", [P, 2, TOK])
        qdT = m.take("qdT", [P, 2, TOK])
        k1T = [m.take(f"k1T{n}", [P, 2, TOK]) for n in "eo"]
        causal = m.take("causal", [P, 4, 4, P])
        masked = m.take("masked", [P, 4, 4, P])
        dist = m.take("dist", [P, P])
        qdecay = m.take("qdecay", [P, 2, P])
        blocks = m.take("blocks", [P, P])
        colw = m.take("colw", [P, 16])
        negs_rows = m.take("negs_rows", [P, H1])
        kdecay = m.take("kdecay", [P, H1])
        normw = m.take("normw", [P, D])
        small = m.take("small", [P, 16])
        o1 = m.take("o1", [P, NT, D])
        state = m.take("state", [P, 2, P])
        state_new = m.take("state_new", [P, 2, P])
        kd = m.take("kd", [P, D])
        v1 = m.take("v1", [P, D])
        st_n = [m.take(f"st_n{n}", [P, KT, P], F32R) for n in "hl"]
        st_k = [m.take(f"st_k{n}", [P, 2, P]) for n in "eo"]
        st_q = m.take("st_q", [P, 2, P])
        st_qd = m.take("st_qd", [P, 2, P])
        graw = m.take("graw", [E, D])
        gT = [m.take(f"gT{n}", [P, KT, E], F32R) for n in "hl"]
        lg = m.take("lg", [P, NT, E])
        pb = m.take("pb", [P, NT, E])
        sel = m.take("sel", [P, NT, 2, E])
        top = m.take("top", [P, NT, 8])
        gs = m.take("gs", [P, 4, NT])
        selT = m.take("selT", [2 * E, TOK], F32R)
        mg_i = m.take("mg_i", [2 * E, 1], I32)
        mg_f = m.take("mg_f", [2 * E, 1])
        iota_g = m.take("iota_g", [2 * E, G])
        onehot = m.take("onehot", [2 * E, G, I])
        st_hot = m.take("st_hot", [2 * E, I], F32R)
        dom = m.take("dom", [1, G], I32)
        raw_gu = m.take("raw_gu", [I, 2, D])
        raw_dn = m.take("raw_dn", [P, 2, I])
        guT = [m.take(f"guT{n}", [P, KT, 2, I], F32R) for n in "hl"]
        dnT = [m.take(f"dnT{n}", [I, D], F32R) for n in "hl"]
        silu = m.take("silu", [I, 2, CH])
        actv = m.take("actv", [I, 2, CH])
        aT = [m.take(f"aT{n}", [I, 2, CH], F32R) for n in "hl"]
        zero_b = m.take("zero_b", [1, CH], BF16)

        xq_dram = nc.dram_tensor("xq_scratch", [P, NT, D], F32)
        tern_dram = nc.dram_tensor("tern_scratch", [P, 8, D], BF16)

        sc = [ctx.enter_context(nc.psum_tensor(f"sc{n}", [P, 2, CH], F32)) for n in range(2)]
        tp = [ctx.enter_context(nc.psum_tensor(f"tp{n}", [P, CH], F32)) for n in range(2)]
        gp = [ctx.enter_context(nc.psum_tensor(f"gp{n}", [P, CH], F32)) for n in range(2)]

        S = {name: sem(name) for name in (
            "x_in raws_in q_in kv_in o_in xq_in spill const_pool consts1 dve_step pool_step xn_done absum_done "
            "tern_done xq_done zero_done s_ready max_done exp_done rcp_done pn_done t_ready t_hi t_lo g_ready g_hi g_lo "
            "ffn_step ffn_pow l1_in sems_in tern_in gu_in dn_in r_ready r_act r_dve sums_done hq_done x2_done sel_done "
            "prep_done staged decays masks_done decay_in pb_done xvar_done pool_waits dve_waits state_done a_hi a_lo ma_done "
            "post_step y_done out_done").split()}
        (x_in, raws_in, q_in, kv_in, o_in, xq_in, spill, const_pool, consts1, dve_step, pool_step, xn_done,
         absum_done, tern_done, xq_done, zero_done, s_ready, max_done, exp_done, rcp_done, pn_done, t_ready, t_hi, t_lo,
         g_ready, g_hi, g_lo, ffn_step, ffn_pow, l1_in, sems_in, tern_in, gu_in, dn_in, r_ready, r_act, r_dve, sums_done,
         hq_done, x2_done, sel_done, prep_done, staged, decays, masks_done, decay_in, pb_done, xvar_done, pool_waits, dve_waits, state_done, a_hi,
         a_lo, ma_done, post_step, y_done, out_done) = S.values()

        XT = [f"XT{c}" for c in range(2 * NCH)]
        QK = [f"{w}{a}{c}" for a in range(2) for w in "QK" for c in range(NCH)]
        V4 = [f"V{n}" for n in range(4)]
        T8 = [f"T{n}" for n in range(8)]
        ACT_READS = ("XT", "W", "Q", "K", "V", "AV", "FT", "F0", "F1", "H")
        DVE_READS = ("XT", "W", "Q", "K", "V", "AV", "FT", "H", "GM", "T", "O", "FP")
        START = Order(XT + ["Wq", "Wk", "Wv", "GM"] + QK + V4 + ["Wo"] + T8, ACT_READS, DVE_READS)
        ROUND = Order(["AV01", "AV00", "FT", "AV11", "Wq", "Wk", "Wv", "F0", "F1"] + QK[:2] + ["AV10"] + QK[2:]
                      + ["V0", "V1", "H0", "H1", "V2", "V3", "O0", "O1", "FP", "O2", "O3", "Wo"], ACT_READS, DVE_READS)
        LAST = Order(["AV01", "AV00", "FT", "AV11", "F0", "F1", "AV10", "H0", "H1", "O0", "O1", "FP", "O2", "O3"],
                     ACT_READS, DVE_READS)
        assert ROUND.n % 2 == 0 and LAST.n % 2 == 0
        start = Round(START, gp, 0, 0, 0, 0)

        def attention_round(u):
            last = isinstance(u, int)
            return Round(LAST if last else ROUND, gp, START.n, START.n + u * ROUND.n, START.na + u * ROUND.na,
                         START.nd + u * ROUND.nd)

        last_round = attention_round(PAIRS - 1)
        TILE = [NT - 1 - s % NT for s in range(2 * NT)]
        TG = [0]
        for i in TILE:
            TG.append(TG[-1] + (2 if i >= 4 else 1))
        NTG = TG[-1]
        LAG = 3
        FSTEPS = 11
        L1_LOADS = 3 + 2 * KT + 2

        ring1 = [tp[0], tp[1], gp[0], gp[1]]
        ACT1 = ("GT", "XA", "XB", "QA", "KA", "SL", "WG", "WD", "V", "GA", "OC", "OT")
        DVE1 = ("TQ", "TP", "GT", "XA", "LG", "XB", "QA", "KA", "SL", "WG", "WD", "KV", "UP", "WB", "SC", "ST", "OT", "PO")
        PRE1 = Order(["TQ0", "TQ1", "TQ2", "TP", "GT"] + [f"XA{c}" for c in range(4)] + ["LG"] + [f"XB{c}" for c in range(4)]
                     + [f"{n}{b}{c}" for n in ("QA", "KA") for b in range(2) for c in range(NCH)] + ["SL0", "SL1"], ACT1, DVE1)
        ROUND1 = Order(["WG", "WD", "GA0", "UP0", "WB0", "KV", "V", "SC0", "SC1", "GA1", "UP1", "WB1", "SC2", "SC3",
                        "OC", "ST"], ACT1, DVE1)
        POST1 = Order(["OT0", "OT1", "OT2", "OT3", "PO0", "PO1", "PO2", "PO3"], ACT1, DVE1)
        assert PRE1.n % 4 == 0 and ROUND1.n % 4 == 0
        pre1 = Round(PRE1, ring1, 0, 0, 0, 0)

        def round1(i):
            return Round(ROUND1, ring1, 0, PRE1.n + i * ROUND1.n, PRE1.na + i * ROUND1.na, PRE1.nd + i * ROUND1.nd)

        r8 = round1(G)
        post1 = Round(POST1, ring1, 0, r8.g, r8.a, r8.d)

        block = ctx.enter_context(nc.Block())

        def widths(i):
            n = (i + 1) * P
            if n <= CH:
                return [(0, 0, max(n, 2 * P))]
            return [(0, 0, n // 2), (1, n // 2, n // 2)]

        def score_view(t, i):
            n = (i + 1) * P
            return t[:, 0, 0:n] if n <= CH else t[:, :, 0:n // 2]

        def prob_view(t, i):
            n = (i + 1) * P
            return t[:, 0:n] if n <= CH else t[:, 0:n].rearrange("p (b n) -> p b n", b=2)

        def chunk(t, c):
            return t[:, c * CH:(c + 1) * CH]

        def place(name, halves):
            if name[:2] == "XT":
                c = int(name[2])
                return [t[:, c // NCH, (c % NCH) * CH:(c % NCH + 1) * CH] for t in xnT]
            if name[0] == "W":
                return [t[:] for t in wT[name[1]]]
            if name[:2] == "AV":
                return [chunk(t, int(name[3])) for t in zT[int(name[2])]]
            if name[0] == "Q":
                return [chunk(t, int(name[2])) for t in qT[int(name[1])]]
            if name[0] == "K":
                return [chunk(t, int(name[2])) for t in kT[int(name[1])]]
            if name[0] == "V":
                c = int(name[1])
                return [t[:, 2 * c:2 * c + 2, :] for t in vv]
            if name == "FT":
                return [t[:] for t in fxT]
            if name[0] == "H":
                c = int(name[1])
                return [t[:, 4 * c:4 * c + 4, :] for t in hT]
            raise KeyError(name)

        def as_shape(src, dst):
            n = 1
            for k in dst.shape[1:]:
                n *= k
            s = src[0:dst.shape[0], 0:n]
            return s if len(dst.shape) == 2 else s.rearrange("p (a b) -> p a b", b=dst.shape[2])

        @block.sync
        def _(sp):
            def load_kv(pair):
                for w, src in (("k", w_k), ("v", w_v)):
                    sp.dma_start(wraw[w][:], src[bass.ds(2 * pair, 2)].rearrange("a h d -> h a d")).then_inc(kv_in, 16)

            def load_q(pair):
                sp.dma_start(wraw["q"][:], w_q[bass.ds(2 * pair, 2)].rearrange("a h d -> h a d")).then_inc(q_in, 16)

            def load_o(pair):
                sp.dma_start(wraw["q"][:], w_o.rearrange("(m p) f -> p m f", p=P)[:, :, bass.ds(pair * 2 * DH, 2 * DH)])\
                  .then_inc(o_in, 16)

            def load_xq(t):
                sp.dma_start(xq_tile[:].rearrange("p (a d) -> p a d", a=1), xq_dram.ap()[:, bass.ds(t, 1), :]).then_inc(xq_in, 16)

            sp.dma_start(acc[:], x[0].rearrange("(t p) d -> p t d", p=P)).then_inc(x_in, 16)
            load_q(0)
            load_kv(0)
            sp.dma_start(raw_fc[:], w_fc.rearrange("(t p) d -> p t d", p=P)).then_inc(raws_in, 16)
            sp.dma_start(raw_pr[:], w_proj.rearrange("(t p) f -> p t f", p=P)).then_inc(raws_in, 16)
            sp.dma_start(raw_l1[:, 0:6, :], qkv_w.rearrange("(t p) d -> p t d", p=P)).then_inc(raws_in, 16)
            sp.dma_start(raw_l1[:, 6:8, :], proj_w.rearrange("(t p) d -> p t d", p=P)).then_inc(raws_in, 16)
            sp.wait_ge(g_ready, start.ready("Wq"))
            load_o(0)
            sp.wait_ge(g_ready, start.ready("Wv"))
            load_kv(1)
            sp.wait_ge(tern_done, 3)
            sp.dma_start(tern_dram.ap(), tern_l1[:]).then_inc(spill, 16)
            sp.wait_ge(xq_done, 1)
            sp.dma_start(xq_dram.ap(), xq[:]).then_inc(spill, 16)
            sp.wait_ge(g_ready, start.ready("Wo"))
            load_q(1)
            sp.wait_ge(spill, 32)
            load_xq(0)

            def prefetch(u, r, more):
                sp.wait_ge(g_ready, r.ready("FT"))
                load_xq(u + 1)
                sp.wait_ge(g_ready, r.ready("Wq"))
                load_o(u + 1)
                if more:
                    sp.wait_ge(g_ready, r.ready("Wv"))
                    load_kv(u + 2)
                    sp.wait_ge(g_ready, r.ready("Wo"))
                    load_q(u + 2)

            with sp.Fori(0, PAIRS - 2) as u:
                prefetch(u, attention_round(u), True)
            u = PAIRS - 2
            prefetch(u, Round(ROUND, gp, START.n, START.n + u * ROUND.n, 0, 0), False)

            sp.wait_ge(g_ready, last_round.ready("O3"))
            sp.wait_ge(g_lo, last_round.read("O3"))
            sp.dma_start(tern1[:], tern_dram.ap()).then_inc(tern_in, 16)
            sp.dma_start(graw[:], gate_w).then_inc(l1_in, 16)
            sp.dma_start(normw[:], norm_w.partition_broadcast(P)).then_inc(l1_in, 16)
            sp.dma_start(negs_rows[:], decay.partition_broadcast(P)).then_inc(l1_in, 16)
            for k in range(KT):
                for c, v in ((0, qkv_norm_w), (2, proj_norm_w)):
                    sp.dma_start(colw[:, c + k:c + k + 1], v[k * P:(k + 1) * P].rearrange("(p a) -> p a", a=1)).then_inc(l1_in, 16)
            for n in range(2):
                sp.dma_start(mg_i[n * E:(n + 1) * E, :], merge.rearrange("(e a) -> e a", a=1)).then_inc(l1_in, 16)
            sp.dma_start(dom[:], dominant.rearrange("(a g) -> a g", a=1)).then_inc(sems_in, 16)
            sp.wait_ge(sems_in, 16)

            def load_expert(i):
                e = sp.value_load(dom[0:1, bass.ds(i, 1)], min_val=0, max_val=E - 1)
                sp.dma_start(raw_gu[:], gate_up[bass.ds(e, 1)].rearrange("a (m i) d -> (a i) m d", m=2)).then_inc(gu_in, 16)
                sp.dma_start(raw_dn[:], down[bass.ds(e, 1)].rearrange("a (m p) i -> (a p) m i", p=P)).then_inc(dn_in, 16)

            load_expert(0)
            with sp.Fori(0, G - 1) as i:
                sp.wait_ge(r_ready, round1(i).ready("WD"))
                load_expert(i + 1)
            for t in range(NT):
                if t % 2 == 0:
                    sp.wait_ge(r_dve, post1.read(f"PO{t // 2}"))
                sp.dma_start(out[0].rearrange("(t p) d -> p t d", p=P)[:, t, :], acc[:, t, :]).then_inc(out_done, 16)
            sp.wait_ge(out_done, 16 * NT)

        @block.gpsimd
        def _(pool):
            n = [0]

            def link(ins):
                n[0] += 1
                ins.then_inc(pool_step, 1)
                pool.wait_ge(pool_step, n[0])

            link(nc.gpsimd.memset(ident[:], 0.0))
            link(nc.gpsimd.affine_select(out=ident[:], in_=ident[:], compare_op=ALU.not_equal, fill=1.0, base=0,
                                         pattern=[[-1, P]], channel_multiplier=1))
            link(nc.gpsimd.memset(mask_b[:], 0.0))
            link(nc.gpsimd.affine_select(out=mask_b[:], in_=mask_b[:], compare_op=ALU.is_ge, fill=-1e10, base=0,
                                         pattern=[[-1, P]], channel_multiplier=1))
            link(nc.gpsimd.tensor_copy(ident_b[:], ident[:]))
            link(nc.gpsimd.memset(half[:], -0.5))
            nc.gpsimd.memset(ones[:], 1.0).then_inc(const_pool, 1)
            pool.wait_ge(dve_step, 2 * NT + 1)
            nc.gpsimd.tensor_tensor(rstd[:], rstd[:], half[:], ALU.pow).then_inc(const_pool, 1)
            pool.wait_ge(xvar_done, 1)
            nc.gpsimd.tensor_tensor(rows[:, 0, :], rows[:, 0, :], half[:], ALU.pow).then_inc(const_pool, 1)
            pool.wait_ge(g_lo, start.read("T7"))
            pool.wait_ge(spill, 32)
            for n_ in range(2):
                nc.gpsimd.memset(pT[1][n_][:, 7, 2 * P:3 * P].bitcast(F32), 0.0).then_inc(zero_done, 1)
                nc.gpsimd.memset(pT[0][n_][:, 3, 2 * P:3 * P].bitcast(F32), 0.0).then_inc(zero_done, 1)

            def normalise(u, s):
                pool.wait_ge(rcp_done, 2 * NT * u + s + 1)
                pool.sem_inc(pool_waits, 1)
                w = (TILE[s] + 1) * P
                nc.gpsimd.tensor_scalar(prob[s % 4][:, 0:w], prob[s % 4][:, 0:w], rinv[:, s % 4:s % 4 + 1], 1.0,
                                        ALU.mult, ALU.mult).then_inc(pn_done, 1)

            with pool.Fori(0, PAIRS) as u:
                for s in range(2 * NT):
                    normalise(u, s)
                pool.wait_ge(ffn_step, FSTEPS * u + 4)
                nc.gpsimd.tensor_tensor(hrow[:, 0:1], hrow[:, 0:1], half[:, 0:1], ALU.pow).then_inc(ffn_pow, 1)

            pool.wait_ge(g_lo, last_round.read("O3"))
            link(nc.gpsimd.iota(dist[:], pattern=[[1, P]], base=0, channel_multiplier=-1, allow_small_or_imprecise_dtypes=True))
            link(nc.gpsimd.iota(small[:, 0:1], pattern=[[1, 1]], base=P, channel_multiplier=-1, allow_small_or_imprecise_dtypes=True))
            link(nc.gpsimd.iota(qdecay[:], pattern=[[0, 2], [1, P]], base=0, channel_multiplier=0, allow_small_or_imprecise_dtypes=True))
            link(nc.gpsimd.iota(iota_g[:], pattern=[[1, G]], base=0, channel_multiplier=0, allow_small_or_imprecise_dtypes=True))
            link(nc.gpsimd.memset(zero_b[:], 0.0))
            nc.gpsimd.memset(state[:], 0.0).then_inc(state_done, 2)
            link(nc.gpsimd.memset(blocks[:], 1.0))
            bv = blocks[:].rearrange("p (g d) -> p g d", d=D1)
            link(nc.gpsimd.affine_select(out=bv, in_=bv, compare_op=ALU.is_ge, fill=0.0, base=0,
                                         pattern=[[-D1, HALF], [0, D1]], channel_multiplier=1))
            link(nc.gpsimd.affine_select(out=bv, in_=bv, compare_op=ALU.is_ge, fill=0.0, base=D1 - 1,
                                         pattern=[[D1, HALF], [0, D1]], channel_multiplier=-1))
            nc.gpsimd.memset(top[:], 0.0).then_inc(consts1, 1)
            for k in range(2):
                pool.wait_ge(post_step, k + 1)
                nc.gpsimd.tensor_tensor(rows[:, k, :], rows[:, k, :], half[:], ALU.pow).then_inc(sums_done, 1)
            pool.wait_ge(masks_done, 1)
            cz = causal[:].rearrange("p a b t -> p (a b) t")
            nc.gpsimd.affine_select(out=cz, in_=cz, compare_op=ALU.is_ge, fill=0.0, base=0,
                                    pattern=[[0, H1], [1, P]], channel_multiplier=-1).then_inc(prep_done, 1)

            pool.wait_ge(r_dve, pre1.read("SL1"))
            pool.wait_ge(sel_done, 2)
            with pool.Fori(0, G) as i:
                r = round1(i)
                pool.wait_ge(r_ready, r.g)
                tok = bass.ds(i * P, P)
                for n_ in range(2):
                    nc.gpsimd.tensor_copy(st_n[n_][:], nT[n_][:, :, tok].bitcast(F32)).then_inc(staged, 1)
                for n_ in range(2):
                    nc.gpsimd.tensor_copy(st_k[n_][:], k1T[n_][:, :, tok]).then_inc(staged, 1)
                nc.gpsimd.tensor_copy(st_q[:], q1T[:, :, tok]).then_inc(staged, 1)
                nc.gpsimd.tensor_copy(st_qd[:], qdT[:, :, tok]).then_inc(staged, 1)
                nc.gpsimd.tensor_copy(st_hot[:].rearrange("e (a i) -> e a i", a=1), onehot[:, bass.ds(i, 1), :]).then_inc(staged, 1)
            for k in range(2):
                pool.wait_ge(y_done, k + 1)
                nc.gpsimd.tensor_tensor(rows[:, 2 + k, :], rows[:, 2 + k, :], half[:], ALU.pow).then_inc(sums_done, 1)

        @block.scalar
        def _(act):
            def high(names, r):
                for name in names:
                    act.wait_ge(g_ready, r.ready(name))
                    if name in ("F0", "F1"):
                        c = int(name[1])
                        nc.scalar.activation(chunk(h, c), r.bank(name)[:], ACT.Gelu, scale=ngamma[:, 0:1]).then_inc(g_hi, 1)
                        continue
                    dst = place(name, 0)[0]
                    nc.scalar.activation(dst, as_shape(r.bank(name), dst), ACT.Copy,
                                         scale=SCALE if name[0] == "Q" else 1.0).then_inc(g_hi, 1)

            def exp(u, s):
                act.wait_ge(max_done, 2 * NT * u + s + 1)
                if s >= 4:
                    act.wait_ge(t_ready, NTG * u + TG[s - 3])
                nc.scalar.activation(prob_view(prob[s % 4], TILE[s]), score_view(sc[s % 2], TILE[s]), ACT.Exp,
                                     bias=nmax[:, s % 4:s % 4 + 1], accum_out=rsum[:, s % 4:s % 4 + 1]).then_inc(exp_done, 1)

            def high_p(u, s):
                i = TILE[s]
                for b in range(TG[s + 1] - TG[s]):
                    w = min(4, i + 1 - 4 * b)
                    act.wait_ge(t_ready, NTG * u + TG[s] + b + 1)
                    q = (i % 4) * P
                    nc.scalar.activation(pT[i // 4][0][:, 4 * b:4 * b + w, q:q + P],
                                         tp[(TG[s] + b) % 2][:, 0:w * P].rearrange("p (j q) -> p j q", q=P),
                                         ACT.Copy).then_inc(t_hi, 1)

            def heads(u, r):
                for s in range(2 * NT):
                    if s >= LAG:
                        high_p(u, s - LAG)
                    exp(u, s)
                    if s == 7:
                        high(["AV01"], r)
                    if s == 11:
                        high(["AV00"], r)
                    if s == 12:
                        high(["FT"], r)
                high(["AV11"], r)

            act.wait_ge(raws_in, 64)
            for k, t in enumerate((raw_fc[:], raw_pr[:], raw_l1[:, 0:6, :], raw_l1[:, 6:8, :])):
                w = t.shape[1] * t.shape[2]
                if k:
                    act.wait_ge(absum_done, k)
                nc.scalar.activation(junk[:, 0:w].rearrange("p (a b) -> p a b", b=t.shape[2]), t, ACT.Abs,
                                     accum_out=absum[:, k:k + 1]).then_inc(absum_done, 1)
            act.wait_ge(const_pool, 1)
            high([x_ for x_ in START.names if x_ in START.act and x_[:2] not in ("GM",) and x_[0] != "T"], start)
            act.wait_ge(spill, 32)
            act.wait_ge(zero_done, 4)
            with act.Fori(0, PAIRS - 1) as u:
                r = attention_round(u)
                heads(u, r)
                for w, s in (("q", 13), ("k", 14), ("v", 15)):
                    high(["W" + w], r)
                    high_p(u, s)
                high(["F0", "F1"] + QK[:2] + ["AV10"] + QK[2:] + ["V0", "V1", "H0", "H1", "V2", "V3", "Wo"], r)
            u, r = PAIRS - 1, last_round
            heads(u, r)
            for s in (13, 14, 15):
                high_p(u, s)
            high(["F0", "F1", "AV10", "H0", "H1"], r)

            act.wait_ge(g_lo, last_round.read("O3"))
            act.wait_ge(l1_in, 16 * L1_LOADS)
            act.wait_ge(consts1, 1)
            act.wait_ge(decay_in, 1)
            for b in range(2):
                nc.scalar.activation(qdecay[:, b, :], qdecay[:, b, :], ACT.Exp, scale=colw[:, 6 + b:7 + b]).then_inc(decays, 1)
            nc.scalar.activation(kdecay[:], negs_rows[:], ACT.Exp, scale=small[:, 0:1]).then_inc(decays, 1)
            nc.scalar.activation(colw[:, 8:10], colw[:, 6:8], ACT.Exp, scale=float(P)).then_inc(decays, 1)
            for a in range(4):
                for b in range(2):
                    for c in range(2):
                        hh = HALF * b + 2 * a + c
                        last = nc.scalar.activation(causal[:, a, 2 * b + c, :], dist[:], ACT.Exp, scale=negs_rows[:, hh:hh + 1])
            last.then_inc(masks_done, 1)

            def high1(name, r):
                act.wait_ge(r_ready, r.ready(name))
                src = r.bank(name)
                if name == "GT":
                    d, scale = gT[0][:], 1.0
                elif name[:2] in ("XA", "XB"):
                    c = int(name[2])
                    k = c // NCH
                    d = (x2T if name[1] == "A" else nT)[0][:, k, (c % NCH) * CH:(c % NCH + 1) * CH]
                    scale = 1.0 if name[1] == "A" else colw[:, k:k + 1]
                elif name[:2] == "QA":
                    d, scale = q1T[:, int(name[2]), int(name[3]) * CH:(int(name[3]) + 1) * CH], ngamma[:, 2:3]
                elif name[:2] == "KA":
                    d, scale = k1T[0][:, int(name[2]), int(name[3]) * CH:(int(name[3]) + 1) * CH], colw[:, 12:13]
                elif name[:2] == "SL":
                    d, scale = chunk(selT, int(name[2])), 1.0
                elif name == "WG":
                    d, scale = guT[0][:].rearrange("p k m i -> p k (m i)"), 1.0
                elif name == "WD":
                    d, scale = dnT[0][:], 1.0
                else:
                    c = int(name[2])
                    k = c // NCH
                    d, scale = nT[0][:, k, (c % NCH) * CH:(c % NCH + 1) * CH], colw[:, 2 + k:3 + k]
                nc.scalar.activation(d, as_shape(src, d), ACT.Copy, scale=scale).then_inc(r_act, 1)

            for name in PRE1.names:
                if name == "LG":
                    continue
                if name[:2] == "QA" and name == "QA00":
                    act.wait_ge(sel_done, 1)
                    nc.scalar.activation(pb[:], lg[:], ACT.Exp).then_inc(pb_done, 1)
                if any(name.startswith(v) for v in ACT1):
                    high1(name, pre1)

            with act.Fori(0, G) as i:
                r = round1(i)
                high1("WG", r)
                high1("WD", r)
                for c in range(2):
                    name = f"GA{c}"
                    act.wait_ge(r_ready, r.ready(name))
                    act.wait_ge(r_dve, r.d - ROUND1.nd + ROUND1.dve[f"UP{c}"])
                    nc.scalar.activation(silu[:, c, :], r.bank(name)[0:I, :], ACT.Silu).then_inc(r_act, 1)
                    if c == 0:
                        act.wait_ge(r_ready, r.ready("V"))
                        nc.scalar.activation(v1[:], r.bank("V")[:, 0:D], ACT.Copy, scale=ngamma[:, 2:3]).then_inc(r_act, 1)
                    act.wait_ge(r_dve, r.read(f"WB{c}"))
                    act.wait_ge(ma_done, 2 * i + c + 1)
                    nc.scalar.activation(aT[0][:, c, :], actv[:, c, :], ACT.Copy).then_inc(a_hi, 1)
                act.wait_ge(r_ready, r.ready("OC"))
                nc.scalar.activation(o1[:, bass.ds(i, 1), :].rearrange("p a d -> p (a d)"), r.bank("OC")[:, 0:D], ACT.Copy, scale=float(D1) ** -0.5)\
                  .then_inc(r_act, 1)
            act.wait_ge(staged, 7 * G)
            for k in range(4):
                high1(f"OT{k}", post1)

        @block.vector
        def _(dve):
            n = [0]

            def link(ins, wait=True):
                n[0] += 1
                ins.then_inc(dve_step, 1)
                if wait:
                    dve.wait_ge(dve_step, n[0])

            def settle():
                dve.wait_ge(dve_step, n[0])

            def layer_stats(src):
                for t in range(NT):
                    link(nc.vector.bn_stats(stats[:, t, :], src[:, t, :]), False)
                settle()
                for t in range(NT):
                    link(nc.vector.bn_aggr(mv[:, t, :], stats[:, t, :]), False)
                settle()

            dve.wait_ge(x_in, 16)
            layer_stats(acc)
            link(nc.vector.tensor_scalar(rstd[:], mv[:, :, 1], EPS_LN, None, ALU.add))
            dve.wait_ge(const_pool, 2)
            for t in range(NT):
                nc.vector.tensor_scalar(xn[:, t, :], acc[:, t, :], mv[:, t, 0:1], rstd[:, t:t + 1],
                                        ALU.subtract, ALU.mult).then_inc(xn_done, 1)

            def low(names, r):
                for name in names:
                    bank = r.bank(name)
                    if name[0] == "T":
                        c = int(name[1])
                        dve.wait_ge(g_ready, r.ready(name))
                        dst = fcT[:, :, 2 * c * P:2 * (c + 1) * P] if c < 4 else prT[:, 2 * (c - 4):2 * (c - 4) + 2, :]
                        nc.vector.tensor_copy(dst, bank[:].bitcast(BF16)[:, 0:CH].rearrange("p (a b) -> p a b", a=2)).then_inc(g_lo, 1)
                    elif name == "GM":
                        dve.wait_ge(g_ready, r.ready(name))
                        link(nc.vector.tensor_scalar(gamma[:, 0:2], bank[:, 0:2], 1.0 / (F * D), None, ALU.mult))
                        link(nc.vector.tensor_scalar(gamma[:, 2:3], bank[:, 2:3], 1.0 / (3 * D * D), 1e-5, ALU.mult, ALU.max))
                        n[0] += 0
                        nc.vector.tensor_scalar(gamma[:, 3:4], bank[:, 3:4], 1.0 / (D * D), 1e-5, ALU.mult, ALU.max).then_inc(g_lo, 1)
                        dve.wait_ge(g_lo, r.read(name))
                        link(nc.vector.tensor_scalar(thr[:, 0:2], gamma[:, 0:2], EPS_BIT, 0.5, ALU.add, ALU.mult))
                        link(nc.vector.tensor_scalar(thr[:, 2:4], gamma[:, 2:4], 0.5, None, ALU.mult))
                        link(nc.vector.tensor_scalar(nthr[:], thr[:], -1.0, None, ALU.mult))
                        link(nc.vector.tensor_scalar(ngamma[:], gamma[:], -1.0, None, ALU.mult))
                    elif name[0] == "O":
                        c = int(name[1])
                        dve.wait_ge(g_ready, r.ready(name))
                        a = acc[:, 2 * c:2 * c + 2, :]
                        nc.vector.tensor_tensor(a, bank[:].rearrange("p (a b) -> p a b", b=D), a, ALU.add).then_inc(g_lo, 1)
                    else:
                        dve.wait_ge(g_hi, r.acted(name))
                        hi, lo = place(name, 0)
                        if name[0] == "Q":
                            nc.vector.scalar_tensor_tensor(out=lo, in0=as_shape(bank, lo), scalar=SCALE, in1=hi.bitcast(F32),
                                                           op0=ALU.mult, op1=ALU.subtract).then_inc(g_lo, 1)
                        else:
                            nc.vector.tensor_tensor(lo, as_shape(bank, lo), hi.bitcast(F32), ALU.subtract).then_inc(g_lo, 1)

            def tern(k, dst, src, w, sig):
                a = above[:, 0:w].rearrange("p (a b) -> p a b", b=src.shape[2])
                link(nc.vector.tensor_scalar(a, src, thr[:, k:k + 1], None, ALU.is_gt))
                ins = nc.vector.scalar_tensor_tensor(out=dst, in0=src, scalar=nthr[:, k:k + 1], in1=a, op0=ALU.is_lt,
                                                     op1=ALU.subtract)
                link(ins)
                if sig:
                    nc.vector.memset(hrow[:, 7:8], 0.0).then_inc(tern_done, 1)

            def piece(k):
                if k == 0:
                    tern(0, tern_fc[:], raw_fc[:], 2 * F, True)
                elif k == 2:
                    tern(1, tern_pr[:], raw_pr[:], 2 * F, True)
                elif k == 4:
                    tern(2, tern_l1[:, 0:6, :], raw_l1[:, 0:6, :], 6 * D, False)
                elif k == 5:
                    tern(3, tern_l1[:, 6:8, :], raw_l1[:, 6:8, :], 2 * D, True)
                elif k == 6:
                    layer_stats(xn)
                    nc.vector.tensor_scalar(rows[:, 0, :], mv[:, :, 1], EPS_BIT, None, ALU.add).then_inc(xvar_done, 1)
                elif k == 8:
                    dve.wait_ge(const_pool, 3)
                    for t in range(NT):
                        link(nc.vector.tensor_scalar(xq[:, t, :], xn[:, t, :], mv[:, t, 0:1], rows[:, 0, t:t + 1],
                                                     ALU.subtract, ALU.mult), False)
                    settle()
                elif k == 9:
                    link(nc.vector.tensor_reduce(rows[:, 1, :], xq[:], AX.X, ALU.max, apply_absolute_value=True))
                    link(nc.vector.reciprocal(rows[:, 2, :], rows[:, 1, :]))
                    link(nc.vector.tensor_scalar(rows[:, 2, :], rows[:, 2, :], QB, None, ALU.mult))
                    link(nc.vector.tensor_scalar(rows[:, 1, :], rows[:, 1, :], 1.0 / QB, None, ALU.mult))
                elif k == 10:
                    for t in range(NT):
                        link(nc.vector.tensor_scalar(xq[:, t, :], xq[:, t, :], rows[:, 2, t:t + 1], QB, ALU.mult, ALU.min), False)
                    settle()
                elif k == 11:
                    for t in range(NT):
                        link(nc.vector.tensor_scalar(xq[:, t, :], xq[:, t, :], -QB, rows[:, 1, t:t + 1], ALU.max, ALU.mult), False)
                    settle()
                    nc.vector.memset(hrow[:, 6:7], 0.0).then_inc(xq_done, 1)

            low(XT + ["Wq", "Wk", "Wv", "GM"], start)
            for k, name in enumerate(QK + V4):
                low([name], start)
                piece(k)
            low(["Wo"] + T8, start)
            dve.wait_ge(spill, 32)
            dve.wait_ge(zero_done, 4)

            def row_max(u, s):
                dve.wait_ge(s_ready, 2 * NT * u + s + 1)
                i = TILE[s]
                nc.vector.tensor_reduce(nmax[:, s % 4:s % 4 + 1], score_view(sc[s % 2], i), AX.X if i < 4 else AX.XY,
                                        ALU.max, negate=True).then_inc(max_done, 1)

            def recip(u, s):
                dve.wait_ge(exp_done, 2 * NT * u + s + 1)
                nc.vector.reciprocal(rinv[:, s % 4:s % 4 + 1], rsum[:, s % 4:s % 4 + 1]).then_inc(rcp_done, 1)

            def low_p(u, s):
                i = TILE[s]
                for b in range(TG[s + 1] - TG[s]):
                    w = min(4, i + 1 - 4 * b)
                    dve.wait_ge(t_hi, NTG * u + TG[s] + b + 1)
                    q = (i % 4) * P
                    nc.vector.tensor_tensor(pT[i // 4][1][:, 4 * b:4 * b + w, q:q + P],
                                            tp[(TG[s] + b) % 2][:, 0:w * P].rearrange("p (j q) -> p j q", q=P),
                                            pT[i // 4][0][:, 4 * b:4 * b + w, q:q + P].bitcast(F32),
                                            ALU.subtract).then_inc(t_lo, 1)

            def heads(u, r):
                for s in range(2 * NT):
                    row_max(u, s)
                    if s >= LAG:
                        low_p(u, s - LAG)
                    if s >= 1:
                        recip(u, s - 1)
                    if s == 7:
                        low(["AV01"], r)
                    if s == 11:
                        low(["AV00"], r)
                    if s == 12:
                        low(["FT"], r)
                recip(u, 2 * NT - 1)
                low(["AV11"], r)

            def ffn(u, r, k):
                def did(ins, k):
                    ins.then_inc(ffn_step, 1)

                def after(k):
                    dve.wait_ge(ffn_step, FSTEPS * u + k)

                if k == 0:
                    dve.wait_ge(g_hi, r.acted("F1"))
                    for c in range(2):
                        did(nc.vector.bn_stats(hstats[:, c, :], chunk(h, c)), 1 + c)
                    after(2)
                    dve.sem_inc(dve_waits, 1)
                    did(nc.vector.bn_aggr(hmv[:], hstats[:].rearrange("p a b -> p (a b)")), 3)
                    after(3)
                    did(nc.vector.tensor_scalar(hrow[:, 0:1], hmv[:, 1:2], EPS_BIT, None, ALU.add), 4)
                elif k == 1:
                    dve.wait_ge(ffn_pow, u + 1)
                    did(nc.vector.tensor_scalar(h[:], h[:], hmv[:, 0:1], hrow[:, 0:1], ALU.subtract, ALU.mult), 5)
                elif k == 2:
                    after(5)
                    did(nc.vector.tensor_reduce(hrow[:, 1:2], h[:], AX.X, ALU.max, apply_absolute_value=True), 6)
                    after(6)
                    did(nc.vector.reciprocal(hrow[:, 2:3], hrow[:, 1:2]), 7)
                    after(7)
                    did(nc.vector.tensor_scalar(hrow[:, 3:4], hrow[:, 2:3], QB, None, ALU.mult), 8)
                    did(nc.vector.tensor_scalar(hrow[:, 4:5], hrow[:, 1:2], 1.0 / QB, None, ALU.mult), 9)
                elif k == 3:
                    after(9)
                    did(nc.vector.tensor_scalar(h[:], h[:], hrow[:, 3:4], QB, ALU.mult, ALU.min), 10)
                    after(10)
                    did(nc.vector.tensor_scalar(h[:], h[:], -QB, hrow[:, 4:5], ALU.max, ALU.mult), 11)

            def ffn_out(u, r):
                dve.wait_ge(g_ready, r.ready("FP"))
                dve.wait_ge(g_lo, r.read("FP") - 1)
                a = acc[:, bass.ds(u, 1), :].rearrange("p a d -> p (a d)")
                nc.vector.scalar_tensor_tensor(out=a, in0=r.bank("FP")[:, 0:D], scalar=ngamma[:, 1:2], in1=a, op0=ALU.mult,
                                               op1=ALU.add).then_inc(g_lo, 1)
                dve.wait_ge(g_lo, r.read("FP"))

            with dve.Fori(0, PAIRS - 1) as u:
                r = attention_round(u)
                heads(u, r)
                for w, s in (("q", 13), ("k", 14), ("v", 15)):
                    low(["W" + w], r)
                    low_p(u, s)
                ffn(u, r, 0)
                low(QK[:2], r)
                ffn(u, r, 1)
                low(["AV10"], r)
                ffn(u, r, 2)
                low(QK[2:4], r)
                ffn(u, r, 3)
                low(QK[4:] + ["V0", "V1", "H0", "H1", "V2", "V3", "O0", "O1"], r)
                ffn_out(u, r)
                low(["O2", "O3", "Wo"], r)
            u, r = PAIRS - 1, last_round
            heads(u, r)
            for s in (13, 14, 15):
                low_p(u, s)
            ffn(u, r, 0)
            low(["AV10"], r)
            for k in (1, 2, 3):
                ffn(u, r, k)
            low(["H0", "H1", "O0", "O1"], r)
            ffn_out(u, r)
            low(["O2", "O3"], r)
            dve.wait_ge(g_lo, last_round.read("O3"))

            dve.wait_ge(l1_in, 16 * L1_LOADS)
            dve.wait_ge(consts1, 1)
            link(nc.vector.tensor_scalar(negs_rows[:], negs_rows[:], -1.0, None, ALU.mult))
            for b in range(2):
                link(nc.vector.scalar_tensor_tensor(out=small[:, 8:8 + HALF], in0=blocks[:].rearrange("p (g d) -> p g d", d=D1)[:, :, 0],
                                                    scalar=1.0, in1=negs_rows[:, b * HALF:(b + 1) * HALF], op0=ALU.mult,
                                                    op1=ALU.mult, accum_out=colw[:, 6 + b:7 + b]))
            pairs = blocks[:].rearrange("p (g c d) -> p c g d", c=2, d=D1)
            for c in range(2):
                link(nc.vector.tensor_reduce(small[:, 1 + c:2 + c], pairs[:, c, :, 0], AX.X, ALU.add))
                link(nc.vector.tensor_scalar(colw[:, 12 + c:13 + c], small[:, 1 + c:2 + c], ngamma[:, 2:3], None, ALU.mult))
            nc.vector.memset(small[:, 4:5], 0.0).then_inc(decay_in, 1)
            layer_stats(acc)
            nc.vector.tensor_scalar(rows[:, 0, :], mv[:, :, 1], EPS_LN, None, ALU.add).then_inc(post_step, 1)
            dve.wait_ge(sums_done, 1)
            for t in range(NT):
                nc.vector.tensor_scalar(x2[:, t, :], acc[:, t, :], mv[:, t, 0:1], rows[:, 0, t:t + 1],
                                        ALU.subtract, ALU.mult).then_inc(x2_done, 1)
            dve.wait_ge(x2_done, NT)

            def squares(src, junk_, k):
                for t in range(NT):
                    link(nc.vector.scalar_tensor_tensor(out=junk_[:, t, :], in0=src[:, t, :], scalar=1.0, in1=src[:, t, :],
                                                        op0=ALU.mult, op1=ALU.mult, accum_out=rows[:, k, t:t + 1]), False)
                settle()

            squares(x2, hq, 1)
            nc.vector.tensor_scalar(rows[:, 1, :], rows[:, 1, :], 1.0 / D, EPS_F32, ALU.mult, ALU.add).then_inc(post_step, 1)
            link(nc.vector.tensor_copy(mg_f[:], mg_i[:]))
            link(nc.vector.tensor_scalar(onehot[:], iota_g[:].rearrange("e (g a) -> e g a", a=1).to_broadcast([2 * E, G, I]),
                                         mg_f[:, 0:1], None, ALU.is_equal))
            dve.wait_ge(sums_done, 2)
            for t in range(NT):
                nc.vector.tensor_scalar(hq[:, t, :], x2[:, t, :], rows[:, 1, t:t + 1], None, ALU.mult).then_inc(hq_done, 1)

            def low1(name, r):
                src = r.bank(name)
                if name in r.order.read_by_act:
                    dve.wait_ge(r_act, r.acted(name))
                else:
                    dve.wait_ge(r_ready, r.ready(name))
                def minus(hi, lo, scale=None):
                    s_ = as_shape(src, lo)
                    if scale is None:
                        return nc.vector.tensor_tensor(lo, s_, hi.bitcast(F32), ALU.subtract)
                    return nc.vector.scalar_tensor_tensor(out=lo, in0=s_, scalar=scale, in1=hi.bitcast(F32), op0=ALU.mult,
                                                          op1=ALU.subtract)
                if name[0] == "T":
                    s_ = src[:].bitcast(BF16)[:, 0:CH].rearrange("p (a b) -> p a b", a=2)
                    ins = nc.vector.tensor_copy(p1T[:] if name == "TP" else
                                                qkvT[:, :, int(name[2]) * 2 * P:(int(name[2]) + 1) * 2 * P], s_)
                elif name == "GT":
                    ins = minus(gT[0][:], gT[1][:])
                elif name[:2] in ("XA", "XB", "OT"):
                    c = int(name[2])
                    k = c // NCH
                    hi, lo = [v[:, k, (c % NCH) * CH:(c % NCH + 1) * CH] for v in (x2T if name[1] == "A" else nT)]
                    ins = minus(hi, lo, None if name[1] == "A" else colw[:, k:k + 1] if name[1] == "B" else colw[:, 2 + k:3 + k])
                elif name == "LG":
                    s_ = src[:, 0:NT * E].rearrange("p (t e) -> p t e", e=E)
                    link(nc.vector.tensor_reduce(gs[:, 0, :], s_, AX.X, ALU.max))
                    ins = nc.vector.tensor_tensor(lg[:], s_, gs[:, 0, :].rearrange("p (t a) -> p t a", a=1).to_broadcast([P, NT, E]),
                                                  ALU.subtract)
                elif name[:2] == "QA":
                    b, c = int(name[2]), int(name[3])
                    dve.wait_ge(decays, 4)
                    ins = nc.vector.scalar_tensor_tensor(
                        out=qdT[:, b, c * CH:(c + 1) * CH].rearrange("p (c t) -> p c t", t=P),
                        in0=src[:].rearrange("p (c t) -> p c t", t=P), scalar=ngamma[:, 2:3],
                        in1=qdecay[:, b:b + 1, :].to_broadcast([P, CH // P, P]), op0=ALU.mult, op1=ALU.mult)
                elif name[:2] == "KA":
                    b, c = int(name[2]), int(name[3])
                    ins = nc.vector.tensor_scalar(k1T[1][:, b, c * CH:(c + 1) * CH], src[:], colw[:, 13:14], None, ALU.mult)
                elif name[:2] == "SL":
                    c = int(name[2])
                    ins = nc.vector.tensor_tensor(selT[E:2 * E, c * CH:(c + 1) * CH], src[E:2 * E, :],
                                                  selT[E:2 * E, c * CH:(c + 1) * CH].bitcast(F32), ALU.subtract)
                elif name == "WG":
                    ins = minus(guT[0][:].rearrange("p k m i -> p k (m i)"), guT[1][:].rearrange("p k m i -> p k (m i)"))
                elif name == "WD":
                    ins = minus(dnT[0][:], dnT[1][:])
                elif name[:2] == "UP":
                    c = int(name[2])
                    dve.wait_ge(r_act, r.acted(f"GA{c}"))
                    ins = nc.vector.tensor_tensor(actv[:, c, :], src[0:I, :], silu[:, c, :], ALU.mult)
                elif name[:2] == "WB":
                    c = int(name[2])
                    dve.wait_ge(r_dve, r.read(name) - 1)
                    ins = nc.vector.tensor_tensor(actv[:, c, :], src[0:I, :], actv[:, c, :], ALU.mult)
                elif name == "KV":
                    ins = nc.vector.scalar_tensor_tensor(
                        out=kd[:].rearrange("p (h d) -> p h d", d=D1), in0=src[:, 0:D].rearrange("p (h d) -> p h d", d=D1),
                        scalar=ngamma[:, 2:3], in1=kdecay[:].rearrange("p (h a) -> p h a", a=1).to_broadcast([P, H1, D1]),
                        op0=ALU.mult, op1=ALU.mult)
                elif name[:2] == "SC":
                    k = int(name[2])
                    ins = nc.vector.tensor_tensor(masked[:, k, :, :], src[:].rearrange("p (h t) -> p h t", t=P),
                                                  causal[:, k, :, :], ALU.mult)
                elif name == "ST":
                    ins = nc.vector.tensor_tensor(state_new[:], src[:, 0:2 * P].rearrange("p (b f) -> p b f", b=2),
                                                  blocks[:].rearrange("p (a f) -> p a f", a=1).to_broadcast([P, 2, P]), ALU.mult)
                elif name[:2] == "PO":
                    c = int(name[2])
                    a = acc[:, 2 * c:2 * c + 2, :]
                    ins = nc.vector.scalar_tensor_tensor(out=a, in0=src[:].rearrange("p (a b) -> p a b", b=D),
                                                         scalar=ngamma[:, 3:4], in1=a, op0=ALU.mult, op1=ALU.add)
                ins.then_inc(r_dve, 1)

            for name in PRE1.names:
                if name in PRE1.read_by_dve:
                    low1(name, pre1)
                if name == "LG":
                    dve.wait_ge(r_dve, pre1.read("LG"))
                    nc.vector.memset(small[:, 5:6], 0.0).then_inc(sel_done, 1)
                if name == "XB3":
                    def over_experts(v):
                        return v.rearrange("p (t a) -> p t a", a=1).to_broadcast([P, NT, E])

                    dve.wait_ge(pb_done, 1)
                    link(nc.vector.tensor_reduce(gs[:, 1, :], pb[:], AX.X, ALU.add))
                    link(nc.vector.reciprocal(gs[:, 2, :], gs[:, 1, :]))
                    link(nc.vector.tensor_tensor(pb[:], pb[:], over_experts(gs[:, 2, :]), ALU.mult))
                    for t in range(NT):
                        link(nc.vector.max(top[:, t, :], pb[:, t, :]), False)
                    settle()
                    for t in range(NT):
                        link(nc.vector.match_replace(lg[:, t, :], top[:, t, :], pb[:, t, :], 0.0), False)
                    settle()
                    link(nc.vector.tensor_reduce(gs[:, 1, :], top[:], AX.X, ALU.add))
                    link(nc.vector.reciprocal(gs[:, 2, :], gs[:, 1, :]))
                    link(nc.vector.tensor_tensor(sel[:, :, 0, :], pb[:], lg[:], ALU.subtract))
                    link(nc.vector.tensor_tensor(sel[:, :, 0, :], sel[:, :, 0, :], over_experts(gs[:, 2, :]), ALU.mult))
                    nc.vector.tensor_copy(sel[:, :, 1, :], sel[:, :, 0, :]).then_inc(sel_done, 1)
            dve.wait_ge(prep_done, 1)
            with dve.Fori(0, G) as i:
                r = round1(i)
                for name in ROUND1.names:
                    if name in ROUND1.read_by_dve:
                        low1(name, r)
                    if name in ("KV", "SC2"):
                        c = 0 if name == "KV" else 1
                        dve.wait_ge(a_hi, 2 * i + c + 1)
                        nc.vector.tensor_tensor(aT[1][:, c, :], actv[:, c, :], aT[0][:, c, :].bitcast(F32),
                                                ALU.subtract).then_inc(a_lo, 1)
                dve.wait_ge(r_dve, r.read("ST"))
                for b in range(2):
                    nc.vector.scalar_tensor_tensor(out=state[:, b, :], in0=state[:, b, :], scalar=colw[:, 8 + b:9 + b],
                                                   in1=state_new[:, b, :], op0=ALU.mult, op1=ALU.add).then_inc(state_done, 1)
                dve.wait_ge(state_done, 2 * i + 4)

            dve.wait_ge(r_act, r8.a)
            squares(o1, x2, 2)
            nc.vector.tensor_scalar(rows[:, 2, :], rows[:, 2, :], 1.0 / D, EPS_OUT, ALU.mult, ALU.add).then_inc(y_done, 1)
            link(nc.vector.tensor_tensor(o1[:], o1[:], normw[:].rearrange("p (a d) -> p a d", a=1).to_broadcast([P, NT, D]), ALU.mult))
            squares(o1, x2, 3)
            dve.wait_ge(sums_done, 3)
            for _k in range(2):
                link(nc.vector.tensor_tensor(rows[:, 3, :], rows[:, 3, :], rows[:, 2, :], ALU.mult))
            nc.vector.tensor_scalar(rows[:, 3, :], rows[:, 3, :], 1.0 / D, EPS_F32, ALU.mult, ALU.add).then_inc(y_done, 1)
            dve.wait_ge(ma_done, 2 + 2 * G)
            for c in range(4):
                a = acc[:, 2 * c:2 * c + 2, :]
                link(nc.vector.tensor_tensor(a, sc[c // 2][:, c % 2, :].rearrange("p (a d) -> p a d", d=D), a, ALU.add), False)
            settle()
            dve.wait_ge(sums_done, 4)
            link(nc.vector.tensor_tensor(rows[:, 3, :], rows[:, 3, :], rows[:, 2, :], ALU.mult))
            for t in range(NT):
                nc.vector.tensor_scalar(hq[:, t, :], o1[:, t, :], rows[:, 3, t:t + 1], None, ALU.mult).then_inc(hq_done, 1)
            for name in POST1.names:
                low1(name, post1)

        @block.tensor
        def _(pe):
            mm = nc.tensor.matmul

            def free(r, name):
                at, o = r.order.at[name], r.order
                if at >= 2:
                    before = o.names[at - 2]
                    if before in o.read_by_dve:
                        pe.wait_ge(g_lo, r.read(before))
                    else:
                        pe.wait_ge(g_hi, r.acted(before))
                elif r is not start:
                    pe.wait_ge(g_lo, r.d - 1 + at)
                return r.bank(name)

            def three(out, lhs, rhs, start, stop, **kw):
                mm(out, lhs[0], rhs[0], start=start, stop=False, **kw)
                mm(out, lhs[0], rhs[1], start=False, stop=False, **kw)
                return mm(out, lhs[1], rhs[0], start=False, stop=stop, **kw)

            def transposes(g, blocks_, idn, dt=None):
                for k, b in enumerate(blocks_):
                    last = nc.tensor.transpose(g[:, k * P:(k + 1) * P], b, idn)
                return last

            def w_transposes(w, r, pair):
                g = free(r, "W" + w)
                pe.wait_ge(*{"q": (q_in, 16 * (pair + 1)), "o": (o_in, 16 * (pair + 1))}.get(w, (kv_in, 32 * (pair + 1))))
                raw = wraw["q" if w == "o" else w]
                transposes(g, [raw[:, a, k * P:(k + 1) * P] for k in range(2) for a in range(2)], ident[:]).then_inc(g_ready, 1)

            def project(name, r):
                a, c = int(name[1]), int(name[2])
                g = free(r, name)
                w = wT[name[0].lower()]
                if name[1:] == "00":
                    pe.wait_ge(g_lo, r.read("W" + name[0].lower()))
                for k in range(KT):
                    last = three(g[:], [v[:, k, a * P:(a + 1) * P] for v in w],
                                 [v[:, k, c * CH:(c + 1) * CH] for v in xnT], k == 0, k == KT - 1)
                last.then_inc(g_ready, 1)

            def values(name, r):
                c = int(name[1])
                g = free(r, name)
                pe.wait_ge(g_lo, r.read("Wv"))
                for t in range(2):
                    for k in range(KT):
                        last = three(g[:, t * 2 * P:(t + 1) * 2 * P], [v[:, k, (2 * c + t) * P:(2 * c + t + 1) * P] for v in xnT],
                                     [v[:, k, :] for v in wT["v"]], k == 0, k == KT - 1)
                last.then_inc(g_ready, 1)

            def scores(u, s, r):
                a, i = s // NT, TILE[s]
                if s == 0:
                    pe.wait_ge(g_lo, r.d - 12)
                if s >= 2:
                    pe.wait_ge(exp_done, 2 * NT * u + s - 1)
                ql, w = [v[:, i * P:(i + 1) * P] for v in qT[a]], widths(i)
                for b, k0, wd in w:
                    mm(sc[s % 2][:, b, 0:wd], ql[0], kT[a][0][:, k0:k0 + wd], start=True, stop=False)
                    mm(sc[s % 2][:, b, 0:wd], ql[0], kT[a][1][:, k0:k0 + wd], start=False, stop=False)
                b, k0, wd = w[-1]
                mm(sc[s % 2][:, b, i * P - k0:i * P - k0 + P], ident_b[:], mask_b[:], start=False, stop=False)
                for b, k0, wd in w:
                    last = mm(sc[s % 2][:, b, 0:wd], ql[1], kT[a][0][:, k0:k0 + wd], start=False, stop=True)
                last.then_inc(s_ready, 1)

            def p_transposes(u, s):
                pe.wait_ge(pn_done, 2 * NT * u + s + 1)
                i = TILE[s]
                for b in range(TG[s + 1] - TG[s]):
                    k = TG[s] + b
                    if k >= 2:
                        pe.wait_ge(t_lo, NTG * u + k - 1)
                    transposes(tp[k % 2], [prob[s % 4][:, j * P:(j + 1) * P] for j in range(4 * b, min(4 * b + 4, i + 1))],
                               ident[:]).then_inc(t_ready, 1)

            def attend(u, name, r):
                a, c = int(name[2]), int(name[3])
                g = free(r, name)
                pe.wait_ge(t_lo, NTG * u + (TG[NT * a + 4] if c else TG[NT * a + 8]))
                if name == "AV01":
                    pe.wait_ge(g_lo, r.d - 6)
                J = 4 * (c + 1)
                for j in range(J):
                    q = min(max(0, j - 4 * c) * P, 2 * P)
                    last = three(g[:, q:], [v[:, j, a * P:(a + 1) * P] for v in vv], [v[:, j, q:] for v in pT[c]],
                                 j == 0, j == J - 1)
                last.then_inc(g_ready, 1)

            def outputs(name, r):
                c = int(name[1])
                g = free(r, name)
                if c == 0:
                    pe.wait_ge(g_lo, r.read("AV10"))
                for t in range(2):
                    for a in range(2):
                        q = (2 * c + t) * P
                        last = three(g[:, t * 2 * P:(t + 1) * 2 * P], [v[:, q:q + P] for v in zT[a]],
                                     [v[:, a, :] for v in wT["o"]], a == 0, a == 1)
                last.then_inc(g_ready, 1)

            def ffn(name, u, r):
                g = free(r, name)
                if name == "FT":
                    pe.wait_ge(xq_in, 16 * (u + 1))
                    last = transposes(g, [xq_tile[:, k * P:(k + 1) * P] for k in range(KT)], ident[:])
                elif name[0] == "F" and name != "FP":
                    c = int(name[1])
                    pe.wait_ge(g_lo, r.read("FT"))
                    for k in range(KT):
                        for n_ in range(2):
                            last = mm(g[:], fxT[n_][:, k, :], fcT[:, k, c * CH:(c + 1) * CH], start=(k == 0 and n_ == 0),
                                      stop=(k == KT - 1 and n_ == 1))
                elif name[0] == "H":
                    c = int(name[1])
                    pe.wait_ge(ffn_step, FSTEPS * u + FSTEPS)
                    last = transposes(g, [h[:, (4 * c + k) * P:(4 * c + k + 1) * P] for k in range(4)], ident[:])
                else:
                    pe.wait_ge(g_lo, r.read("H1"))
                    for k in range(FT_):
                        for n_ in range(2):
                            last = mm(g[:, 0:D], hT[n_][:, k, :], prT[:, k, :], start=(k == 0 and n_ == 0),
                                      stop=(k == FT_ - 1 and n_ == 1))
                last.then_inc(g_ready, 1)

            def heads(u, r):
                for s in range(2 * NT):
                    scores(u, s, r)
                    if s >= LAG:
                        p_transposes(u, s - LAG)
                    if s == 7:
                        attend(u, "AV01", r)
                    if s == 11:
                        attend(u, "AV00", r)
                    if s == 12:
                        ffn("FT", u, r)
                attend(u, "AV11", r)

            pe.wait_ge(const_pool, 1)
            for name in XT:
                c = int(name[2])
                kt, c = c // NCH, c % NCH
                g = free(start, name)
                pe.wait_ge(xn_done, 4 * c + 4)
                transposes(g, [xn[:, 4 * c + t, kt * P:(kt + 1) * P] for t in range(4)], ident[:]).then_inc(g_ready, 1)
            for w in "qkv":
                w_transposes(w, start, 0)
            g = free(start, "GM")
            pe.wait_ge(absum_done, 4)
            mm(g[:, 0:4], ones[:], absum[:], start=True, stop=True).then_inc(g_ready, 1)
            for name in QK:
                project(name, start)
            for name in V4:
                values(name, start)
            w_transposes("o", start, 0)
            for c in range(8):
                g = free(start, f"T{c}")[:].bitcast(BF16)
                pe.wait_ge(tern_done, 1 if c < 4 else 2)
                if c < 4:
                    b = [tern_fc[:, 2 * c + t, k * P:(k + 1) * P] for k in range(KT) for t in range(2)]
                else:
                    b = [tern_pr[:, k, (2 * (c - 4) + t) * P:(2 * (c - 4) + t + 1) * P] for t in range(2) for k in range(KT)]
                transposes(g, b, ident_b[:]).then_inc(g_ready, 1)
            pe.wait_ge(zero_done, 4)
            with pe.Fori(0, PAIRS - 1) as u:
                r = attention_round(u)
                heads(u, r)
                for w, s in (("q", 13), ("k", 14), ("v", 15)):
                    w_transposes(w, r, u + 1)
                    p_transposes(u, s)
                ffn("F0", u, r)
                ffn("F1", u, r)
                for name in QK[:2]:
                    project(name, r)
                attend(u, "AV10", r)
                for name in QK[2:]:
                    project(name, r)
                for name in ("V0", "V1"):
                    values(name, r)
                ffn("H0", u, r)
                ffn("H1", u, r)
                for name in ("V2", "V3"):
                    values(name, r)
                outputs("O0", r)
                outputs("O1", r)
                ffn("FP", u, r)
                outputs("O2", r)
                outputs("O3", r)
                w_transposes("o", r, u + 1)
            u, r = PAIRS - 1, last_round
            heads(u, r)
            for s in (13, 14, 15):
                p_transposes(u, s)
            ffn("F0", u, r)
            ffn("F1", u, r)
            attend(u, "AV10", r)
            ffn("H0", u, r)
            ffn("H1", u, r)
            outputs("O0", r)
            outputs("O1", r)
            ffn("FP", u, r)
            outputs("O2", r)
            outputs("O3", r)

            def free1(r, name):
                at, o, g, a, d = r.order.at[name], r.order, r.g, r.a, r.d
                if at >= 4:
                    before = o.names[at - 4]
                elif r is pre1:
                    return r.bank(name)
                else:
                    o = ROUND1
                    before = o.names[o.n - 4 + at]
                    a, d = a - o.na, d - o.nd
                if before in o.read_by_dve:
                    pe.wait_ge(r_dve, d + o.dve[before])
                else:
                    pe.wait_ge(r_act, a + o.act[before])
                return r.bank(name)

            pe.wait_ge(g_lo, last_round.read("O3"))
            pe.wait_ge(consts1, 1)
            for c in range(4):
                last = mm(sc[c // 2][:, c % 2, :], zero_b[:, 0:P], zero_b[:], start=True, stop=True)
            last.then_inc(ma_done, 2)
            pe.wait_ge(tern_in, 16)
            for k in range(4):
                g = free1(pre1, PRE1.names[k])[:].bitcast(BF16)
                if k < 3:
                    b = [tern1[:, 2 * k + t, d * P:(d + 1) * P] for d in range(KT) for t in range(2)]
                else:
                    b = [tern1[:, 6 + t, d * P:(d + 1) * P] for d in range(KT) for t in range(2)]
                transposes(g, b, ident_b[:]).then_inc(r_ready, 1)
            g = free1(pre1, "GT")
            pe.wait_ge(l1_in, 16 * L1_LOADS)
            for k in range(KT):
                last = nc.tensor.transpose(g[:, k * E:(k + 1) * E], graw[:, k * P:(k + 1) * P], ident[0:E, 0:E])
            last.then_inc(r_ready, 1)

            def token_transposes(name, src, done, base, r):
                c = int(name[2])
                g = free1(r, name)
                k, c = c // NCH, c % NCH
                pe.wait_ge(done, base + 4 * c + 4)
                transposes(g, [src[:, 4 * c + t, k * P:(k + 1) * P] for t in range(4)], ident[:]).then_inc(r_ready, 1)

            for c in range(4):
                token_transposes(f"XA{c}", x2, x2_done, 0, pre1)
            g = free1(pre1, "LG")
            pe.wait_ge(r_dve, pre1.read("XA3"))
            for t in range(NT):
                for k in range(KT):
                    last = three(g[:, t * E:(t + 1) * E], [v[:, k, t * P:(t + 1) * P] for v in x2T],
                                 [v[:, k, :] for v in gT], k == 0, k == KT - 1)
            last.then_inc(r_ready, 1)
            for c in range(4):
                token_transposes(f"XB{c}", hq, hq_done, 0, pre1)
            pe.wait_ge(r_dve, pre1.read("XB3"))
            for name in [x_ for x_ in PRE1.names if x_[:2] in ("QA", "KA")]:
                b, c = int(name[2]), int(name[3])
                g = free1(pre1, name)
                o = (D if name[0] == "K" else 0) + b * P
                for k in range(KT):
                    for n_ in range(2):
                        last = mm(g[:], qkvT[:, k, o:o + P], nT[n_][:, k, c * CH:(c + 1) * CH], start=(k == 0 and n_ == 0),
                                  stop=(k == KT - 1 and n_ == 1))
                last.then_inc(r_ready, 1)
            pe.wait_ge(sel_done, 2)
            for c in range(NCH):
                g = free1(pre1, f"SL{c}")
                for t in range(4):
                    last = nc.tensor.transpose(g[0:2 * E, t * P:(t + 1) * P], sel[:, 4 * c + t, :, :].rearrange("p a e -> p (a e)"), ident[:])
                last.then_inc(r_ready, 1)
            pe.wait_ge(r_dve, PRE1.nd)
            pe.wait_ge(r_act, PRE1.na)

            def expert_weights(i, r):
                g = free1(r, "WG")
                pe.wait_ge(gu_in, 16 * (i + 1))
                for k in range(KT):
                    for m_ in range(2):
                        last = nc.tensor.transpose(g[:, (2 * k + m_) * I:(2 * k + m_ + 1) * I], raw_gu[:, m_, k * P:(k + 1) * P], ident[0:I, 0:I])
                last.then_inc(r_ready, 1)
                g = free1(r, "WD")
                pe.wait_ge(dn_in, 16 * (i + 1))
                for k in range(2):
                    last = nc.tensor.transpose(g[0:I, k * P:(k + 1) * P], raw_dn[:, k, :], ident[:])
                last.then_inc(r_ready, 1)

            def expert_hidden(i, r, c):
                for m_, name in enumerate((f"GA{c}", f"UP{c}")):
                    g = free1(r, name)
                    if c == 0 and m_ == 0:
                        pe.wait_ge(r_dve, r.read("WG"))
                    for k in range(KT):
                        last = three(g[0:I, :], [v[:, k, m_, :] for v in guT], [v[:, k, c * CH:(c + 1) * CH] for v in x2T],
                                     k == 0, k == KT - 1)
                    last.then_inc(r_ready, 1)
                g = free1(r, f"WB{c}")
                pe.wait_ge(staged, 7 * i + 7)
                mm(g[0:I, :], st_hot[:], selT[:, c * CH:(c + 1) * CH], start=True, stop=True).then_inc(r_ready, 1)

            def expert_out(i, r, c):
                pe.wait_ge(a_lo, 2 * i + c + 1)
                for t in range(4):
                    tt = 4 * c + t
                    last = three(sc[tt // 4][:, (tt // 2) % 2, (tt % 2) * D:(tt % 2 + 1) * D],
                                 [v[:, c, t * P:(t + 1) * P] for v in aT], [v[:] for v in dnT], False, False,
                                 skip_group_check=True)
                last.then_inc(ma_done, 1)

            def keys_values(i, r):
                pe.wait_ge(staged, 7 * i + 7)
                for m_, name in enumerate(("KV", "V")):
                    g = free1(r, name)
                    for k in range(KT):
                        for n_ in range(2):
                            last = mm(g[:, 0:D], st_n[n_][:, k, :], qkvT[:, k, (m_ + 1) * D:(m_ + 2) * D],
                                      start=(k == 0 and n_ == 0), stop=(k == KT - 1 and n_ == 1))
                    last.then_inc(r_ready, 1)

            def chunk_scores(i, r, k):
                g = free1(r, f"SC{k}")
                rows_ = slice(32 * k, 32 * k + 32)
                for b in range(2):
                    for c in range(2):
                        last = mm(g[:, (2 * b + c) * P:(2 * b + c + 1) * P], st_k[c][rows_, b, :], st_q[rows_, b, :],
                                  start=True, stop=True)
                last.then_inc(r_ready, 1)

            def chunk_out(i, r):
                g = free1(r, "OC")
                pe.wait_ge(state_done, 2 * i + 2)
                pe.wait_ge(r_act, r.acted("V"))
                for b in range(2):
                    mm(g[:, b * P:(b + 1) * P], st_qd[:, b, :], state[:, b, :], start=(b == 0), stop=False,
                       skip_group_check=True)
                pe.wait_ge(r_dve, r.read("SC3"))
                for k in range(4):
                    for b in range(2):
                        for c in range(2):
                            hh = HALF * b + 2 * k + c
                            last = mm(g[:, hh * D1:(hh + 1) * D1], masked[:, k, 2 * b + c, :], v1[:, hh * D1:(hh + 1) * D1],
                                      start=False, stop=(k == 3 and b == 1 and c == 1), skip_group_check=True)
                last.then_inc(r_ready, 1)
                g = free1(r, "ST")
                for b in range(2):
                    last = mm(g[:, b * P:(b + 1) * P], kd[:, b * P:(b + 1) * P], v1[:, b * P:(b + 1) * P], start=True, stop=True)
                last.then_inc(r_ready, 1)

            with pe.Fori(0, G) as i:
                r = round1(i)
                expert_weights(i, r)
                expert_hidden(i, r, 0)
                keys_values(i, r)
                chunk_scores(i, r, 0)
                chunk_scores(i, r, 1)
                expert_hidden(i, r, 1)
                expert_out(i, r, 0)
                chunk_scores(i, r, 2)
                chunk_scores(i, r, 3)
                chunk_out(i, r)
                expert_out(i, r, 1)
            for c in range(4):
                token_transposes(f"OT{c}", hq, hq_done, NT, post1)
            pe.wait_ge(r_dve, post1.read("OT3"))
            for c in range(4):
                g = free1(post1, f"PO{c}")
                for t in range(2):
                    q = (2 * c + t) * P
                    for k in range(KT):
                        for n_ in range(2):
                            last = mm(g[:, t * D:(t + 1) * D], nT[n_][:, k, q:q + P], p1T[:, k, :], start=(k == 0 and n_ == 0),
                                      stop=(k == KT - 1 and n_ == 1))
                last.then_inc(r_ready, 1)


_INS = ["L0_attn_x", "L0_attn_W_K", "L0_attn_W_Q", "L0_attn_W_V", "L0_attn_W_O", "L0_ffn_w_fc", "L0_ffn_w_proj",
        "L1_attn_qkv_w", "L1_attn_qkv_norm_w", "L1_attn_proj_w", "L1_attn_proj_norm_w", "L1_attn_norm_w", "L1_attn_s",
        "L1_ffn_gate_weight", "L1_ffn_gate_up_proj", "L1_ffn_down_proj", "L1_ffn_merge_groups", "L1_ffn_dominant_experts"]
_OUTS = [((1, 1024, 256), "float32")]


def kernel(**inputs):
    import numpy as _np
    import concourse.bacc as _bacc
    from concourse import mybir as _mybir
    from concourse.bass_utils import run_bass_kernel_spmd as _run

    nc = _bacc.Bacc("TRN2", target_bir_lowering=False, num_devices=1)
    arrays, args = {}, []
    for name in _INS:
        a = _np.ascontiguousarray(inputs[name])
        arrays[f"in_{name}_dram"] = a
        args.append(nc.dram_tensor(f"in_{name}_dram", a.shape, _mybir.dt.from_np(a.dtype), kind="ExternalInput").ap())
    for i, (shape, dtype) in enumerate(_OUTS):
        dt = _mybir.dt.from_np(_np.dtype(dtype))
        args.append(nc.dram_tensor(f"out_{i}_dram", shape, dt, kind="ExternalOutput").ap())
    transformer_kernel(nc, *args)
    r = _run(nc, [arrays], core_ids=[0])
    return r.results[0]["out_0_dram"]
```

```python
from contextlib import ExitStack

import numpy as np

import concourse.bass as bass
from concourse import mybir

F32 = mybir.dt.float32
F32R = mybir.dt.float32r
BF16 = mybir.dt.bfloat16
I32 = mybir.dt.int32
ALU = mybir.AluOpType
ACT = mybir.ActivationFunctionType
AX = mybir.AxisListType

P = 128


class Order:

    def __init__(self, names, act, dve, banks):
        self.names, self.at, self.act, self.dve, a, d = names, {}, {}, {}, 0, 0
        self.bank = {name: n % banks if isinstance(banks, int) else banks[n] for n, name in enumerate(names)}
        self.last = {b: name for name, b in self.bank.items()}
        self.before = {}
        for n, name in enumerate(names):
            same = [x for x in names[:n] if self.bank[x] == self.bank[name]]
            self.before[name] = same[-1] if same else None
            a += any(name.startswith(x) for x in act)
            d += any(name.startswith(x) for x in dve)
            self.at[name], self.act[name], self.dve[name] = n, a, d
        self.read_by_dve = {name for name in names if any(name.startswith(x) for x in dve)}
        self.read_by_act = {name for name in names if any(name.startswith(x) for x in act)}
        self.n, self.na, self.nd = len(names), a, d


class Round:

    def __init__(self, order, banks, g, a, d):
        self.order, self.banks, self.g, self.a, self.d = order, banks, g, a, d

    def bank(self, name):
        return self.banks[self.order.bank[name]]

    def ready(self, name):
        return self.g + self.order.at[name] + 1

    def acted(self, name):
        return self.a + self.order.act[name]

    def read(self, name):
        return self.d + self.order.dve[name]



class Memory:

    def __init__(self, nc, first, last):
        self.nc, self.next, self.last = nc, first, last

    def take(self, name, shape, dt=F32):
        size = 1
        for n in shape[1:]:
            size *= n
        size = (size * (2 if dt == BF16 else 4) + 31) // 32 * 32
        at, self.next = self.next, self.next + size
        assert self.next <= self.last, (name, self.next, self.last)
        return self.nc.alloc_sbuf_tensor_at(name, shape, dt, offset=at)


def transformer_kernel(nc, x, w_k, w_q, w_v, w_o, w_fc, w_proj, qkv_w, qkv_norm_w, proj_w, proj_norm_w, norm_w, decay,
                       gate_w, gate_up, down, merge, dominant, out, dbg=None):
    _, TOK, D = x.shape
    H, DH, _ = w_q.shape
    NT, KT = TOK // P, D // P
    PAIRS = H // 2
    F = w_fc.shape[0]
    FT_ = F // P
    CH = 512
    NCH = TOK // CH
    SCALE = float(DH) ** -0.5
    EPS_LN, EPS_BIT, EPS_F32, EPS_OUT = 1e-5, 1e-6, float(np.finfo(np.float32).eps), 1e-6
    QB = 128.0
    H1, D1 = decay.shape[0], D // decay.shape[0]
    E, I2, _ = gate_up.shape
    I = I2 // 2
    G = dominant.shape[0]
    HALF = H1 // 2

    ctx = ExitStack()
    with ctx:
        def sem(name):
            return ctx.enter_context(nc.semaphore(name))

        first, last_byte = (nc.sbuf_base + 31) // 32 * 32, nc.sbuf_usable_end
        always = Memory(nc, first, last_byte)
        ident = always.take("ident", [P, P])
        ident_b = always.take("ident_b", [P, P], BF16)
        mask_b = always.take("mask_b", [P, P], BF16)
        half = always.take("half", [P, NT])
        ones = always.take("ones", [P, P])
        acc = always.take("acc", [P, NT, D])
        stats = always.take("stats", [P, NT, 6])
        mv = always.take("mv", [P, NT, 2])
        rstd = always.take("rstd", [P, NT])
        rows = always.take("rows", [P, 4, NT])
        absum = always.take("absum", [P, 4])
        gamma = always.take("gamma", [P, 4])
        thr = always.take("thr", [P, 4])
        nthr = always.take("nthr", [P, 4])
        thr_l1 = always.take("thr_l1", [P, 2, 8])
        ngamma = always.take("ngamma", [P, 4])
        shared = always.next

        m = Memory(nc, shared, last_byte)
        xnT = [m.take(f"xnT{n}", [P, KT, TOK], F32R) for n in "hl"]
        wraw = {w: m.take(f"raw_{w}", [P, 2, D]) for w in "qkv"}
        wT = {w: [m.take(f"wT_{w}{n}", [P, 2, 2 * P], F32R) for n in "hl"] for w in "qkvo"}
        qT = [[m.take(f"qT{a}{n}", [P, TOK], F32R) for n in "hl"] for a in range(2)]
        kT = [[m.take(f"kT{a}{n}", [P, TOK], F32R) for n in "hl"] for a in range(2)]
        vv = [m.take(f"v{n}", [P, NT, 2 * DH], F32R) for n in "hl"]
        prob = [m.take(f"prob{n}", [P, (NT - n) * P]) for n in range(4)]
        nmax = m.take("nmax", [P, 4])
        rsum = m.take("rsum", [P, 4])
        rinv = m.take("rinv", [P, 4])
        xq_tile = m.take("xq_tile", [P, D])
        fxT = [m.take(f"fxT{n}", [P, KT, P], F32R) for n in "hl"]
        fcT = m.take("fcT", [P, KT, F], F32R)
        prT = m.take("prT", [P, FT_, D], F32R)
        h_place = m.next
        h = m.take("h", [P, F])
        hT = [m.take(f"hT{n}", [P, FT_, P], F32R) for n in "hl"]
        hstats = m.take("hstats", [P, 2, 6])
        hmv = m.take("hmv", [P, 2])
        hrow = m.take("hrow", [P, 8])
        xstats = m.take("xstats", [P, 6])
        xmv = m.take("xmv", [P, 2])
        xrow = m.take("xrow", [P, 8])
        thr_now = m.take("thr_now", [P, 2, 1])
        raw1 = m.take("raw1", [P, D])
        below1 = m.take("below1", [P, D], BF16)
        above1 = m.take("above1", [P, D], BF16)
        tern1_tile = m.take("tern1_tile", [P, D], BF16)
        late = m.next
        pT = [[m.take(f"pT{c}{n}", [P, 4 * (c + 1), CH], F32R) for n in "hl"] for c in range(2)]
        zT = [[m.take(f"zT{a}{n}", [P, TOK], F32R) for n in "hl"] for a in range(2)]
        PT0, PT1, ROW = 4 * CH * 4, 8 * CH * 4, CH * 4
        ends = [late + PT0, late + 2 * PT0, late + 2 * PT0 + PT1, late + 2 * PT0 + 2 * PT1]
        zero_at = [(e - ROW + 2 * P * 4, e - ROW + 3 * P * 4) for e in ends]
        m0 = Memory(nc, zero_at[0][1], zero_at[1][0])
        above = m0.take("above", [P, 2 * F], BF16)
        m0 = Memory(nc, zero_at[1][1], zero_at[2][0])
        xn = m0.take("xn", [P, NT, D])
        tern_pr = m0.take("tern_pr", [P, KT, F], BF16)
        m0 = Memory(nc, zero_at[2][1], zero_at[3][0])
        raw_fc = m0.take("raw_fc", [P, F // P, D])
        tern_fc = m0.take("tern_fc", [P, F // P, D], BF16)
        m0 = Memory(nc, zero_at[3][1], m.next)
        raw_pr = m0.take("raw_pr", [P, KT, F])
        raw_l1 = m0.take("raw_l1", [P, 8, D])
        junk = nc.alloc_sbuf_tensor_at("junk", [P, 2 * F], BF16, offset=h_place)

        m = Memory(nc, shared, last_byte)
        tern1 = m.take("tern1", [P, 8, D], BF16)
        x2 = m.take("x2", [P, NT, D])
        hq = m.take("hq", [P, NT, D])
        x2T = [m.take(f"x2T{n}", [P, KT, TOK], F32R) for n in "hl"]
        nT = [m.take(f"nT{n}", [P, KT, TOK], F32R) for n in "hl"]
        qkvT = m.take("qkvT", [P, KT, 3 * D], F32R)
        p1T = m.take("p1T", [P, KT, D], F32R)
        q1T = m.take("q1T", [P, 2, TOK])
        qdT = m.take("qdT", [P, 2, TOK])
        k1T = [m.take(f"k1T{n}", [P, 2, TOK]) for n in "eo"]
        causal = m.take("causal", [P, 4, 4, P])
        masked = m.take("masked", [P, 4, 4, P])
        dist = m.take("dist", [P, P])
        qdecay = m.take("qdecay", [P, 2, P])
        blocks = m.take("blocks", [P, P])
        colw = m.take("colw", [P, 16])
        negs_rows = m.take("negs_rows", [P, H1])
        kdecay = m.take("kdecay", [P, H1])
        normw = m.take("normw", [P, D])
        small = m.take("small", [P, 16])
        y_now = m.take("y_now", [P, D])
        y_square = m.take("y_square", [P, D])
        y_sums = m.take("y_sums", [P, 2, 1])
        factor = m.take("factor", [P, NT])
        o1 = m.take("o1", [P, NT, D])
        state = m.take("state", [P, 2, P])
        state_new = m.take("state_new", [P, 2, P])
        kd = m.take("kd", [P, D])
        v1 = m.take("v1", [P, D])
        v_apart = m.take("v_apart", [P, 2, HALF * P])
        st_n = [m.take(f"st_n{n}", [P, KT, P], F32R) for n in "hl"]
        st_k = [m.take(f"st_k{n}", [P, 2, P]) for n in "eo"]
        st_q = m.take("st_q", [P, 2, 4, P])
        st_qd = m.take("st_qd", [P, 2, P])
        graw = m.take("graw", [E, D])
        gT = [m.take(f"gT{n}", [P, KT, E], F32R) for n in "hl"]
        lg = m.take("lg", [P, NT, E])
        pb = m.take("pb", [P, NT, E])
        sel = m.take("sel", [P, NT, 2, E])
        top = m.take("top", [P, NT, 8])
        gs = m.take("gs", [P, 4, NT])
        selT = m.take("selT", [2 * E, TOK], F32R)
        mg_i = m.take("mg_i", [2 * E, 1], I32)
        mg_f = m.take("mg_f", [2 * E, 1])
        iota_g = m.take("iota_g", [2 * E, G])
        onehot = m.take("onehot", [2 * E, G, I])
        st_hot = m.take("st_hot", [2 * E, I], F32R)
        dom = m.take("dom", [1, G], I32)
        raw_gu = m.take("raw_gu", [I, 2, D])
        raw_dn = m.take("raw_dn", [P, 2, I])
        guT = [m.take(f"guT{n}", [P, KT, 2, I], F32R) for n in "hl"]
        dnT = [m.take(f"dnT{n}", [I, D], F32R) for n in "hl"]
        silu = m.take("silu", [I, 2, CH])
        actv = m.take("actv", [I, 2, CH])
        aT = [m.take(f"aT{n}", [I, 2, CH], F32R) for n in "hl"]
        zero_b = m.take("zero_b", [1, CH], BF16)

        xn_dram = nc.dram_tensor("xn_scratch", [P, NT, D], F32)
        raw1_dram = nc.dram_tensor("raw1_scratch", [P, 8, D], F32)
        tern_dram = nc.dram_tensor("tern_scratch", [P, 8, D], BF16)

        sc = [ctx.enter_context(nc.psum_tensor(f"sc{n}", [P, 2, CH], F32)) for n in range(2)]
        tp = [ctx.enter_context(nc.psum_tensor(f"tp{n}", [P, CH], F32)) for n in range(2)]
        gp = [ctx.enter_context(nc.psum_tensor(f"gp{n}", [P, CH], F32)) for n in range(2)]

        S = {name: sem(name) for name in (
            "x_in x_in2 fc_in pr_in raws_in xq_step raw1_in tern1_done tern1_out tern1_step q_in kv_in o_in xq_in spill const_pool consts1 dve_step pool_step xn_done absum_done "
            "tern_done xq_done zero_done s_ready max_done exp_done rcp_done pn_done t_ready t_hi t_lo g_ready g_hi g_lo "
            "ffn_step ffn_pow l1_in sems_in tern_in gu_in dn_in r_ready r_act r_dve sums_done hq_done x2_done sel_done q_staged "
            "prep_done staged decays masks_done decay_in pb_done xvar_done pool_waits dve_waits state_done a_hi a_lo ma_done "
            "post_step y_done y_step out_done").split()}
        (x_in, x_in2, fc_in, pr_in, raws_in, xq_step, raw1_in, tern1_done, tern1_out, tern1_step, q_in, kv_in, o_in, xq_in, spill, const_pool, consts1, dve_step, pool_step, xn_done,
         absum_done, tern_done, xq_done, zero_done, s_ready, max_done, exp_done, rcp_done, pn_done, t_ready, t_hi, t_lo,
         g_ready, g_hi, g_lo, ffn_step, ffn_pow, l1_in, sems_in, tern_in, gu_in, dn_in, r_ready, r_act, r_dve, sums_done,
         hq_done, x2_done, sel_done, q_staged, prep_done, staged, decays, masks_done, decay_in, pb_done, xvar_done, pool_waits, dve_waits, state_done, a_hi,
         a_lo, ma_done, post_step, y_done, y_step, out_done) = S.values()

        XT = [f"XT{k * NCH + c}" for c in range(NCH) for k in range(KT)]
        QK = [f"{w}{a}{c}" for a in range(2) for w in "QK" for c in range(NCH)]
        V4 = [f"V{n}" for n in range(4)]
        T8 = [f"T{n}" for n in range(8)]
        ACT_READS = ("XT", "W", "Q", "K", "V", "AV", "FT", "F0", "F1", "H")
        DVE_READS = ("XT", "W", "Q", "K", "V", "AV", "FT", "H", "GM", "GN", "T", "O", "FP")
        START = Order(XT + ["Wq", "Wk", "GM", "Q00", "Q01", "Wv", "K00", "K01", "GN"] + T8, ACT_READS, DVE_READS, 2)
        BESIDE = {0: ["Q10"], 1: ["K10"], 2: ["V0"], 3: ["Q11"], 4: ["K11"], 5: ["V1"], 6: ["V2", "Wo"], 7: ["V3", ("AV01", 0, 2)],
                  8: [("AV01", 2, 4)], 9: [("AV01", 4, 6)], 10: [("AV01", 6, 8)], 11: [("AV00", 0, 2)], 12: [("AV00", 2, 4), "FT"],
                  13: ["Wq"], 14: ["Wk"], 15: ["Wv", ("AV11", 0, 2)]}
        WITH_TILES = ["Q10", "K10", "V0", "Q11", "K11", "V1", "V2", "Wo", "V3", "AV01", "AV00", "FT", "Wq", "Wk", "Wv", "AV11"]
        AFTER = ["F0", "F1", "K00", "Q00", "K01", "Q01", "O2", "AV10", "O3", "H0", "H1", "O0", "FP", "O1"]
        NAMES = WITH_TILES + AFTER
        BANKS = [n % 2 for n in range(len(WITH_TILES))] + [0, 2, 3, 1, 0, 2, 3, 1, 0, 2, 3, 1, 0, 2]
        NEXT_PAIR = ("Wq", "Wk", "Wv", "Q00", "K00", "Q01", "K01")
        here = [n for n, name in enumerate(NAMES) if name not in NEXT_PAIR]
        ROUND = Order(NAMES, ACT_READS, DVE_READS, BANKS)
        LAST = Order([NAMES[n] for n in here], ACT_READS, DVE_READS, [BANKS[n] for n in here])
        banks4 = [gp[0], gp[1], tp[0], tp[1]]
        start = Round(START, banks4, 0, 0, 0)

        def attention_round(u):
            return Round(LAST if isinstance(u, int) else ROUND, banks4, START.n + u * ROUND.n, START.na + u * ROUND.na,
                         START.nd + u * ROUND.nd)

        def reads_after(name):
            return min(o.nd - o.dve[name] for o in (START, ROUND) if name in o.at)

        def reads_after_bank(b):
            return min(o.nd - o.dve[o.last[b]] for o in (START, ROUND) if b in o.last)

        last_round = attention_round(PAIRS - 1)
        TILE = [NT - 1 - s % NT for s in range(2 * NT)]
        TG = [0]
        for i in TILE:
            TG.append(TG[-1] + (2 if i >= 4 else 1))
        NTG = TG[-1]
        LAG = 3
        FSTEPS = 11
        XSTEP = 2
        XSTEPS = 11
        STAGED = 6
        YSTEPS = 4
        L1_LOADS = 3 + 2 * KT + 2

        ACT1 = ("GT", "XA", "XB", "QA", "KA", "SL", "WG", "WD", "V", "GA", "OC", "OT")
        DVE1 = ("TQ", "TP", "GT", "XA", "LG", "XB", "QA", "KA", "SL", "WG", "WD", "KV", "UP", "WB", "SC", "ST", "OT", "PO")
        PRE1 = Order(["TQ0", "TQ1", "TQ2", "TP", "GT"] + [f"XA{c}" for c in range(4)] + ["LG"] + [f"XB{c}" for c in range(4)]
                     + [f"{n}{b}{c}" for n in ("QA", "KA") for b in range(2) for c in range(NCH)] + ["SL0", "SL1"], ACT1, DVE1, 4)
        ROUND1 = Order(["WG", "WD", "KV", "V", "SC0", "SC1", "GA0", "UP0", "WB0", "SC2", "SC3", "GA1", "UP1", "WB1",
                        "OC", "ST"], ACT1, DVE1, 4)
        POST1 = Order(["OT0", "OT2", "OT1", "OT3", "PO0", "PO1", "PO2", "PO3"], ACT1, DVE1, 4)
        assert PRE1.n % 4 == 0 and ROUND1.n % 4 == 0
        pre1 = Round(PRE1, banks4, 0, 0, 0)

        def round1(i):
            return Round(ROUND1, banks4, PRE1.n + i * ROUND1.n, PRE1.na + i * ROUND1.na, PRE1.nd + i * ROUND1.nd)

        def round_before(r):
            return Round(ROUND1, banks4, r.g - ROUND1.n, r.a - ROUND1.na, r.d - ROUND1.nd)

        r8 = round1(G)
        post1 = Round(POST1, banks4, r8.g, r8.a, r8.d)

        block = ctx.enter_context(nc.Block())

        def widths(i):
            n = (i + 1) * P
            if n <= CH:
                return [(0, 0, max(n, 2 * P))]
            return [(0, 0, n // 2), (1, n // 2, n // 2)]

        def score_view(t, i):
            n = (i + 1) * P
            return t[:, 0, 0:n] if n <= CH else t[:, :, 0:n // 2]

        def prob_view(t, i):
            n = (i + 1) * P
            return t[:, 0:n] if n <= CH else t[:, 0:n].rearrange("p (b n) -> p b n", b=2)

        def chunk(t, c):
            return t[:, c * CH:(c + 1) * CH]

        def finished(s, r):
            names = [x_ if isinstance(x_, str) else x_[0] for x_ in BESIDE[s] if isinstance(x_, str) or x_[2] == 4 * (int(x_[0][3]) + 1)]
            return [x_ for x_ in names if x_ in r.order.at]

        def place(name, halves):
            if name[:2] == "XT":
                c = int(name[2])
                return [t[:, c // NCH, (c % NCH) * CH:(c % NCH + 1) * CH] for t in xnT]
            if name[0] == "W":
                return [t[:] for t in wT[name[1]]]
            if name[:2] == "AV":
                return [chunk(t, int(name[3])) for t in zT[int(name[2])]]
            if name[0] == "Q":
                return [chunk(t, int(name[2])) for t in qT[int(name[1])]]
            if name[0] == "K":
                return [chunk(t, int(name[2])) for t in kT[int(name[1])]]
            if name[0] == "V":
                c = int(name[1])
                return [t[:, 2 * c:2 * c + 2, :] for t in vv]
            if name == "FT":
                return [t[:] for t in fxT]
            if name[0] == "H":
                c = int(name[1])
                return [t[:, 4 * c:4 * c + 4, :] for t in hT]
            raise KeyError(name)

        def diagonal(t, b):
            first_ = t[:, b, 0:D1]
            return bass.AP(first_.tensor, first_.offset, [first_.ap[0], [P + D1, HALF], [1, D1]])

        def as_shape(src, dst):
            n = 1
            for k in dst.shape[1:]:
                n *= k
            s = src[0:dst.shape[0], 0:n]
            return s if len(dst.shape) == 2 else s.rearrange("p (a b) -> p a b", b=dst.shape[2])

        @block.sync
        def _(sp):
            def load_kv(pair):
                for w, src in (("k", w_k), ("v", w_v)):
                    sp.dma_start(wraw[w][:], src[bass.ds(2 * pair, 2)].rearrange("a h d -> h a d")).then_inc(kv_in, 16)

            def load_q(pair):
                sp.dma_start(wraw["q"][:], w_q[bass.ds(2 * pair, 2)].rearrange("a h d -> h a d")).then_inc(q_in, 16)

            def load_o(pair):
                sp.dma_start(wraw["q"][:], w_o.rearrange("(m p) f -> p m f", p=P)[:, :, bass.ds(pair * 2 * DH, 2 * DH)])\
                  .then_inc(o_in, 16)

            def load_xq(t):
                sp.dma_start(xq_tile[:].rearrange("p (a d) -> p a d", a=1), xn_dram.ap()[:, bass.ds(t, 1), :]).then_inc(xq_in, 16)

            def load_raw1(t):
                sp.dma_start(raw1[:].rearrange("p (a d) -> p a d", a=1), raw1_dram.ap()[:, bass.ds(t, 1), :]).then_inc(raw1_in, 16)

            def store_tern1(t):
                sp.wait_ge(tern1_done, t + 1)
                sp.dma_start(tern_dram.ap()[:, bass.ds(t, 1), :], tern1_tile[:].rearrange("p (a d) -> p a d", a=1)).then_inc(tern1_out, 16)

            for c in range(NCH):
                tiles = slice(c * NT // NCH, (c + 1) * NT // NCH)
                sp.dma_start(acc[:, tiles, :], x[0].rearrange("(t p) d -> p t d", p=P)[:, tiles, :]).then_inc((x_in, x_in2)[c], 16)
            load_q(0)
            load_kv(0)
            sp.dma_start(raw_fc[:], w_fc.rearrange("(t p) d -> p t d", p=P)).then_inc(fc_in, 16)
            sp.dma_start(raw_pr[:], w_proj.rearrange("(t p) f -> p t f", p=P)).then_inc(pr_in, 16)
            sp.dma_start(raw_l1[:, 0:6, :], qkv_w.rearrange("(t p) d -> p t d", p=P)).then_inc(raws_in, 16)
            sp.dma_start(raw_l1[:, 6:8, :], proj_w.rearrange("(t p) d -> p t d", p=P)).then_inc(raws_in, 16)
            sp.wait_ge(g_ready, start.ready("Wq"))
            load_o(0)
            sp.wait_ge(g_ready, start.ready("Wv"))
            load_kv(1)
            sp.wait_ge(xn_done, NT)
            sp.dma_start(xn_dram.ap(), xn[:]).then_inc(spill, 16)
            sp.wait_ge(raws_in, 32)
            sp.dma_start(raw1_dram.ap(), raw_l1[:]).then_inc(spill, 16)
            sp.wait_ge(spill, 32)
            load_xq(0)
            load_raw1(0)

            def prefetch(u, r, more):
                sp.wait_ge(g_ready, r.ready("Wo"))
                load_q(u + 1)
                sp.wait_ge(g_ready, r.ready("FT"))
                load_xq(u + 1)
                sp.wait_ge(g_ready, r.ready("Wq"))
                load_o(u + 1)
                if more:
                    sp.wait_ge(g_ready, r.ready("Wv"))
                    load_kv(u + 2)
                store_tern1(u)
                load_raw1(u + 1)

            with sp.Fori(0, PAIRS - 2) as u:
                prefetch(u, attention_round(u), True)
            u = PAIRS - 2
            prefetch(u, Round(ROUND, banks4, START.n + u * ROUND.n, 0, 0), False)
            store_tern1(PAIRS - 1)

            sp.wait_ge(g_ready, last_round.ready("O1"))
            sp.wait_ge(g_lo, last_round.read("O1"))
            sp.wait_ge(tern1_out, 16 * PAIRS)
            sp.dma_start(tern1[:], tern_dram.ap()).then_inc(tern_in, 16)
            sp.dma_start(graw[:], gate_w).then_inc(l1_in, 16)
            sp.dma_start(normw[:], norm_w.partition_broadcast(P)).then_inc(l1_in, 16)
            sp.dma_start(negs_rows[:], decay.partition_broadcast(P)).then_inc(l1_in, 16)
            for k in range(KT):
                for c, v in ((0, qkv_norm_w), (2, proj_norm_w)):
                    sp.dma_start(colw[:, c + k:c + k + 1], v[k * P:(k + 1) * P].rearrange("(p a) -> p a", a=1)).then_inc(l1_in, 16)
            for n in range(2):
                sp.dma_start(mg_i[n * E:(n + 1) * E, :], merge.rearrange("(e a) -> e a", a=1)).then_inc(l1_in, 16)
            sp.dma_start(dom[:], dominant.rearrange("(a g) -> a g", a=1)).then_inc(sems_in, 16)
            sp.wait_ge(sems_in, 16)

            def load_expert(i):
                e = sp.value_load(dom[0:1, bass.ds(i, 1)], min_val=0, max_val=E - 1)
                sp.dma_start(raw_gu[:], gate_up[bass.ds(e, 1)].rearrange("a (m i) d -> (a i) m d", m=2)).then_inc(gu_in, 16)
                sp.dma_start(raw_dn[:], down[bass.ds(e, 1)].rearrange("a (m p) i -> (a p) m i", p=P)).then_inc(dn_in, 16)

            load_expert(0)
            with sp.Fori(0, G - 1) as i:
                sp.wait_ge(r_ready, round1(i).ready("WD"))
                load_expert(i + 1)
            for t in range(NT):
                if t % 2 == 0:
                    sp.wait_ge(r_dve, post1.read(f"PO{t // 2}"))
                sp.dma_start(out[0].rearrange("(t p) d -> p t d", p=P)[:, t, :], acc[:, t, :]).then_inc(out_done, 16)
            sp.wait_ge(out_done, 16 * NT)

        @block.gpsimd
        def _(pool):
            n = [0]

            def link(ins):
                n[0] += 1
                ins.then_inc(pool_step, 1)
                pool.wait_ge(pool_step, n[0])

            link(nc.gpsimd.memset(ident[:], 0.0))
            link(nc.gpsimd.affine_select(out=ident[:], in_=ident[:], compare_op=ALU.not_equal, fill=1.0, base=0,
                                         pattern=[[-1, P]], channel_multiplier=1))
            link(nc.gpsimd.memset(mask_b[:], 0.0))
            link(nc.gpsimd.affine_select(out=mask_b[:], in_=mask_b[:], compare_op=ALU.is_ge, fill=-1e10, base=0,
                                         pattern=[[-1, P]], channel_multiplier=1))
            link(nc.gpsimd.tensor_copy(ident_b[:], ident[:]))
            link(nc.gpsimd.memset(half[:], -0.5))
            nc.gpsimd.memset(ones[:], 1.0).then_inc(const_pool, 1)
            for n_ in range(2):
                nc.gpsimd.memset(pT[1][n_][:, 7, 2 * P:3 * P].bitcast(F32), 0.0).then_inc(zero_done, 1)
                nc.gpsimd.memset(pT[0][n_][:, 3, 2 * P:3 * P].bitcast(F32), 0.0).then_inc(zero_done, 1)
            for c in range(NCH):
                tiles = slice(c * NT // NCH, (c + 1) * NT // NCH)
                pool.wait_ge(xvar_done, c + 1)
                nc.gpsimd.tensor_tensor(rstd[:, tiles], rstd[:, tiles], half[:, tiles], ALU.pow).then_inc(const_pool, 1)

            def normalise(u, s):
                pool.wait_ge(rcp_done, 2 * NT * u + s + 1)
                pool.sem_inc(pool_waits, 1)
                w = (TILE[s] + 1) * P
                nc.gpsimd.tensor_scalar(prob[s % 4][:, 0:w], prob[s % 4][:, 0:w], rinv[:, s % 4:s % 4 + 1], 1.0,
                                        ALU.mult, ALU.mult).then_inc(pn_done, 1)

            with pool.Fori(0, PAIRS) as u:
                for s in range(2 * NT):
                    normalise(u, s)
                    if s == XSTEP:
                        pool.wait_ge(xq_step, XSTEPS * u + 3)
                        nc.gpsimd.tensor_tensor(xrow[:, 0:1], xrow[:, 0:1], half[:, 0:1], ALU.pow).then_inc(xq_step, 1)
                pool.wait_ge(raw1_in, 16 * (u + 1))
                nc.gpsimd.tensor_copy(thr_now[:], thr_l1[:, :, bass.ds(u, 1)]).then_inc(tern1_step, 1)
                pool.wait_ge(tern1_step, 3 * u + 1)
                pool.sem_inc(pool_waits, 1)
                nc.gpsimd.tensor_scalar(above1[:], raw1[:], thr_now[:, 0, 0:1], None, ALU.is_gt).then_inc(tern1_step, 1)
                nc.gpsimd.tensor_scalar(below1[:], raw1[:], thr_now[:, 1, 0:1], None, ALU.is_lt).then_inc(tern1_step, 1)
                pool.wait_ge(tern1_step, 3 * u + 3)
                pool.wait_ge(tern1_out, 16 * u)
                nc.gpsimd.tensor_tensor(tern1_tile[:], below1[:], above1[:], ALU.subtract).then_inc(tern1_done, 1)
                pool.wait_ge(ffn_step, FSTEPS * u + 4)
                nc.gpsimd.tensor_tensor(hrow[:, 0:1], hrow[:, 0:1], half[:, 0:1], ALU.pow).then_inc(ffn_pow, 1)

            pool.wait_ge(g_lo, last_round.read("O1"))
            pool.wait_ge(tern1_out, 16 * PAIRS)
            link(nc.gpsimd.iota(dist[:], pattern=[[1, P]], base=0, channel_multiplier=-1, allow_small_or_imprecise_dtypes=True))
            link(nc.gpsimd.iota(small[:, 0:1], pattern=[[1, 1]], base=P, channel_multiplier=-1, allow_small_or_imprecise_dtypes=True))
            link(nc.gpsimd.iota(qdecay[:], pattern=[[0, 2], [1, P]], base=0, channel_multiplier=0, allow_small_or_imprecise_dtypes=True))
            link(nc.gpsimd.iota(iota_g[:], pattern=[[1, G]], base=0, channel_multiplier=0, allow_small_or_imprecise_dtypes=True))
            link(nc.gpsimd.memset(zero_b[:], 0.0))
            link(nc.gpsimd.memset(v_apart[:], 0.0))
            link(nc.gpsimd.memset(st_q[:], 0.0))
            nc.gpsimd.memset(state[:], 0.0).then_inc(state_done, 2)
            nc.gpsimd.memset(y_now[:], 0.0).then_inc(y_step, 2)
            link(nc.gpsimd.memset(blocks[:], 1.0))
            bv = blocks[:].rearrange("p (g d) -> p g d", d=D1)
            link(nc.gpsimd.affine_select(out=bv, in_=bv, compare_op=ALU.is_ge, fill=0.0, base=0,
                                         pattern=[[-D1, HALF], [0, D1]], channel_multiplier=1))
            link(nc.gpsimd.affine_select(out=bv, in_=bv, compare_op=ALU.is_ge, fill=0.0, base=D1 - 1,
                                         pattern=[[D1, HALF], [0, D1]], channel_multiplier=-1))
            nc.gpsimd.memset(top[:], 0.0).then_inc(consts1, 1)
            for k in range(2):
                pool.wait_ge(post_step, k + 1)
                nc.gpsimd.tensor_tensor(rows[:, k, :], rows[:, k, :], half[:], ALU.pow).then_inc(sums_done, 1)
            pool.wait_ge(masks_done, 1)
            cz = causal[:].rearrange("p a b t -> p (a b) t")
            nc.gpsimd.affine_select(out=cz, in_=cz, compare_op=ALU.is_ge, fill=0.0, base=0,
                                    pattern=[[0, H1], [1, P]], channel_multiplier=-1).then_inc(prep_done, 1)

            pool.wait_ge(r_dve, pre1.read("SL1"))
            pool.wait_ge(sel_done, 2)
            with pool.Fori(0, G) as i:
                r = round1(i)
                tok = bass.ds(i * P, P)
                pool.wait_ge(r_ready, round_before(r).ready("V"))
                for n_ in range(2):
                    nc.gpsimd.tensor_copy(st_n[n_][:], nT[n_][:, :, tok].bitcast(F32)).then_inc(staged, 1)
                pool.wait_ge(r_ready, round_before(r).ready("SC3"))
                for n_ in range(2):
                    nc.gpsimd.tensor_copy(st_k[n_][:], k1T[n_][:, :, tok]).then_inc(staged, 1)
                pool.wait_ge(r_ready, round_before(r).ready("WB1"))
                nc.gpsimd.tensor_copy(st_hot[:].rearrange("e (a i) -> e a i", a=1), onehot[:, bass.ds(i, 1), :]).then_inc(staged, 1)
                pool.wait_ge(r_ready, round_before(r).ready("OC"))
                nc.gpsimd.tensor_copy(st_qd[:], qdT[:, :, tok]).then_inc(staged, 1)
            for k in range(2):
                pool.wait_ge(y_done, k + 1)
                nc.gpsimd.tensor_tensor(rows[:, 2 + k, :], rows[:, 2 + k, :], half[:], ALU.pow).then_inc(sums_done, 1)

        @block.scalar
        def _(act):
            def high(names, r):
                for name in names:
                    act.wait_ge(g_ready, r.ready(name))
                    if name in ("F0", "F1"):
                        c = int(name[1])
                        nc.scalar.activation(chunk(h, c), r.bank(name)[:], ACT.Gelu, scale=ngamma[:, 0:1]).then_inc(g_hi, 1)
                        continue
                    dst = place(name, 0)[0]
                    nc.scalar.activation(dst, as_shape(r.bank(name), dst), ACT.Copy,
                                         scale=SCALE if name[0] == "Q" else 1.0).then_inc(g_hi, 1)

            def exp(u, s):
                act.wait_ge(max_done, 2 * NT * u + s + 1)
                if s >= 4:
                    act.wait_ge(t_ready, NTG * u + TG[s - 3])
                nc.scalar.activation(prob_view(prob[s % 4], TILE[s]), score_view(sc[s % 2], TILE[s]), ACT.Exp,
                                     bias=nmax[:, s % 4:s % 4 + 1], accum_out=rsum[:, s % 4:s % 4 + 1]).then_inc(exp_done, 1)

            def high_p(u, s):
                i = TILE[s]
                for b in range(TG[s + 1] - TG[s]):
                    w = min(4, i + 1 - 4 * b)
                    act.wait_ge(t_ready, NTG * u + TG[s] + b + 1)
                    q = (i % 4) * P
                    nc.scalar.activation(pT[i // 4][0][:, 4 * b:4 * b + w, q:q + P],
                                         tp[(TG[s] + b) % 2][:, 0:w * P].rearrange("p (j q) -> p j q", q=P),
                                         ACT.Copy).then_inc(t_hi, 1)

            def heads(u, r):
                for s in range(2 * NT):
                    if s >= 1:
                        high(finished(s - 1, r), r)
                    if s >= LAG:
                        high_p(u, s - LAG)
                    exp(u, s)
                high(finished(2 * NT - 1, r), r)
                for s in range(2 * NT - LAG, 2 * NT):
                    high_p(u, s)
                high(["AV11"], r)

            def magnitude(k, t):
                w = t.shape[1] * t.shape[2]
                if k:
                    act.wait_ge(absum_done, k)
                nc.scalar.activation(junk[:, 0:w].rearrange("p (a b) -> p a b", b=t.shape[2]), t, ACT.Abs,
                                     accum_out=absum[:, k:k + 1]).then_inc(absum_done, 1)

            act.wait_ge(fc_in, 16)
            magnitude(0, raw_fc[:])
            high(XT[:2], start)
            act.wait_ge(pr_in, 16)
            magnitude(1, raw_pr[:])
            high(XT[2:] + ["Wq", "Wk", "Q00", "Q01", "Wv", "K00", "K01"], start)
            act.wait_ge(raws_in, 32)
            magnitude(2, raw_l1[:, 0:6, :])
            magnitude(3, raw_l1[:, 6:8, :])
            act.wait_ge(spill, 32)
            act.wait_ge(tern_done, 2)
            with act.Fori(0, PAIRS - 1) as u:
                r = attention_round(u)
                heads(u, r)
                high([x_ for x_ in AFTER if x_ in ROUND.read_by_act], r)
            u, r = PAIRS - 1, last_round
            heads(u, r)
            high([x_ for x_ in AFTER if x_ in LAST.read_by_act], r)

            act.wait_ge(g_lo, last_round.read("O1"))
            act.wait_ge(l1_in, 16 * L1_LOADS)
            act.wait_ge(consts1, 1)
            act.wait_ge(decay_in, 1)
            for b in range(2):
                nc.scalar.activation(qdecay[:, b, :], qdecay[:, b, :], ACT.Exp, scale=colw[:, 6 + b:7 + b]).then_inc(decays, 1)
            nc.scalar.activation(kdecay[:], negs_rows[:], ACT.Exp, scale=small[:, 0:1]).then_inc(decays, 1)
            nc.scalar.activation(colw[:, 8:10], colw[:, 6:8], ACT.Exp, scale=float(P)).then_inc(decays, 1)
            for a in range(4):
                for b in range(2):
                    for c in range(2):
                        hh = HALF * b + 2 * a + c
                        last = nc.scalar.activation(causal[:, 2 * b + c, a, :], dist[:], ACT.Exp, scale=negs_rows[:, hh:hh + 1])
            last.then_inc(masks_done, 1)

            def high1(name, r):
                act.wait_ge(r_ready, r.ready(name))
                src = r.bank(name)
                if name == "GT":
                    d, scale = gT[0][:], 1.0
                elif name[:2] in ("XA", "XB"):
                    c = int(name[2])
                    k = c // NCH
                    d = (x2T if name[1] == "A" else nT)[0][:, k, (c % NCH) * CH:(c % NCH + 1) * CH]
                    scale = 1.0 if name[1] == "A" else colw[:, k:k + 1]
                elif name[:2] == "QA":
                    d, scale = q1T[:, int(name[2]), int(name[3]) * CH:(int(name[3]) + 1) * CH], ngamma[:, 2:3]
                elif name[:2] == "KA":
                    d, scale = k1T[0][:, int(name[2]), int(name[3]) * CH:(int(name[3]) + 1) * CH], colw[:, 12:13]
                elif name[:2] == "SL":
                    d, scale = chunk(selT, int(name[2])), 1.0
                elif name == "WG":
                    d, scale = guT[0][:].rearrange("p k m i -> p k (m i)"), 1.0
                elif name == "WD":
                    d, scale = dnT[0][:], 1.0
                else:
                    c = int(name[2])
                    k = c // NCH
                    d, scale = nT[0][:, k, (c % NCH) * CH:(c % NCH + 1) * CH], colw[:, 2 + k:3 + k]
                nc.scalar.activation(d, as_shape(src, d), ACT.Copy, scale=scale).then_inc(r_act, 1)

            for name in PRE1.names:
                if name == "LG":
                    continue
                if name[:2] == "QA" and name == "QA00":
                    act.wait_ge(sel_done, 1)
                    nc.scalar.activation(pb[:], lg[:], ACT.Exp).then_inc(pb_done, 1)
                if any(name.startswith(v) for v in ACT1):
                    high1(name, pre1)

            with act.Fori(0, G) as i:
                r = round1(i)
                act.wait_ge(r_ready, round_before(r).ready("SC3"))
                for a in range(4):
                    two = slice(2 * D1 * a, 2 * D1 * (a + 1))
                    nc.scalar.activation(st_q[two, :, a, :], q1T[two, :, bass.ds(i * P, P)], ACT.Copy).then_inc(q_staged, 1)
                high1("WG", r)
                high1("WD", r)
                act.wait_ge(r_ready, r.ready("V"))
                nc.scalar.activation(v1[:], r.bank("V")[:, 0:D], ACT.Copy, scale=ngamma[:, 2:3])
                for b in range(2):
                    last_ = nc.scalar.activation(diagonal(v_apart, b), r.bank("V")[:, b * P:(b + 1) * P].rearrange(
                        "p (h d) -> p h d", d=D1), ACT.Copy, scale=ngamma[:, 2:3])
                last_.then_inc(r_act, 1)
                for c in range(2):
                    name = f"GA{c}"
                    act.wait_ge(r_ready, r.ready(name))
                    act.wait_ge(r_dve, r.d - ROUND1.nd + ROUND1.dve[f"UP{c}"])
                    nc.scalar.activation(silu[:, c, :], r.bank(name)[0:I, :], ACT.Silu).then_inc(r_act, 1)
                    act.wait_ge(r_dve, r.read(f"WB{c}"))
                    act.wait_ge(ma_done, 2 * i + c + 1)
                    nc.scalar.activation(aT[0][:, c, :], actv[:, c, :], ACT.Copy).then_inc(a_hi, 1)
                act.wait_ge(r_ready, r.ready("OC"))
                act.wait_ge(y_step, YSTEPS * i + 2)
                nc.scalar.activation(y_now[:], r.bank("OC")[:, 0:D], ACT.Copy, scale=float(D1) ** -0.5).then_inc(r_act, 1)
            act.wait_ge(staged, STAGED * G)
            for name in POST1.names[:4]:
                high1(name, post1)

        @block.vector
        def _(dve):
            n = [0]

            def link(ins, wait=True):
                n[0] += 1
                ins.then_inc(dve_step, 1)
                if wait:
                    dve.wait_ge(dve_step, n[0])

            def settle():
                dve.wait_ge(dve_step, n[0])

            def layer_stats(src, tiles=range(NT)):
                for t in tiles:
                    link(nc.vector.bn_stats(stats[:, t, :], src[:, t, :]), False)
                settle()
                for t in tiles:
                    link(nc.vector.bn_aggr(mv[:, t, :], stats[:, t, :]), False)
                settle()

            for c in range(NCH):
                tiles = range(c * NT // NCH, (c + 1) * NT // NCH)
                dve.wait_ge((x_in, x_in2)[c], 16)
                layer_stats(acc, tiles)
                nc.vector.tensor_scalar(rstd[:, tiles[0]:tiles[-1] + 1], mv[:, tiles[0]:tiles[-1] + 1, 1], EPS_LN, None,
                                        ALU.add).then_inc(xvar_done, 1)
            for t in range(NT):
                if t % (NT // NCH) == 0:
                    dve.wait_ge(const_pool, 2 + t // (NT // NCH))
                nc.vector.tensor_scalar(xn[:, t, :], acc[:, t, :], mv[:, t, 0:1], rstd[:, t:t + 1],
                                        ALU.subtract, ALU.mult).then_inc(xn_done, 1)

            def low(names, r):
                for name in names:
                    bank = r.bank(name)
                    if name[0] == "T":
                        c = int(name[1])
                        dve.wait_ge(g_ready, r.ready(name))
                        dst = fcT[:, :, 2 * c * P:2 * (c + 1) * P] if c < 4 else prT[:, 2 * (c - 4):2 * (c - 4) + 2, :]
                        nc.vector.tensor_copy(dst, bank[:].bitcast(BF16)[:, 0:CH].rearrange("p (a b) -> p a b", a=2)).then_inc(g_lo, 1)
                    elif name == "GM":
                        dve.wait_ge(g_ready, r.ready(name))
                        nc.vector.tensor_scalar(gamma[:, 0:2], bank[:, 0:2], 1.0 / (F * D), None, ALU.mult).then_inc(g_lo, 1)
                        dve.wait_ge(g_lo, r.read(name))
                        link(nc.vector.tensor_scalar(thr[:, 0:2], gamma[:, 0:2], EPS_BIT, 0.5, ALU.add, ALU.mult))
                        link(nc.vector.tensor_scalar(nthr[:, 0:2], thr[:, 0:2], -1.0, None, ALU.mult))
                        link(nc.vector.tensor_scalar(ngamma[:, 0:2], gamma[:, 0:2], -1.0, None, ALU.mult))
                    elif name == "GN":
                        dve.wait_ge(g_ready, r.ready(name))
                        link(nc.vector.tensor_scalar(gamma[:, 2:3], bank[:, 2:3], 1.0 / (3 * D * D), 1e-5, ALU.mult, ALU.max))
                        nc.vector.tensor_scalar(gamma[:, 3:4], bank[:, 3:4], 1.0 / (D * D), 1e-5, ALU.mult, ALU.max).then_inc(g_lo, 1)
                        dve.wait_ge(g_lo, r.read(name))
                        link(nc.vector.tensor_scalar(ngamma[:, 2:4], gamma[:, 2:4], -1.0, None, ALU.mult), False)
                        for c, half_gamma in enumerate((0.5, -0.5)):
                            link(nc.vector.tensor_scalar(thr_l1[:, c, 0:6], gamma[:, 2:3].to_broadcast([P, 6]), half_gamma, None, ALU.mult), False)
                            link(nc.vector.tensor_scalar(thr_l1[:, c, 6:8], gamma[:, 3:4].to_broadcast([P, 2]), half_gamma, None, ALU.mult), False)
                        nc.vector.memset(hrow[:, 5:6], 0.0).then_inc(tern_done, 1)
                    elif name[0] == "O":
                        c = int(name[1])
                        dve.wait_ge(g_ready, r.ready(name))
                        a = acc[:, 2 * c:2 * c + 2, :]
                        nc.vector.tensor_tensor(a, bank[:].rearrange("p (a b) -> p a b", b=D), a, ALU.add).then_inc(g_lo, 1)
                    else:
                        dve.wait_ge(g_hi, r.acted(name))
                        hi, lo = place(name, 0)
                        if name[0] == "Q":
                            nc.vector.scalar_tensor_tensor(out=lo, in0=as_shape(bank, lo), scalar=SCALE, in1=hi.bitcast(F32),
                                                           op0=ALU.mult, op1=ALU.subtract).then_inc(g_lo, 1)
                        else:
                            nc.vector.tensor_tensor(lo, as_shape(bank, lo), hi.bitcast(F32), ALU.subtract).then_inc(g_lo, 1)

            def tern(k, dst, src, w, sig):
                a = above[:, 0:w].rearrange("p (a b) -> p a b", b=src.shape[2])
                link(nc.vector.tensor_scalar(a, src, thr[:, k:k + 1], None, ALU.is_gt))
                ins = nc.vector.scalar_tensor_tensor(out=dst, in0=src, scalar=nthr[:, k:k + 1], in1=a, op0=ALU.is_lt,
                                                     op1=ALU.subtract)
                link(ins)
                if sig:
                    nc.vector.memset(hrow[:, 7:8], 0.0).then_inc(tern_done, 1)

            low(XT + ["Wq", "Wk", "GM"], start)
            tern(0, tern_fc[:], raw_fc[:], 2 * F, True)
            low(["Q00", "Q01", "Wv"], start)
            tern(1, tern_pr[:], raw_pr[:], 2 * F, True)
            low(["K00", "K01", "GN"] + T8, start)
            dve.wait_ge(spill, 32)

            def quantise_x(u, s):
                def after(k):
                    dve.wait_ge(xq_step, XSTEPS * u + k)

                if s == 0:
                    dve.wait_ge(xq_in, 16 * (u + 1))
                    dve.sem_inc(dve_waits, 1)
                    nc.vector.bn_stats(xstats[:], xq_tile[:]).then_inc(xq_step, 1)
                elif s == 1:
                    after(1)
                    dve.sem_inc(dve_waits, 1)
                    nc.vector.bn_aggr(xmv[:], xstats[:]).then_inc(xq_step, 1)
                elif s == 2:
                    after(2)
                    nc.vector.tensor_scalar(xrow[:, 0:1], xmv[:, 1:2], EPS_BIT, None, ALU.add).then_inc(xq_step, 1)
                elif s == 5:
                    after(4)
                    nc.vector.tensor_scalar(xq_tile[:], xq_tile[:], xmv[:, 0:1], xrow[:, 0:1], ALU.subtract, ALU.mult).then_inc(xq_step, 1)
                elif s == 6:
                    after(5)
                    nc.vector.tensor_reduce(xrow[:, 1:2], xq_tile[:], AX.X, ALU.max, apply_absolute_value=True).then_inc(xq_step, 1)
                elif s == 7:
                    after(6)
                    nc.vector.reciprocal(xrow[:, 2:3], xrow[:, 1:2]).then_inc(xq_step, 1)
                elif s == 8:
                    after(7)
                    nc.vector.tensor_scalar(xrow[:, 3:4], xrow[:, 2:3], QB, None, ALU.mult).then_inc(xq_step, 1)
                    nc.vector.tensor_scalar(xrow[:, 4:5], xrow[:, 1:2], 1.0 / QB, None, ALU.mult).then_inc(xq_step, 1)
                elif s == 9:
                    after(9)
                    nc.vector.tensor_scalar(xq_tile[:], xq_tile[:], xrow[:, 3:4], QB, ALU.mult, ALU.min).then_inc(xq_step, 1)
                elif s == 10:
                    after(10)
                    nc.vector.tensor_scalar(xq_tile[:], xq_tile[:], -QB, xrow[:, 4:5], ALU.max, ALU.mult).then_inc(xq_step, 1)

            def row_max(u, s):
                dve.wait_ge(s_ready, 2 * NT * u + s + 1)
                i = TILE[s]
                nc.vector.tensor_reduce(nmax[:, s % 4:s % 4 + 1], score_view(sc[s % 2], i), AX.X if i < 4 else AX.XY,
                                        ALU.max, negate=True).then_inc(max_done, 1)

            def recip(u, s):
                dve.wait_ge(exp_done, 2 * NT * u + s + 1)
                nc.vector.reciprocal(rinv[:, s % 4:s % 4 + 1], rsum[:, s % 4:s % 4 + 1]).then_inc(rcp_done, 1)

            def low_p(u, s):
                i = TILE[s]
                for b in range(TG[s + 1] - TG[s]):
                    w = min(4, i + 1 - 4 * b)
                    dve.wait_ge(t_hi, NTG * u + TG[s] + b + 1)
                    q = (i % 4) * P
                    nc.vector.tensor_tensor(pT[i // 4][1][:, 4 * b:4 * b + w, q:q + P],
                                            tp[(TG[s] + b) % 2][:, 0:w * P].rearrange("p (j q) -> p j q", q=P),
                                            pT[i // 4][0][:, 4 * b:4 * b + w, q:q + P].bitcast(F32),
                                            ALU.subtract).then_inc(t_lo, 1)

            def heads(u, r):
                for s in range(2 * NT):
                    row_max(u, s)
                    quantise_x(u, s)
                    if s >= 1:
                        recip(u, s - 1)
                        low(finished(s - 1, r), r)
                    if s >= LAG:
                        low_p(u, s - LAG)
                recip(u, 2 * NT - 1)
                low(finished(2 * NT - 1, r), r)
                for s in range(2 * NT - LAG, 2 * NT):
                    low_p(u, s)
                low(["AV11"], r)

            def ffn(u, r, k):
                def did(ins, k):
                    ins.then_inc(ffn_step, 1)

                def after(k):
                    dve.wait_ge(ffn_step, FSTEPS * u + k)

                if k == 0:
                    dve.wait_ge(g_hi, r.acted("F1"))
                    for c in range(2):
                        did(nc.vector.bn_stats(hstats[:, c, :], chunk(h, c)), 1 + c)
                    after(2)
                    dve.sem_inc(dve_waits, 1)
                    did(nc.vector.bn_aggr(hmv[:], hstats[:].rearrange("p a b -> p (a b)")), 3)
                    after(3)
                    did(nc.vector.tensor_scalar(hrow[:, 0:1], hmv[:, 1:2], EPS_BIT, None, ALU.add), 4)
                elif k == 1:
                    dve.wait_ge(ffn_pow, u + 1)
                    did(nc.vector.tensor_scalar(h[:], h[:], hmv[:, 0:1], hrow[:, 0:1], ALU.subtract, ALU.mult), 5)
                elif k == 2:
                    after(5)
                    did(nc.vector.tensor_reduce(hrow[:, 1:2], h[:], AX.X, ALU.max, apply_absolute_value=True), 6)
                    after(6)
                    did(nc.vector.reciprocal(hrow[:, 2:3], hrow[:, 1:2]), 7)
                    after(7)
                    did(nc.vector.tensor_scalar(hrow[:, 3:4], hrow[:, 2:3], QB, None, ALU.mult), 8)
                    did(nc.vector.tensor_scalar(hrow[:, 4:5], hrow[:, 1:2], 1.0 / QB, None, ALU.mult), 9)
                elif k == 3:
                    after(9)
                    did(nc.vector.tensor_scalar(h[:], h[:], hrow[:, 3:4], QB, ALU.mult, ALU.min), 10)
                    after(10)
                    did(nc.vector.tensor_scalar(h[:], h[:], -QB, hrow[:, 4:5], ALU.max, ALU.mult), 11)

            def ffn_out(u, r):
                dve.wait_ge(g_ready, r.ready("FP"))
                dve.wait_ge(g_lo, r.read("FP") - 1)
                a = acc[:, bass.ds(u, 1), :].rearrange("p a d -> p (a d)")
                nc.vector.scalar_tensor_tensor(out=a, in0=r.bank("FP")[:, 0:D], scalar=ngamma[:, 1:2], in1=a, op0=ALU.mult,
                                               op1=ALU.add).then_inc(g_lo, 1)
                dve.wait_ge(g_lo, r.read("FP"))

            with dve.Fori(0, PAIRS - 1) as u:
                r = attention_round(u)
                heads(u, r)
                ffn(u, r, 0)
                low(["K00", "Q00"], r)
                ffn(u, r, 1)
                low(["K01", "Q01", "O2"], r)
                ffn(u, r, 2)
                low(["AV10"], r)
                ffn(u, r, 3)
                low(["O3", "H0", "H1", "O0"], r)
                ffn_out(u, r)
                low(["O1"], r)
            u, r = PAIRS - 1, last_round
            heads(u, r)
            ffn(u, r, 0)
            ffn(u, r, 1)
            low(["O2"], r)
            ffn(u, r, 2)
            low(["AV10"], r)
            ffn(u, r, 3)
            low(["O3", "H0", "H1", "O0"], r)
            ffn_out(u, r)
            low(["O1"], r)
            dve.wait_ge(g_lo, last_round.read("O1"))

            dve.wait_ge(l1_in, 16 * L1_LOADS)
            dve.wait_ge(consts1, 1)
            link(nc.vector.tensor_scalar(negs_rows[:], negs_rows[:], -1.0, None, ALU.mult))
            for b in range(2):
                link(nc.vector.scalar_tensor_tensor(out=small[:, 8:8 + HALF], in0=blocks[:].rearrange("p (g d) -> p g d", d=D1)[:, :, 0],
                                                    scalar=1.0, in1=negs_rows[:, b * HALF:(b + 1) * HALF], op0=ALU.mult,
                                                    op1=ALU.mult, accum_out=colw[:, 6 + b:7 + b]))
            pairs = blocks[:].rearrange("p (g c d) -> p c g d", c=2, d=D1)
            for c in range(2):
                link(nc.vector.tensor_reduce(small[:, 1 + c:2 + c], pairs[:, c, :, 0], AX.X, ALU.add))
                link(nc.vector.tensor_scalar(colw[:, 12 + c:13 + c], small[:, 1 + c:2 + c], ngamma[:, 2:3], None, ALU.mult))
            nc.vector.memset(small[:, 4:5], 0.0).then_inc(decay_in, 1)
            layer_stats(acc)
            nc.vector.tensor_scalar(rows[:, 0, :], mv[:, :, 1], EPS_LN, None, ALU.add).then_inc(post_step, 1)
            dve.wait_ge(sums_done, 1)
            for t in range(NT):
                nc.vector.tensor_scalar(x2[:, t, :], acc[:, t, :], mv[:, t, 0:1], rows[:, 0, t:t + 1],
                                        ALU.subtract, ALU.mult).then_inc(x2_done, 1)
            dve.wait_ge(x2_done, NT)

            def squares(src, junk_, k):
                for t in range(NT):
                    link(nc.vector.scalar_tensor_tensor(out=junk_[:, t, :], in0=src[:, t, :], scalar=1.0, in1=src[:, t, :],
                                                        op0=ALU.mult, op1=ALU.mult, accum_out=rows[:, k, t:t + 1]), False)
                settle()

            squares(x2, hq, 1)
            nc.vector.tensor_scalar(rows[:, 1, :], rows[:, 1, :], 1.0 / D, EPS_F32, ALU.mult, ALU.add).then_inc(post_step, 1)
            link(nc.vector.tensor_copy(mg_f[:], mg_i[:]))
            link(nc.vector.tensor_scalar(onehot[:], iota_g[:].rearrange("e (g a) -> e g a", a=1).to_broadcast([2 * E, G, I]),
                                         mg_f[:, 0:1], None, ALU.is_equal))
            dve.wait_ge(sums_done, 2)
            for t in range(NT):
                nc.vector.tensor_scalar(hq[:, t, :], x2[:, t, :], rows[:, 1, t:t + 1], None, ALU.mult).then_inc(hq_done, 1)

            def low1(name, r):
                src = r.bank(name)
                if name in r.order.read_by_act:
                    dve.wait_ge(r_act, r.acted(name))
                else:
                    dve.wait_ge(r_ready, r.ready(name))
                def minus(hi, lo, scale=None):
                    s_ = as_shape(src, lo)
                    if scale is None:
                        return nc.vector.tensor_tensor(lo, s_, hi.bitcast(F32), ALU.subtract)
                    return nc.vector.scalar_tensor_tensor(out=lo, in0=s_, scalar=scale, in1=hi.bitcast(F32), op0=ALU.mult,
                                                          op1=ALU.subtract)
                if name[0] == "T":
                    s_ = src[:].bitcast(BF16)[:, 0:CH].rearrange("p (a b) -> p a b", a=2)
                    ins = nc.vector.tensor_copy(p1T[:] if name == "TP" else
                                                qkvT[:, :, int(name[2]) * 2 * P:(int(name[2]) + 1) * 2 * P], s_)
                elif name == "GT":
                    ins = minus(gT[0][:], gT[1][:])
                elif name[:2] in ("XA", "XB", "OT"):
                    c = int(name[2])
                    k = c // NCH
                    hi, lo = [v[:, k, (c % NCH) * CH:(c % NCH + 1) * CH] for v in (x2T if name[1] == "A" else nT)]
                    ins = minus(hi, lo, None if name[1] == "A" else colw[:, k:k + 1] if name[1] == "B" else colw[:, 2 + k:3 + k])
                elif name == "LG":
                    s_ = src[:, 0:NT * E].rearrange("p (t e) -> p t e", e=E)
                    link(nc.vector.tensor_reduce(gs[:, 0, :], s_, AX.X, ALU.max))
                    ins = nc.vector.tensor_tensor(lg[:], s_, gs[:, 0, :].rearrange("p (t a) -> p t a", a=1).to_broadcast([P, NT, E]),
                                                  ALU.subtract)
                elif name[:2] == "QA":
                    b, c = int(name[2]), int(name[3])
                    dve.wait_ge(decays, 4)
                    ins = nc.vector.scalar_tensor_tensor(
                        out=qdT[:, b, c * CH:(c + 1) * CH].rearrange("p (c t) -> p c t", t=P),
                        in0=src[:].rearrange("p (c t) -> p c t", t=P), scalar=ngamma[:, 2:3],
                        in1=qdecay[:, b:b + 1, :].to_broadcast([P, CH // P, P]), op0=ALU.mult, op1=ALU.mult)
                elif name[:2] == "KA":
                    b, c = int(name[2]), int(name[3])
                    ins = nc.vector.tensor_scalar(k1T[1][:, b, c * CH:(c + 1) * CH], src[:], colw[:, 13:14], None, ALU.mult)
                elif name[:2] == "SL":
                    c = int(name[2])
                    ins = nc.vector.tensor_tensor(selT[E:2 * E, c * CH:(c + 1) * CH], src[E:2 * E, :],
                                                  selT[E:2 * E, c * CH:(c + 1) * CH].bitcast(F32), ALU.subtract)
                elif name == "WG":
                    ins = minus(guT[0][:].rearrange("p k m i -> p k (m i)"), guT[1][:].rearrange("p k m i -> p k (m i)"))
                elif name == "WD":
                    ins = minus(dnT[0][:], dnT[1][:])
                elif name[:2] == "UP":
                    c = int(name[2])
                    dve.wait_ge(r_act, r.acted(f"GA{c}"))
                    ins = nc.vector.tensor_tensor(actv[:, c, :], src[0:I, :], silu[:, c, :], ALU.mult)
                elif name[:2] == "WB":
                    c = int(name[2])
                    dve.wait_ge(r_dve, r.read(name) - 1)
                    ins = nc.vector.tensor_tensor(actv[:, c, :], src[0:I, :], actv[:, c, :], ALU.mult)
                elif name == "KV":
                    ins = nc.vector.scalar_tensor_tensor(
                        out=kd[:].rearrange("p (h d) -> p h d", d=D1), in0=src[:, 0:D].rearrange("p (h d) -> p h d", d=D1),
                        scalar=ngamma[:, 2:3], in1=kdecay[:].rearrange("p (h a) -> p h a", a=1).to_broadcast([P, H1, D1]),
                        op0=ALU.mult, op1=ALU.mult)
                elif name[:2] == "SC":
                    k = int(name[2])
                    ins = nc.vector.tensor_tensor(masked[:, k, :, :], src[:].rearrange("p (h t) -> p h t", t=P),
                                                  causal[:, k, :, :], ALU.mult)
                elif name == "ST":
                    ins = nc.vector.tensor_tensor(state_new[:], src[:, 0:2 * P].rearrange("p (b f) -> p b f", b=2),
                                                  blocks[:].rearrange("p (a f) -> p a f", a=1).to_broadcast([P, 2, P]), ALU.mult)
                elif name[:2] == "PO":
                    c = int(name[2])
                    for t in (2 * c, 2 * c + 1):
                        ins = nc.vector.scalar_tensor_tensor(out=acc[:, t, :], in0=src[:, (t % 2) * D:(t % 2 + 1) * D],
                                                             scalar=factor[:, t:t + 1], in1=acc[:, t, :], op0=ALU.mult, op1=ALU.add)
                ins.then_inc(r_dve, 1)

            for name in PRE1.names:
                if name in PRE1.read_by_dve:
                    low1(name, pre1)
                if name == "LG":
                    dve.wait_ge(r_dve, pre1.read("LG"))
                    nc.vector.memset(small[:, 5:6], 0.0).then_inc(sel_done, 1)
                if name == "XB3":
                    def over_experts(v):
                        return v.rearrange("p (t a) -> p t a", a=1).to_broadcast([P, NT, E])

                    dve.wait_ge(pb_done, 1)
                    link(nc.vector.tensor_reduce(gs[:, 1, :], pb[:], AX.X, ALU.add))
                    link(nc.vector.reciprocal(gs[:, 2, :], gs[:, 1, :]))
                    link(nc.vector.tensor_tensor(pb[:], pb[:], over_experts(gs[:, 2, :]), ALU.mult))
                    for t in range(NT):
                        link(nc.vector.max(top[:, t, :], pb[:, t, :]), False)
                    settle()
                    for t in range(NT):
                        link(nc.vector.match_replace(lg[:, t, :], top[:, t, :], pb[:, t, :], 0.0), False)
                    settle()
                    link(nc.vector.tensor_reduce(gs[:, 1, :], top[:], AX.X, ALU.add))
                    link(nc.vector.reciprocal(gs[:, 2, :], gs[:, 1, :]))
                    link(nc.vector.tensor_tensor(sel[:, :, 0, :], pb[:], lg[:], ALU.subtract))
                    link(nc.vector.tensor_tensor(sel[:, :, 0, :], sel[:, :, 0, :], over_experts(gs[:, 2, :]), ALU.mult))
                    nc.vector.tensor_copy(sel[:, :, 1, :], sel[:, :, 0, :]).then_inc(sel_done, 1)
            dve.wait_ge(prep_done, 1)
            with dve.Fori(0, G) as i:
                r = round1(i)
                for name in ROUND1.names:
                    if name in ROUND1.read_by_dve:
                        low1(name, r)
                    if name in ("SC2", "WB1"):
                        c = 0 if name == "SC2" else 1
                        dve.wait_ge(a_hi, 2 * i + c + 1)
                        nc.vector.tensor_tensor(aT[1][:, c, :], actv[:, c, :], aT[0][:, c, :].bitcast(F32),
                                                ALU.subtract).then_inc(a_lo, 1)
                dve.wait_ge(r_dve, r.read("ST"))
                for b in range(2):
                    nc.vector.scalar_tensor_tensor(out=state[:, b, :], in0=state[:, b, :], scalar=colw[:, 8 + b:9 + b],
                                                   in1=state_new[:, b, :], op0=ALU.mult, op1=ALU.add).then_inc(state_done, 1)
                dve.wait_ge(r_act, r.acted("OC"))
                nc.vector.scalar_tensor_tensor(out=y_square[:], in0=y_now[:], scalar=1.0, in1=y_now[:], op0=ALU.mult,
                                               op1=ALU.mult, accum_out=y_sums[:, 0, :]).then_inc(y_step, 1)
                z_now = o1[:, bass.ds(i, 1), :].rearrange("p a d -> p (a d)")
                nc.vector.scalar_tensor_tensor(out=z_now, in0=y_now[:], scalar=1.0, in1=normw[:], op0=ALU.mult,
                                               op1=ALU.mult).then_inc(y_step, 1)
                dve.wait_ge(y_step, YSTEPS * i + 4)
                nc.vector.scalar_tensor_tensor(out=y_square[:], in0=z_now, scalar=1.0, in1=z_now, op0=ALU.mult,
                                               op1=ALU.mult, accum_out=y_sums[:, 1, :]).then_inc(y_step, 1)
                dve.wait_ge(y_step, YSTEPS * i + 5)
                nc.vector.tensor_scalar(rows[:, 2:4, bass.ds(i, 1)], y_sums[:], 1.0, None, ALU.mult).then_inc(y_step, 1)
                dve.wait_ge(state_done, 2 * i + 4)

            dve.wait_ge(y_step, YSTEPS * G + 2)
            nc.vector.tensor_scalar(rows[:, 2, :], rows[:, 2, :], 1.0 / D, EPS_OUT, ALU.mult, ALU.add).then_inc(y_done, 1)

            def add_experts(c):
                dve.wait_ge(ma_done, 2 + 2 * G - 1 + c // 2)
                a = acc[:, 2 * c:2 * c + 2, :]
                link(nc.vector.tensor_tensor(a, sc[c // 2][:, c % 2, :].rearrange("p (a d) -> p a d", d=D), a, ALU.add), False)

            add_experts(0)
            add_experts(1)
            low1(POST1.names[0], post1)
            dve.wait_ge(sums_done, 3)
            for _k in range(2):
                link(nc.vector.tensor_tensor(rows[:, 3, :], rows[:, 3, :], rows[:, 2, :], ALU.mult))
            nc.vector.tensor_scalar(rows[:, 3, :], rows[:, 3, :], 1.0 / D, EPS_F32, ALU.mult, ALU.add).then_inc(y_done, 1)
            for name in POST1.names[1:4]:
                low1(name, post1)
            add_experts(2)
            add_experts(3)
            dve.wait_ge(sums_done, 4)
            link(nc.vector.scalar_tensor_tensor(out=factor[:], in0=rows[:, 3, :], scalar=ngamma[:, 3:4], in1=rows[:, 2, :],
                                                op0=ALU.mult, op1=ALU.mult))
            for name in POST1.names[4:]:
                low1(name, post1)

        @block.tensor
        def _(pe):
            mm = nc.tensor.matmul

            def free(r, name):
                before = r.order.before[name]
                if before in r.order.read_by_dve:
                    pe.wait_ge(g_lo, r.read(before))
                elif before:
                    pe.wait_ge(g_hi, r.acted(before))
                elif r.order.bank[name] >= 2:
                    pe.wait_ge(t_lo, r.groups + NTG - (3 - r.order.bank[name]))
                elif r is not start:
                    pe.wait_ge(g_lo, r.d - reads_after_bank(r.order.bank[name]))
                return r.bank(name)

            def three(out, lhs, rhs, start, stop, **kw):
                mm(out, lhs[0], rhs[0], start=start, stop=False, **kw)
                mm(out, lhs[0], rhs[1], start=False, stop=False, **kw)
                return mm(out, lhs[1], rhs[0], start=False, stop=stop, **kw)

            def transposes(g, blocks_, idn, dt=None):
                for k, b in enumerate(blocks_):
                    last = nc.tensor.transpose(g[:, k * P:(k + 1) * P], b, idn)
                return last

            def w_transposes(w, r, pair):
                g = free(r, "W" + w)
                pe.wait_ge(*{"q": (q_in, 16 * (pair + 1)), "o": (o_in, 16 * (pair + 1))}.get(w, (kv_in, 32 * (pair + 1))))
                raw = wraw["q" if w == "o" else w]
                transposes(g, [raw[:, a, k * P:(k + 1) * P] for k in range(2) for a in range(2)], ident[:]).then_inc(g_ready, 1)

            def project(name, r):
                a, c = int(name[1]), int(name[2])
                g = free(r, name)
                w = wT[name[0].lower()]
                if name[1:] == "00":
                    pe.wait_ge(g_lo, r.read("W" + name[0].lower()))
                for k in range(KT):
                    last = three(g[:], [v[:, k, a * P:(a + 1) * P] for v in w],
                                 [v[:, k, c * CH:(c + 1) * CH] for v in xnT], k == 0, k == KT - 1)
                last.then_inc(g_ready, 1)

            def values(name, r):
                c = int(name[1])
                g = free(r, name)
                if name == "V0":
                    pe.wait_ge(g_lo, r.d - reads_after("Wv"))
                for t in range(2):
                    for k in range(KT):
                        last = three(g[:, t * 2 * P:(t + 1) * 2 * P], [v[:, k, (2 * c + t) * P:(2 * c + t + 1) * P] for v in xnT],
                                     [v[:, k, :] for v in wT["v"]], k == 0, k == KT - 1)
                last.then_inc(g_ready, 1)

            def scores(u, s, r):
                a, i = s // NT, TILE[s]
                if s == 0:
                    pe.wait_ge(g_lo, r.d - min(reads_after("Q01"), reads_after("K01")))
                if s == NT:
                    pe.wait_ge(g_lo, r.read("K11"))
                if s >= 2:
                    pe.wait_ge(exp_done, 2 * NT * u + s - 1)
                ql, w = [v[:, i * P:(i + 1) * P] for v in qT[a]], widths(i)
                for b, k0, wd in w:
                    mm(sc[s % 2][:, b, 0:wd], ql[0], kT[a][0][:, k0:k0 + wd], start=True, stop=False)
                    mm(sc[s % 2][:, b, 0:wd], ql[0], kT[a][1][:, k0:k0 + wd], start=False, stop=False)
                b, k0, wd = w[-1]
                mm(sc[s % 2][:, b, i * P - k0:i * P - k0 + P], ident_b[:], mask_b[:], start=False, stop=False)
                for b, k0, wd in w:
                    last = mm(sc[s % 2][:, b, 0:wd], ql[1], kT[a][0][:, k0:k0 + wd], start=False, stop=True)
                last.then_inc(s_ready, 1)

            def p_transposes(u, s, r):
                pe.wait_ge(pn_done, 2 * NT * u + s + 1)
                i = TILE[s]
                for b in range(TG[s + 1] - TG[s]):
                    k = TG[s] + b
                    if k >= 2:
                        pe.wait_ge(t_lo, NTG * u + k - 1)
                    else:
                        pe.wait_ge(g_lo, r.d - reads_after_bank(2 + k))
                    transposes(tp[k % 2], [prob[s % 4][:, j * P:(j + 1) * P] for j in range(4 * b, min(4 * b + 4, i + 1))],
                               ident[:]).then_inc(t_ready, 1)

            def attend(u, name, r, j0, j1):
                a, c = int(name[2]), int(name[3])
                J = 4 * (c + 1)
                if j0 == 0:
                    g = free(r, name)
                    pe.wait_ge(t_lo, NTG * u + (TG[NT * a + 4] if c else TG[NT * a + 8]))
                    if name == "AV01":
                        pe.wait_ge(g_lo, r.read("V2"))
                if name == "AV01" and j0 == 6:
                    pe.wait_ge(g_lo, r.read("V3"))
                g = r.bank(name)
                for j in range(j0, j1):
                    q = min(max(0, j - 4 * c) * P, 2 * P)
                    last = three(g[:, q:], [v[:, j, a * P:(a + 1) * P] for v in vv], [v[:, j, q:] for v in pT[c]],
                                 j == 0, j == J - 1)
                if j1 == J:
                    last.then_inc(g_ready, 1)

            def outputs(name, r):
                c = int(name[1])
                g = free(r, name)
                if c in (0, NT // 4):
                    pe.wait_ge(g_lo, r.read("AV10" if c == 0 else "AV11"))
                for t in range(2):
                    for a in range(2):
                        q = (2 * c + t) * P
                        last = three(g[:, t * 2 * P:(t + 1) * 2 * P], [v[:, q:q + P] for v in zT[a]],
                                     [v[:, a, :] for v in wT["o"]], a == 0, a == 1)
                last.then_inc(g_ready, 1)

            def ffn(name, u, r):
                g = free(r, name)
                if name == "FT":
                    pe.wait_ge(xq_step, XSTEPS * (u + 1))
                    last = transposes(g, [xq_tile[:, k * P:(k + 1) * P] for k in range(KT)], ident[:])
                elif name[0] == "F" and name != "FP":
                    c = int(name[1])
                    pe.wait_ge(g_lo, r.read("FT"))
                    for k in range(KT):
                        for n_ in range(2):
                            last = mm(g[:], fxT[n_][:, k, :], fcT[:, k, c * CH:(c + 1) * CH], start=(k == 0 and n_ == 0),
                                      stop=(k == KT - 1 and n_ == 1))
                elif name[0] == "H":
                    c = int(name[1])
                    pe.wait_ge(ffn_step, FSTEPS * u + FSTEPS)
                    last = transposes(g, [h[:, (4 * c + k) * P:(4 * c + k + 1) * P] for k in range(4)], ident[:])
                else:
                    pe.wait_ge(g_lo, r.read("H1"))
                    for k in range(FT_):
                        for n_ in range(2):
                            last = mm(g[:, 0:D], hT[n_][:, k, :], prT[:, k, :], start=(k == 0 and n_ == 0),
                                      stop=(k == FT_ - 1 and n_ == 1))
                last.then_inc(g_ready, 1)

            def beside(u, r, s):
                for x_ in BESIDE[s]:
                    if not isinstance(x_, str):
                        attend(u, x_[0], r, x_[1], x_[2])
                    elif x_ not in r.order.at:
                        continue
                    elif x_[0] in "QK":
                        project(x_, r)
                    elif x_[0] == "V":
                        values(x_, r)
                    elif x_[0] == "W":
                        w_transposes(x_[1], r, u if x_ == "Wo" else u + 1)
                    else:
                        ffn(x_, u, r)

            def heads(u, r):
                r.groups = NTG * u
                for s in range(2 * NT):
                    scores(u, s, r)
                    if s >= LAG:
                        p_transposes(u, s - LAG, r)
                    beside(u, r, s)
                for k in range(LAG):
                    p_transposes(u, 2 * NT - LAG + k, r)
                    attend(u, "AV11", r, 2 * k + 2, 2 * k + 4)

            pe.wait_ge(const_pool, 1)
            for name in XT:
                c = int(name[2])
                kt, c = c // NCH, c % NCH
                g = free(start, name)
                pe.wait_ge(xn_done, 4 * c + 4)
                transposes(g, [xn[:, 4 * c + t, kt * P:(kt + 1) * P] for t in range(4)], ident[:]).then_inc(g_ready, 1)
            w_transposes("q", start, 0)
            w_transposes("k", start, 0)
            g = free(start, "GM")
            pe.wait_ge(absum_done, 2)
            mm(g[:, 0:2], ones[:], absum[:, 0:2], start=True, stop=True).then_inc(g_ready, 1)
            project("Q00", start)
            project("Q01", start)
            w_transposes("v", start, 0)
            project("K00", start)
            project("K01", start)
            g = free(start, "GN")
            pe.wait_ge(absum_done, 4)
            mm(g[:, 2:4], ones[:], absum[:, 2:4], start=True, stop=True).then_inc(g_ready, 1)
            for c in range(8):
                g = free(start, f"T{c}")[:].bitcast(BF16)
                pe.wait_ge(tern_done, 1 if c < 4 else 2)
                if c < 4:
                    b = [tern_fc[:, 2 * c + t, k * P:(k + 1) * P] for k in range(KT) for t in range(2)]
                else:
                    b = [tern_pr[:, k, (2 * (c - 4) + t) * P:(2 * (c - 4) + t + 1) * P] for t in range(2) for k in range(KT)]
                transposes(g, b, ident_b[:]).then_inc(g_ready, 1)
            def after_heads(u, r):
                for name in AFTER:
                    if name not in r.order.at:
                        continue
                    if name[0] in "QK":
                        project(name, r)
                    elif name[0] == "A":
                        attend(u, name, r, 0, 4)
                    elif name[0] == "O":
                        outputs(name, r)
                    else:
                        ffn(name, u, r)

            pe.wait_ge(zero_done, 4)
            with pe.Fori(0, PAIRS - 1) as u:
                r = attention_round(u)
                heads(u, r)
                after_heads(u, r)
            heads(PAIRS - 1, last_round)
            after_heads(PAIRS - 1, last_round)

            def free1(r, name):
                at, o, g, a, d = r.order.at[name], r.order, r.g, r.a, r.d
                if o.before[name]:
                    before = o.before[name]
                elif r is pre1:
                    return r.bank(name)
                else:
                    o = ROUND1
                    before = o.names[o.n - 4 + at]
                    a, d = a - o.na, d - o.nd
                if before in o.read_by_dve:
                    pe.wait_ge(r_dve, d + o.dve[before])
                else:
                    pe.wait_ge(r_act, a + o.act[before])
                return r.bank(name)

            pe.wait_ge(g_lo, last_round.read("O1"))
            pe.wait_ge(consts1, 1)
            for c in range(4):
                last = mm(sc[c // 2][:, c % 2, :], zero_b[:, 0:P], zero_b[:], start=True, stop=True)
            last.then_inc(ma_done, 2)
            pe.wait_ge(tern_in, 16)
            for k in range(4):
                g = free1(pre1, PRE1.names[k])[:].bitcast(BF16)
                if k < 3:
                    b = [tern1[:, 2 * k + t, d * P:(d + 1) * P] for d in range(KT) for t in range(2)]
                else:
                    b = [tern1[:, 6 + t, d * P:(d + 1) * P] for d in range(KT) for t in range(2)]
                transposes(g, b, ident_b[:]).then_inc(r_ready, 1)
            g = free1(pre1, "GT")
            pe.wait_ge(l1_in, 16 * L1_LOADS)
            for k in range(KT):
                last = nc.tensor.transpose(g[:, k * E:(k + 1) * E], graw[:, k * P:(k + 1) * P], ident[0:E, 0:E])
            last.then_inc(r_ready, 1)

            def token_transposes(name, src, done, base, r):
                c = int(name[2])
                g = free1(r, name)
                k, c = c // NCH, c % NCH
                pe.wait_ge(done, base + 4 * c + 4)
                transposes(g, [src[:, 4 * c + t, k * P:(k + 1) * P] for t in range(4)], ident[:]).then_inc(r_ready, 1)

            for c in range(4):
                token_transposes(f"XA{c}", x2, x2_done, 0, pre1)
            g = free1(pre1, "LG")
            pe.wait_ge(r_dve, pre1.read("XA3"))
            for t in range(NT):
                for k in range(KT):
                    last = three(g[:, t * E:(t + 1) * E], [v[:, k, t * P:(t + 1) * P] for v in x2T],
                                 [v[:, k, :] for v in gT], k == 0, k == KT - 1)
            last.then_inc(r_ready, 1)
            for c in range(4):
                token_transposes(f"XB{c}", hq, hq_done, 0, pre1)
            pe.wait_ge(r_dve, pre1.read("XB3"))
            for name in [x_ for x_ in PRE1.names if x_[:2] in ("QA", "KA")]:
                b, c = int(name[2]), int(name[3])
                g = free1(pre1, name)
                o = (D if name[0] == "K" else 0) + b * P
                for k in range(KT):
                    for n_ in range(2):
                        last = mm(g[:], qkvT[:, k, o:o + P], nT[n_][:, k, c * CH:(c + 1) * CH], start=(k == 0 and n_ == 0),
                                  stop=(k == KT - 1 and n_ == 1))
                last.then_inc(r_ready, 1)
            pe.wait_ge(sel_done, 2)
            for c in range(NCH):
                g = free1(pre1, f"SL{c}")
                for t in range(4):
                    last = nc.tensor.transpose(g[0:2 * E, t * P:(t + 1) * P], sel[:, 4 * c + t, :, :].rearrange("p a e -> p (a e)"), ident[:])
                last.then_inc(r_ready, 1)
            pe.wait_ge(r_dve, PRE1.nd)
            pe.wait_ge(r_act, PRE1.na)

            def expert_weights(i, r):
                g = free1(r, "WG")
                pe.wait_ge(gu_in, 16 * (i + 1))
                for k in range(KT):
                    for m_ in range(2):
                        last = nc.tensor.transpose(g[:, (2 * k + m_) * I:(2 * k + m_ + 1) * I], raw_gu[:, m_, k * P:(k + 1) * P], ident[0:I, 0:I])
                last.then_inc(r_ready, 1)
                g = free1(r, "WD")
                pe.wait_ge(dn_in, 16 * (i + 1))
                for k in range(2):
                    last = nc.tensor.transpose(g[0:I, k * P:(k + 1) * P], raw_dn[:, k, :], ident[:])
                last.then_inc(r_ready, 1)

            def expert_hidden(i, r, c):
                for m_, name in enumerate((f"GA{c}", f"UP{c}")):
                    g = free1(r, name)
                    if c == 0 and m_ == 0:
                        pe.wait_ge(r_dve, r.read("WG"))
                    for k in range(KT):
                        last = three(g[0:I, :], [v[:, k, m_, :] for v in guT], [v[:, k, c * CH:(c + 1) * CH] for v in x2T],
                                     k == 0, k == KT - 1)
                    last.then_inc(r_ready, 1)
                g = free1(r, f"WB{c}")
                pe.wait_ge(staged, STAGED * i + 5)
                mm(g[0:I, :], st_hot[:], selT[:, c * CH:(c + 1) * CH], start=True, stop=True).then_inc(r_ready, 1)

            def expert_out(i, r, c):
                pe.wait_ge(a_lo, 2 * i + c + 1)
                for t in range(4):
                    tt = 4 * c + t
                    last = three(sc[tt // 4][:, (tt // 2) % 2, (tt % 2) * D:(tt % 2 + 1) * D],
                                 [v[:, c, t * P:(t + 1) * P] for v in aT], [v[:] for v in dnT], False, False,
                                 skip_group_check=True)
                last.then_inc(ma_done, 1)

            def keys_values(i, r):
                pe.wait_ge(staged, STAGED * i + 2)
                for m_, name in enumerate(("KV", "V")):
                    g = free1(r, name)
                    for k in range(KT):
                        for n_ in range(2):
                            last = mm(g[:, 0:D], st_n[n_][:, k, :], qkvT[:, k, (m_ + 1) * D:(m_ + 2) * D],
                                      start=(k == 0 and n_ == 0), stop=(k == KT - 1 and n_ == 1))
                    last.then_inc(r_ready, 1)

            def chunk_scores(i, r, k):
                g = free1(r, f"SC{k}")
                if k == 0:
                    pe.wait_ge(staged, STAGED * i + 4)
                    pe.wait_ge(q_staged, 4 * i + 4)
                mm(g[:], st_k[k % 2][:, k // 2, :], st_q[:, k // 2, :, :], start=True, stop=True).then_inc(r_ready, 1)

            def chunk_out(i, r):
                g = free1(r, "OC")
                pe.wait_ge(staged, STAGED * (i + 1))
                pe.wait_ge(state_done, 2 * i + 2)
                pe.wait_ge(r_act, r.acted("V"))
                for b in range(2):
                    mm(g[:, b * P:(b + 1) * P], st_qd[:, b, :], state[:, b, :], start=(b == 0), stop=False,
                       skip_group_check=True)
                pe.wait_ge(r_dve, r.read("SC3"))
                for k in range(4):
                    for a in range(4):
                        b, h_ = k // 2, 2 * a + k % 2
                        last = mm(g[:, b * P:(b + 1) * P], masked[:, k, a, :], v_apart[:, b, h_ * P:(h_ + 1) * P],
                                  start=False, stop=(k == 3 and a == 3), skip_group_check=True)
                last.then_inc(r_ready, 1)
                g = free1(r, "ST")
                for b in range(2):
                    last = mm(g[:, b * P:(b + 1) * P], kd[:, b * P:(b + 1) * P], v1[:, b * P:(b + 1) * P], start=True, stop=True)
                last.then_inc(r_ready, 1)

            with pe.Fori(0, G) as i:
                r = round1(i)
                expert_weights(i, r)
                keys_values(i, r)
                chunk_scores(i, r, 0)
                chunk_scores(i, r, 1)
                expert_hidden(i, r, 0)
                chunk_scores(i, r, 2)
                chunk_scores(i, r, 3)
                expert_hidden(i, r, 1)
                expert_out(i, r, 0)
                chunk_out(i, r)
                expert_out(i, r, 1)
            for name in POST1.names[:4]:
                k, c = int(name[2]) // NCH, int(name[2]) % NCH
                g = free1(post1, name)
                pe.wait_ge(y_step, YSTEPS * (4 * c + 4) + 2)
                transposes(g, [o1[:, 4 * c + t, k * P:(k + 1) * P] for t in range(4)], ident[:]).then_inc(r_ready, 1)
            pe.wait_ge(r_dve, post1.read("OT3"))
            for c in range(4):
                g = free1(post1, f"PO{c}")
                for t in range(2):
                    q = (2 * c + t) * P
                    for k in range(KT):
                        for n_ in range(2):
                            last = mm(g[:, t * D:(t + 1) * D], nT[n_][:, k, q:q + P], p1T[:, k, :], start=(k == 0 and n_ == 0),
                                      stop=(k == KT - 1 and n_ == 1))
                last.then_inc(r_ready, 1)


_INS = ["L0_attn_x", "L0_attn_W_K", "L0_attn_W_Q", "L0_attn_W_V", "L0_attn_W_O", "L0_ffn_w_fc", "L0_ffn_w_proj",
        "L1_attn_qkv_w", "L1_attn_qkv_norm_w", "L1_attn_proj_w", "L1_attn_proj_norm_w", "L1_attn_norm_w", "L1_attn_s",
        "L1_ffn_gate_weight", "L1_ffn_gate_up_proj", "L1_ffn_down_proj", "L1_ffn_merge_groups", "L1_ffn_dominant_experts"]
_OUTS = [((1, 1024, 256), "float32")]


def kernel(**inputs):
    import numpy as _np
    import concourse.bacc as _bacc
    from concourse import mybir as _mybir
    from concourse.bass_utils import run_bass_kernel_spmd as _run

    nc = _bacc.Bacc("TRN2", target_bir_lowering=False, num_devices=1)
    arrays, args = {}, []
    for name in _INS:
        a = _np.ascontiguousarray(inputs[name])
        arrays[f"in_{name}_dram"] = a
        args.append(nc.dram_tensor(f"in_{name}_dram", a.shape, _mybir.dt.from_np(a.dtype), kind="ExternalInput").ap())
    for i, (shape, dtype) in enumerate(_OUTS):
        dt = _mybir.dt.from_np(_np.dtype(dtype))
        args.append(nc.dram_tensor(f"out_{i}_dram", shape, dt, kind="ExternalOutput").ap())
    transformer_kernel(nc, *args)
    r = _run(nc, [arrays], core_ids=[0])
    return r.results[0]["out_0_dram"]
```

```python
from contextlib import ExitStack

import numpy as np

import concourse.bass as bass
from concourse import mybir

F32 = mybir.dt.float32
F32R = mybir.dt.float32r
BF16 = mybir.dt.bfloat16
I32 = mybir.dt.int32
ALU = mybir.AluOpType
ACT = mybir.ActivationFunctionType
AX = mybir.AxisListType

P = 128


class Order:

    def __init__(self, names, act, dve, banks):
        self.names, self.at, self.act, self.dve, a, d = names, {}, {}, {}, 0, 0
        self.bank = {name: n % banks if isinstance(banks, int) else banks[n] for n, name in enumerate(names)}
        self.last = {b: name for name, b in self.bank.items()}
        self.before = {}
        for n, name in enumerate(names):
            same = [x for x in names[:n] if self.bank[x] == self.bank[name]]
            self.before[name] = same[-1] if same else None
            a += any(name.startswith(x) for x in act)
            d += any(name.startswith(x) for x in dve)
            self.at[name], self.act[name], self.dve[name] = n, a, d
        self.read_by_dve = {name for name in names if any(name.startswith(x) for x in dve)}
        self.read_by_act = {name for name in names if any(name.startswith(x) for x in act)}
        self.n, self.na, self.nd = len(names), a, d


class Round:

    def __init__(self, order, banks, g, a, d):
        self.order, self.banks, self.g, self.a, self.d = order, banks, g, a, d

    def bank(self, name):
        return self.banks[self.order.bank[name]]

    def ready(self, name):
        return self.g + self.order.at[name] + 1

    def acted(self, name):
        return self.a + self.order.act[name]

    def read(self, name):
        return self.d + self.order.dve[name]


class Memory:

    def __init__(self, nc, first, last):
        self.nc, self.next, self.last = nc, first, last

    def take(self, name, shape, dt=F32):
        size = 1
        for n in shape[1:]:
            size *= n
        size = (size * (2 if dt == BF16 else 4) + 31) // 32 * 32
        at, self.next = self.next, self.next + size
        assert self.next <= self.last, (name, self.next, self.last)
        return self.nc.alloc_sbuf_tensor_at(name, shape, dt, offset=at)


def transformer_kernel(nc, x, w_k, w_q, w_v, w_o, w_fc, w_proj, qkv_w, qkv_norm_w, proj_w, proj_norm_w, norm_w, decay,
                       gate_w, gate_up, down, merge, dominant, out):
    _, TOK, D = x.shape
    H, DH, _ = w_q.shape
    NT, KT = TOK // P, D // P
    PAIRS = H // 2
    F = w_fc.shape[0]
    FT_ = F // P
    CH = 512
    NCH = TOK // CH
    SCALE = float(DH) ** -0.5
    EPS_LN, EPS_BIT, EPS_F32, EPS_OUT = 1e-5, 1e-6, float(np.finfo(np.float32).eps), 1e-6
    QB = 128.0
    H1, D1 = decay.shape[0], D // decay.shape[0]
    E, I2, _ = gate_up.shape
    I = I2 // 2
    G = dominant.shape[0]
    HALF = H1 // 2

    ctx = ExitStack()
    with ctx:
        def sem(name):
            return ctx.enter_context(nc.semaphore(name))

        first, last_byte = (nc.sbuf_base + 31) // 32 * 32, nc.sbuf_usable_end
        always = Memory(nc, first, last_byte)
        ident = always.take("ident", [P, P])
        ident_b = always.take("ident_b", [P, P], BF16)
        mask_b = always.take("mask_b", [P, P], BF16)
        half = always.take("half", [P, NT])
        ones = always.take("ones", [P, P])
        acc = always.take("acc", [P, NT, D])
        stats = always.take("stats", [P, NT, 6])
        mv = always.take("mv", [P, NT, 2])
        rstd = always.take("rstd", [P, NT])
        rows = always.take("rows", [P, 4, NT])
        absum = always.take("absum", [P, 4])
        gamma = always.take("gamma", [P, 4])
        thr = always.take("thr", [P, 4])
        nthr = always.take("nthr", [P, 4])
        thr_l1 = always.take("thr_l1", [P, 2, 8])
        ngamma = always.take("ngamma", [P, 4])
        shared = always.next

        m = Memory(nc, shared, last_byte)
        xnT = [m.take(f"xnT{n}", [P, KT, TOK], F32R) for n in "hl"]
        wraw = {w: m.take(f"raw_{w}", [P, 2, D]) for w in "qkv"}
        wT = {w: [m.take(f"wT_{w}{n}", [P, 2, 2 * P], F32R) for n in "hl"] for w in "qkv"}
        early_end = m.next
        wT["o"] = [m.take(f"wT_o{n}", [P, 2, 2 * P], F32R) for n in "hl"]
        qT = [[m.take(f"qT{a}{n}", [P, TOK], F32R) for n in "hl"] for a in range(2)]
        kT = [[m.take(f"kT{a}{n}", [P, TOK], F32R) for n in "hl"] for a in range(2)]
        vv = [m.take(f"v{n}", [P, NT, 2 * DH], F32R) for n in "hl"]
        prob = [m.take(f"prob{n}", [P, (NT - n) * P]) for n in range(4)]
        nmax = m.take("nmax", [P, 4])
        rsum = m.take("rsum", [P, 4])
        rinv = m.take("rinv", [P, 4])
        xq_tile = m.take("xq_tile", [P, D])
        fxT = [m.take(f"fxT{n}", [P, KT, P], F32R) for n in "hl"]
        fcT = m.take("fcT", [P, KT, F], F32R)
        prT = m.take("prT", [P, FT_, D], F32R)
        h_place = m.next
        h = m.take("h", [P, F])
        hT_place = m.next
        hT = [m.take(f"hT{n}", [P, FT_, P], F32R) for n in "hl"]
        hstats = m.take("hstats", [P, 2, 6])
        hmv = m.take("hmv", [P, 2])
        hrow = m.take("hrow", [P, 8])
        xstats = m.take("xstats", [P, 6])
        xmv = m.take("xmv", [P, 2])
        xrow = m.take("xrow", [P, 8])
        thr_now = m.take("thr_now", [P, 2, 1])
        raw1 = m.take("raw1", [P, D])
        below1 = m.take("below1", [P, D], BF16)
        above1 = m.take("above1", [P, D], BF16)
        tern1_tile = m.take("tern1_tile", [P, D], BF16)
        late = m.next
        pT = [[m.take(f"pT{c}{n}", [P, 4 * (c + 1), CH], F32R) for n in "hl"] for c in range(2)]
        zT = [[m.take(f"zT{a}{n}", [P, TOK], F32R) for n in "hl"] for a in range(2)]
        PT0, PT1, ROW = 4 * CH * 4, 8 * CH * 4, CH * 4
        ends = [late + PT0, late + 2 * PT0, late + 2 * PT0 + PT1, late + 2 * PT0 + 2 * PT1]
        zero_at = [(e - ROW + 2 * P * 4, e - ROW + 3 * P * 4) for e in ends]
        m0 = Memory(nc, zero_at[0][1], zero_at[1][0])
        above_fc = m0.take("above_fc", [P, 2 * F], BF16)
        m0 = Memory(nc, zero_at[1][1], zero_at[2][0])
        xn = m0.take("xn", [P, NT, D])
        tern_pr = m0.take("tern_pr", [P, KT, F], BF16)
        m0 = Memory(nc, zero_at[2][1], zero_at[3][0])
        raw_fc = m0.take("raw_fc", [P, F // P, D])
        tern_fc = m0.take("tern_fc", [P, F // P, D], BF16)
        m0 = Memory(nc, zero_at[3][1], m.next)
        raw_pr = m0.take("raw_pr", [P, KT, F])
        raw_l1 = m0.take("raw_l1", [P, 8, D])
        above_pr = nc.alloc_sbuf_tensor_at("above_pr", [P, 2 * F], BF16, offset=hT_place)
        junk = nc.alloc_sbuf_tensor_at("junk", [P, 2 * F], BF16, offset=h_place)

        m = Memory(nc, shared, early_end)
        tern1 = m.take("tern1", [P, 8, D], BF16)
        qkvT = m.take("qkvT", [P, KT, 3 * D], F32R)
        p1T = m.take("p1T", [P, KT, D], F32R)
        causal = m.take("causal", [P, 4, 4, P])
        dist = m.take("dist", [P, P])
        qdecay = m.take("qdecay", [P, 2, P])
        blocks = m.take("blocks", [P, P])
        quarters = m.take("quarters", [P, 4])
        colw = m.take("colw", [P, 16])
        negs_rows = m.take("negs_rows", [P, H1])
        kdecay = m.take("kdecay", [P, H1])
        normw = m.take("normw", [P, D])
        small = m.take("small", [P, 16])
        graw = m.take("graw", [E, D])
        gT = [m.take(f"gT{n}", [P, KT, E], F32R) for n in "hl"]
        mg_i = m.take("mg_i", [2 * E, 1], I32)
        mg_f = m.take("mg_f", [2 * E, 1])
        iota_g = m.take("iota_g", [2 * E, G])
        onehot = m.take("onehot", [2 * E, G, I])
        dom = m.take("dom", [1, G], I32)
        raw_gu = m.take("raw_gu", [I, 2, D])
        raw_dn = m.take("raw_dn", [P, 2, I])
        zero_b = m.take("zero_b", [1, CH], BF16)
        m = Memory(nc, early_end, last_byte)
        x2 = m.take("x2", [P, NT, D])
        hq = m.take("hq", [P, NT, D])
        x2T = [m.take(f"x2T{n}", [P, KT, TOK], F32R) for n in "hl"]
        nT = [m.take(f"nT{n}", [P, KT, TOK], F32R) for n in "hl"]
        q1T = m.take("q1T", [P, 2, TOK])
        qdT = m.take("qdT", [P, 2, TOK])
        k1T = [m.take(f"k1T{n}", [P, 2, TOK]) for n in "eo"]
        masked = m.take("masked", [P, 4, 4, P])
        y_square = m.take("y_square", [P, 2, D])
        y_sums = m.take("y_sums", [P, 2, 1])
        factor = m.take("factor", [P, NT])
        o1 = m.take("o1", [P, NT, D])
        state = m.take("state", [P, 2, P])
        state_new = m.take("state_new", [P, 2, P])
        kd = m.take("kd", [P, D])
        v1 = m.take("v1", [P, D])
        v_apart = m.take("v_apart", [P, 2, HALF * P])
        st_n = [m.take(f"st_n{n}", [P, KT, P], F32R) for n in "hl"]
        st_k = [m.take(f"st_k{n}", [P, 2, P]) for n in "eo"]
        st_q = m.take("st_q", [P, 2, 4, P])
        q_chunk = m.take("q_chunk", [P, 2, P])
        st_qd = m.take("st_qd", [P, 2, P])
        lg = m.take("lg", [P, NT, E])
        pb = m.take("pb", [P, NT, E])
        sel = m.take("sel", [P, NT, 2, E])
        top = m.take("top", [P, NT, 8])
        gs = m.take("gs", [P, 4, NT])
        selT = m.take("selT", [2 * E, TOK], F32R)
        st_hot = m.take("st_hot", [2 * E, I], F32R)
        guT = [m.take(f"guT{n}", [P, KT, 2, I], F32R) for n in "hl"]
        dnT = [m.take(f"dnT{n}", [I, D], F32R) for n in "hl"]
        silu = m.take("silu", [I, 2, CH])
        logits_T = silu[0:E].rearrange("e c n -> e (c n)")
        actv = m.take("actv", [I, 2, CH])
        aT = [m.take(f"aT{n}", [I, 2, CH], F32R) for n in "hl"]

        xn_dram = nc.dram_tensor("xn_scratch", [P, NT, D], F32)
        raw1_dram = nc.dram_tensor("raw1_scratch", [P, 8, D], F32)
        tern_dram = nc.dram_tensor("tern_scratch", [P, 8, D], BF16)

        sc = [ctx.enter_context(nc.psum_tensor(f"sc{n}", [P, 2, CH], F32)) for n in range(2)]
        tp = [ctx.enter_context(nc.psum_tensor(f"tp{n}", [P, CH], F32)) for n in range(2)]
        gp = [ctx.enter_context(nc.psum_tensor(f"gp{n}", [P, CH], F32)) for n in range(2)]

        x_in, x_in2, fc_in, pr_in, raws_in, q_in, kv_in, o_in = [
            sem(name) for name in "x_in x_in2 fc_in pr_in raws_in q_in kv_in o_in".split()]
        xq_in, raw1_in, l1_in, sems_in, tern_in, gu_in, dn_in = [
            sem(name) for name in "xq_in raw1_in l1_in sems_in tern_in gu_in dn_in".split()]
        spill, tern1_out, out_done = [sem(name) for name in ("spill", "tern1_out", "out_done")]
        const_pool, consts1, consts2, zero_done, dve_step, pool_step, pool_waits, dve_waits = [
            sem(name) for name in "const_pool consts1 consts2 zero_done dve_step pool_step pool_waits dve_waits".split()]
        xvar_done, xn_done, absum_done, scales_done, above_done, tern_done = [
            sem(name) for name in "xvar_done xn_done absum_done scales_done above_done tern_done".split()]
        s_ready, max_done, exp_done, rcp_done, pn_done = [
            sem(name) for name in "s_ready max_done exp_done rcp_done pn_done".split()]
        t_ready, t_hi, t_lo = [sem(name) for name in ("t_ready", "t_hi", "t_lo")]
        g_ready, g_hi, g_lo = [sem(name) for name in ("g_ready", "g_hi", "g_lo")]
        xq_step, ffn_step, ffn_pow, tern1_step, tern1_done = [
            sem(name) for name in "xq_step ffn_step ffn_pow tern1_step tern1_done".split()]
        r_ready, r_act, r_dve = [sem(name) for name in ("r_ready", "r_act", "r_dve")]
        post_step, sums_done, x2_done, hq_done, hq_late = [
            sem(name) for name in "post_step sums_done x2_done hq_done hq_late".split()]
        decay_in, decays, masks_done, prep_done, pb_done, sel_done = [
            sem(name) for name in "decay_in decays masks_done prep_done pb_done sel_done".split()]
        staged, state_done, a_hi, a_lo, ma_done = [sem(name) for name in ("staged", "state_done", "a_hi", "a_lo", "ma_done")]
        y_step, y_done = [sem(name) for name in ("y_step", "y_done")]

        XT = [f"XT{k * NCH + c}" for c in range(NCH) for k in range(KT)]
        T8 = [f"U{n}" for n in range(4)] + [f"T{n}" for n in range(4, 8)]
        ACT_READS = ("XT", "U", "W", "Q", "K", "V", "AV", "FT", "F0", "F1", "H", "GT")
        DVE_READS = ("XT", "W", "Q", "K", "V", "AV", "FT", "H", "GM", "GN", "GT", "T", "O", "FP")
        START = Order(XT + ["Wq", "Wk", "Q00", "Q01", "Wv", "GM", "K00", "K01"] + T8 + ["GN"], ACT_READS, DVE_READS, 2)
        BESIDE = {0: ["V0"], 1: ["Q10"], 2: ["K10"], 3: ["V1"], 4: ["K11"], 5: ["Q11"], 6: ["V2", "Wo"],
                  8: [("AV01", 0, 2), "V3", ("AV01", 2, 4)], 9: [("AV01", 4, 6)], 10: [("AV01", 6, 8)],
                  11: [("AV00", 0, 2)], 12: ["FT", ("AV00", 2, 4)], 13: ["Wq"], 14: ["Wk"],
                  15: ["Wv", ("AV11", 0, 2)], 16: [("AV11", 2, 4)], 18: [("AV11", 4, 6), ("AV11", 6, 8)]}
        WITH_TILES = ["V0", "Q10", "K10", "V1", "K11", "Q11", "V2", "Wo", "V3", "AV01", "FT", "AV00", "Wq", "Wk",
                      "Wv", "AV11"]
        TILE_BANKS = [0, 1, 0, 1, 0, 1, 0, 1, 1, 0, 0, 1, 0, 1, 0, 1]
        LOWS_FIRST = (6, 9)
        EXP_FIRST = (7,)
        SUMS_LAST = (3, 6)
        AFTER = ["F0", "F1", "K01", "Q00", "K00", "Q01", "O2", "AV10", "O3", "O0", "H0", "H1", "O1", "FP"]
        FFN_STEPS = {"Q00": 1, "O2": 2, "AV10": 3}
        AFTER_LAST = ["F0", "F1", "O2", "AV10", "TQ0", "TQ1", "O3", "O0", "O1", "TQ2", "TP", "H0", "H1", "FP", "GT"]
        BANKS_LAST = [0, 2, 3, 1, 0, 2, 3, 1, 0, 2, 3, 1, 0, 2, 3]
        NAMES = WITH_TILES + AFTER
        BANKS = TILE_BANKS + [0, 2, 3, 1, 0, 2, 3, 1, 0, 2, 3, 1, 0, 2]
        NEXT_PAIR = ("Wq", "Wk", "Wv", "Q00", "K00", "Q01", "K01")
        here = [n for n, name in enumerate(WITH_TILES) if name not in NEXT_PAIR]
        ROUND = Order(NAMES, ACT_READS, DVE_READS, BANKS)
        LAST = Order([NAMES[n] for n in here] + AFTER_LAST, ACT_READS, DVE_READS, [BANKS[n] for n in here] + BANKS_LAST)
        banks4 = [gp[0], gp[1], tp[0], tp[1]]
        start = Round(START, banks4, 0, 0, 0)

        def attention_round(u):
            return Round(LAST if isinstance(u, int) else ROUND, banks4, START.n + u * ROUND.n, START.na + u * ROUND.na,
                         START.nd + u * ROUND.nd)

        def reads_after(name):
            return min(o.nd - o.dve[name] for o in (START, ROUND) if name in o.at)

        def reads_after_bank(b):
            return min(o.nd - o.dve[o.last[b]] for o in (START, ROUND) if b in o.last)

        last_round = attention_round(PAIRS - 1)
        TILE = [NT - 1 - s % NT for s in range(2 * NT)]
        TG = [0]
        for i in TILE:
            TG.append(TG[-1] + (2 if i >= 4 else 1))
        NTG = TG[-1]
        LAG = 3
        FSTEPS = 11
        XSTEPS = 11
        STAGED = 9
        YSTEPS = 3
        L1_LOADS = 3 + 2 * KT + 2

        ACT1 = ("XA", "LT", "XB", "QA", "KA", "SL", "WG", "WD", "V", "GA", "OC", "OT")
        DVE1 = ("XA", "LG", "XB", "QA", "SL", "WG", "WD", "KV", "UP", "WB", "SC", "OC", "ST", "OT", "PO")
        PRE1 = Order(["XA0", "XA2", "XA1", "XA3", "LT0", "LT1", "XB0", "XB2", "XB1", "XB3", "LG"]
                     + [f"{n}{b}{c}" for n in ("QA", "KA") for b in range(2) for c in range(NCH)] + ["SL0", "SL1"], ACT1, DVE1, 4)
        ROUND1 = Order(["KV", "V", "WG", "WD", "SC0", "SC1", "GA0", "UP0", "WB0", "SC2", "SC3", "GA1", "UP1", "WB1",
                        "OC", "ST"], ACT1, DVE1, 4)
        POST1 = Order(["OT0", "OT2", "OT1", "OT3", "PO0", "PO1", "PO2", "PO3"], ACT1, DVE1, 4)
        assert ROUND1.n % 4 == 0
        pre1 = Round(PRE1, banks4, 0, 0, 0)

        def round1(i):
            return Round(ROUND1, banks4, PRE1.n + i * ROUND1.n, PRE1.na + i * ROUND1.na, PRE1.nd + i * ROUND1.nd)

        def round_before(r):
            return Round(ROUND1, banks4, r.g - ROUND1.n, r.a - ROUND1.na, r.d - ROUND1.nd)

        r8 = round1(G)
        post1 = Round(POST1, banks4, r8.g, r8.a, r8.d)

        block = ctx.enter_context(nc.Block())

        def widths(i):
            n = (i + 1) * P
            if n <= CH:
                return [(0, 0, max(n, 2 * P))]
            return [(0, 0, n // 2), (1, n // 2, n // 2)]

        def score_view(t, i):
            n = (i + 1) * P
            return t[:, 0, 0:n] if n <= CH else t[:, :, 0:n // 2]

        def prob_view(t, i):
            n = (i + 1) * P
            return t[:, 0:n] if n <= CH else t[:, 0:n].rearrange("p (b n) -> p b n", b=2)

        def chunk(t, c):
            return t[:, c * CH:(c + 1) * CH]

        def finished(s, r):
            names = [x_ if isinstance(x_, str) else x_[0] for x_ in BESIDE.get(s, ())
                     if isinstance(x_, str) or x_[2] == 4 * (int(x_[0][3]) + 1)]
            return [x_ for x_ in names if x_ in r.order.at]

        def place(name):
            if name[0] == "U":
                return [fcT[:, :, 2 * int(name[1]) * P:2 * (int(name[1]) + 1) * P]]
            if name[:2] == "XT":
                c = int(name[2])
                return [t[:, c // NCH, (c % NCH) * CH:(c % NCH + 1) * CH] for t in xnT]
            if name[0] == "W":
                return [t[:] for t in wT[name[1]]]
            if name[:2] == "AV":
                return [chunk(t, int(name[3])) for t in zT[int(name[2])]]
            if name[0] == "Q":
                return [chunk(t, int(name[2])) for t in qT[int(name[1])]]
            if name[0] == "K":
                return [chunk(t, int(name[2])) for t in kT[int(name[1])]]
            if name[0] == "V":
                c = int(name[1])
                return [t[:, 2 * c:2 * c + 2, :] for t in vv]
            if name == "FT":
                return [t[:] for t in fxT]
            if name == "GT":
                return [t[:] for t in gT]
            if name[0] == "H":
                c = int(name[1])
                return [t[:, 4 * c:4 * c + 4, :] for t in hT]
            raise KeyError(name)

        def diagonal(t, b):
            first_ = t[:, b, 0:D1]
            return bass.AP(first_.tensor, first_.offset, [first_.ap[0], [P + D1, HALF], [1, D1]])

        def as_shape(src, dst):
            n = 1
            for k in dst.shape[1:]:
                n *= k
            s = src[0:dst.shape[0], 0:n]
            return s if len(dst.shape) == 2 else s.rearrange("p (a b) -> p a b", b=dst.shape[2])

        @block.sync
        def _(sp):
            def load_kv(pair):
                for w, src in (("k", w_k), ("v", w_v)):
                    sp.dma_start(wraw[w][:], src[bass.ds(2 * pair, 2)].rearrange("a h d -> h a d")).then_inc(kv_in, 16)

            def load_q(pair):
                sp.dma_start(wraw["q"][:], w_q[bass.ds(2 * pair, 2)].rearrange("a h d -> h a d")).then_inc(q_in, 16)

            def load_o(pair):
                sp.dma_start(wraw["q"][:], w_o.rearrange("(m p) f -> p m f", p=P)[:, :, bass.ds(pair * 2 * DH, 2 * DH)])\
                  .then_inc(o_in, 16)

            def load_xq(t):
                sp.dma_start(xq_tile[:].rearrange("p (a d) -> p a d", a=1), xn_dram.ap()[:, bass.ds(t, 1), :]).then_inc(xq_in, 16)

            def load_raw1(t):
                sp.dma_start(raw1[:].rearrange("p (a d) -> p a d", a=1), raw1_dram.ap()[:, bass.ds(t, 1), :]).then_inc(raw1_in, 16)

            def store_tern1(t):
                sp.wait_ge(tern1_done, t + 1)
                sp.dma_start(tern_dram.ap()[:, bass.ds(t, 1), :], tern1_tile[:].rearrange("p (a d) -> p a d", a=1)).then_inc(tern1_out, 16)

            for c in range(NCH):
                tiles = slice(c * NT // NCH, (c + 1) * NT // NCH)
                sp.dma_start(acc[:, tiles, :], x[0].rearrange("(t p) d -> p t d", p=P)[:, tiles, :]).then_inc((x_in, x_in2)[c], 16)
            load_q(0)
            load_kv(0)
            sp.dma_start(raw_fc[:], w_fc.rearrange("(t p) d -> p t d", p=P)).then_inc(fc_in, 16)
            sp.dma_start(raw_pr[:], w_proj.rearrange("(t p) f -> p t f", p=P)).then_inc(pr_in, 16)
            sp.dma_start(raw_l1[:, 0:6, :], qkv_w.rearrange("(t p) d -> p t d", p=P)).then_inc(raws_in, 16)
            sp.dma_start(raw_l1[:, 6:8, :], proj_w.rearrange("(t p) d -> p t d", p=P)).then_inc(raws_in, 16)
            sp.wait_ge(g_ready, start.ready("Wq"))
            load_o(0)
            sp.wait_ge(g_ready, start.ready("Wv"))
            load_kv(1)
            sp.wait_ge(xn_done, NT)
            sp.dma_start(xn_dram.ap(), xn[:]).then_inc(spill, 16)
            sp.wait_ge(raws_in, 32)
            sp.dma_start(raw1_dram.ap(), raw_l1[:]).then_inc(spill, 16)
            sp.wait_ge(spill, 32)
            load_xq(0)
            load_raw1(0)

            def prefetch(u, r, more):
                for name in WITH_TILES:
                    load = {"FT": load_xq, "Wo": load_q, "Wq": load_o}.get(name)
                    if load or (name == "Wv" and more):
                        sp.wait_ge(g_ready, r.ready(name))
                    if load:
                        load(u + 1)
                    elif name == "Wv" and more:
                        load_kv(u + 2)
                store_tern1(u)
                load_raw1(u + 1)

            with sp.Fori(0, PAIRS - 2) as u:
                prefetch(u, attention_round(u), True)
            u = PAIRS - 2
            prefetch(u, Round(ROUND, banks4, START.n + u * ROUND.n, 0, 0), False)

            sp.wait_ge(g_ready, last_round.ready("V3"))
            sp.dma_start(graw[:], gate_w).then_inc(l1_in, 16)
            sp.dma_start(normw[:], norm_w.partition_broadcast(P)).then_inc(l1_in, 16)
            sp.dma_start(negs_rows[:], decay.partition_broadcast(P)).then_inc(l1_in, 16)
            for k in range(KT):
                for c, v in ((0, qkv_norm_w), (2, proj_norm_w)):
                    sp.dma_start(colw[:, c + k:c + k + 1], v[k * P:(k + 1) * P].rearrange("(p a) -> p a", a=1)).then_inc(l1_in, 16)
            for n in range(2):
                sp.dma_start(mg_i[n * E:(n + 1) * E, :], merge.rearrange("(e a) -> e a", a=1)).then_inc(l1_in, 16)
            store_tern1(PAIRS - 1)
            sp.wait_ge(tern1_out, 16 * PAIRS)
            sp.dma_start(tern1[:], tern_dram.ap()).then_inc(tern_in, 16)
            sp.dma_start(dom[:], dominant.rearrange("(a g) -> a g", a=1)).then_inc(sems_in, 16)
            sp.wait_ge(sems_in, 16)

            def load_expert(i):
                e = sp.value_load(dom[0:1, bass.ds(i, 1)], min_val=0, max_val=E - 1)
                sp.dma_start(raw_gu[:], gate_up[bass.ds(e, 1)].rearrange("a (m i) d -> (a i) m d", m=2)).then_inc(gu_in, 16)
                sp.dma_start(raw_dn[:], down[bass.ds(e, 1)].rearrange("a (m p) i -> (a p) m i", p=P)).then_inc(dn_in, 16)

            load_expert(0)
            with sp.Fori(0, G - 1) as i:
                sp.wait_ge(r_ready, round1(i).ready("WD"))
                load_expert(i + 1)
            for t in range(NT):
                if t % 2 == 0:
                    sp.wait_ge(r_dve, post1.read(f"PO{t // 2}"))
                sp.dma_start(out[0].rearrange("(t p) d -> p t d", p=P)[:, t, :], acc[:, t, :]).then_inc(out_done, 16)
            sp.wait_ge(out_done, 16 * NT)

        @block.gpsimd
        def _(pool):
            n = [0]

            def link(ins):
                n[0] += 1
                ins.then_inc(pool_step, 1)
                pool.wait_ge(pool_step, n[0])

            link(nc.gpsimd.memset(ident[:], 0.0))
            link(nc.gpsimd.affine_select(out=ident[:], in_=ident[:], compare_op=ALU.not_equal, fill=1.0, base=0,
                                         pattern=[[-1, P]], channel_multiplier=1))
            link(nc.gpsimd.memset(mask_b[:], 0.0))
            link(nc.gpsimd.affine_select(out=mask_b[:], in_=mask_b[:], compare_op=ALU.is_ge, fill=-1e10, base=0,
                                         pattern=[[-1, P]], channel_multiplier=1))
            link(nc.gpsimd.tensor_copy(ident_b[:], ident[:]))
            link(nc.gpsimd.memset(half[:], -0.5))
            nc.gpsimd.memset(ones[:], 1.0).then_inc(const_pool, 1)
            for n_ in range(2):
                nc.gpsimd.memset(pT[1][n_][:, 7, 2 * P:3 * P].bitcast(F32), 0.0).then_inc(zero_done, 1)
                nc.gpsimd.memset(pT[0][n_][:, 3, 2 * P:3 * P].bitcast(F32), 0.0).then_inc(zero_done, 1)
            for c in range(NCH):
                tiles = slice(c * NT // NCH, (c + 1) * NT // NCH)
                pool.wait_ge(xvar_done, c + 1)
                nc.gpsimd.tensor_tensor(rstd[:, tiles], rstd[:, tiles], half[:, tiles], ALU.pow).then_inc(const_pool, 1)

            pool.wait_ge(scales_done, 1)
            pool.wait_ge(pr_in, 16)
            nc.gpsimd.tensor_scalar(above_pr[:].rearrange("p (a b) -> p a b", b=F), raw_pr[:], thr[:, 1:2], None,
                                    ALU.is_gt).then_inc(above_done, 1)
            pool.wait_ge(scales_done, 2)
            for c, half_gamma in enumerate((0.5, -0.5)):
                link(nc.gpsimd.tensor_scalar(thr_l1[:, c, 0:6], gamma[:, 2:3].to_broadcast([P, 6]), half_gamma, None, ALU.mult))
                link(nc.gpsimd.tensor_scalar(thr_l1[:, c, 6:8], gamma[:, 3:4].to_broadcast([P, 2]), half_gamma, None, ALU.mult))

            def normalise(u, s):
                pool.wait_ge(rcp_done, 2 * NT * u + s + 1)
                pool.sem_inc(pool_waits, 1)
                w = (TILE[s] + 1) * P
                nc.gpsimd.tensor_scalar(prob[s % 4][:, 0:w], prob[s % 4][:, 0:w], rinv[:, s % 4:s % 4 + 1], 1.0,
                                        ALU.mult, ALU.mult).then_inc(pn_done, 1)

            def heads(u):
                pool.wait_ge(xq_step, XSTEPS * u + 3)
                nc.gpsimd.tensor_tensor(xrow[:, 0:1], xrow[:, 0:1], half[:, 0:1], ALU.pow).then_inc(xq_step, 1)
                for s in range(2 * NT):
                    normalise(u, s)
                    if s == 6:
                        pool.wait_ge(raw1_in, 16 * (u + 1))
                        nc.gpsimd.tensor_copy(thr_now[:], thr_l1[:, :, bass.ds(u, 1)]).then_inc(tern1_step, 1)
                        pool.wait_ge(tern1_step, 3 * u + 1)
                        pool.sem_inc(pool_waits, 1)
                        nc.gpsimd.tensor_scalar(above1[:], raw1[:], thr_now[:, 0, 0:1], None, ALU.is_gt).then_inc(tern1_step, 1)
                        nc.gpsimd.tensor_scalar(below1[:], raw1[:], thr_now[:, 1, 0:1], None, ALU.is_lt).then_inc(tern1_step, 1)
                        pool.wait_ge(tern1_step, 3 * u + 3)
                        pool.wait_ge(tern1_out, 16 * u)
                        nc.gpsimd.tensor_tensor(tern1_tile[:], below1[:], above1[:], ALU.subtract).then_inc(tern1_done, 1)

            def ffn_rstd(u):
                pool.wait_ge(ffn_step, FSTEPS * u + 4)
                nc.gpsimd.tensor_tensor(hrow[:, 0:1], hrow[:, 0:1], half[:, 0:1], ALU.pow).then_inc(ffn_pow, 1)

            with pool.Fori(0, PAIRS - 1) as u:
                heads(u)
                ffn_rstd(u)
            heads(PAIRS - 1)

            pool.wait_ge(g_ready, last_round.ready("V3"))
            link(nc.gpsimd.iota(dist[:], pattern=[[1, P]], base=0, channel_multiplier=-1, allow_small_or_imprecise_dtypes=True))
            link(nc.gpsimd.iota(small[:, 0:1], pattern=[[1, 1]], base=P, channel_multiplier=-1, allow_small_or_imprecise_dtypes=True))
            link(nc.gpsimd.iota(qdecay[:], pattern=[[0, 2], [1, P]], base=0, channel_multiplier=0, allow_small_or_imprecise_dtypes=True))
            link(nc.gpsimd.iota(iota_g[:], pattern=[[1, G]], base=0, channel_multiplier=0, allow_small_or_imprecise_dtypes=True))
            link(nc.gpsimd.memset(zero_b[:], 0.0))
            link(nc.gpsimd.memset(quarters[:], 1.0))
            link(nc.gpsimd.affine_select(out=quarters[:], in_=quarters[:], compare_op=ALU.is_ge, fill=0.0, base=0,
                                         pattern=[[-2 * D1, 4]], channel_multiplier=1))
            link(nc.gpsimd.affine_select(out=quarters[:], in_=quarters[:], compare_op=ALU.is_ge, fill=0.0, base=2 * D1 - 1,
                                         pattern=[[2 * D1, 4]], channel_multiplier=-1))
            link(nc.gpsimd.memset(blocks[:], 1.0))
            bv = blocks[:].rearrange("p (g d) -> p g d", d=D1)
            link(nc.gpsimd.affine_select(out=bv, in_=bv, compare_op=ALU.is_ge, fill=0.0, base=0,
                                         pattern=[[-D1, HALF], [0, D1]], channel_multiplier=1))
            link(nc.gpsimd.affine_select(out=bv, in_=bv, compare_op=ALU.is_ge, fill=0.0, base=D1 - 1,
                                         pattern=[[D1, HALF], [0, D1]], channel_multiplier=-1))
            nc.gpsimd.memset(mg_f[:], 0.0).then_inc(consts1, 1)
            ffn_rstd(PAIRS - 1)
            for c in range(NCH):
                tiles = slice(c * NT // NCH, (c + 1) * NT // NCH)
                pool.wait_ge(post_step, c + 1)
                nc.gpsimd.tensor_tensor(rows[:, 0, tiles], rows[:, 0, tiles], half[:, tiles], ALU.pow).then_inc(sums_done, 1)
            pool.wait_ge(sums_done, 2)
            link(nc.gpsimd.tensor_tensor(rows[:, 1, :], rows[:, 0, :], rows[:, 0, :], ALU.mult))
            link(nc.gpsimd.tensor_tensor(rows[:, 1, :], rows[:, 1, :], mv[:, :, 1], ALU.mult))
            link(nc.gpsimd.tensor_scalar(rows[:, 1, :], rows[:, 1, :], EPS_F32, None, ALU.add))
            nc.gpsimd.tensor_tensor(rows[:, 1, :], rows[:, 1, :], half[:], ALU.pow).then_inc(sums_done, 1)
            pool.wait_ge(masks_done, 1)
            cz = causal[:].rearrange("p a b t -> p (a b) t")
            nc.gpsimd.affine_select(out=cz, in_=cz, compare_op=ALU.is_ge, fill=0.0, base=0,
                                    pattern=[[0, H1], [1, P]], channel_multiplier=-1).then_inc(prep_done, 1)

            nc.gpsimd.memset(v_apart[:], 0.0).then_inc(consts2, 1)
            nc.gpsimd.memset(state[:], 0.0).then_inc(state_done, 2)

            pool.wait_ge(r_dve, pre1.read("XB3"))
            with pool.Fori(0, G) as i:
                r = round1(i)
                tok = bass.ds(i * P, P)
                pool.wait_ge(r_ready, round_before(r).ready("V"))
                for n_ in range(2):
                    nc.gpsimd.tensor_copy(st_n[n_][:], nT[n_][:, :, tok].bitcast(F32)).then_inc(staged, 1)
                pool.wait_ge(r_ready, round_before(r).ready("SC3"))
                pool.wait_ge(r_act, r.a - 2)
                for n_ in range(2):
                    nc.gpsimd.tensor_copy(st_k[n_][:], k1T[n_][:, :, tok]).then_inc(staged, 1)
                nc.gpsimd.tensor_copy(q_chunk[:], q1T[:, :, tok]).then_inc(staged, 1)
                pool.wait_ge(staged, STAGED * i + 5)
                for b in range(2):
                    nc.gpsimd.tensor_tensor(st_q[:, b, :, :], q_chunk[:, b:b + 1, :].to_broadcast([P, 4, P]),
                                            quarters[:].rearrange("p (a n) -> p a n", n=1).to_broadcast([P, 4, P]),
                                            ALU.mult).then_inc(staged, 1)
                pool.wait_ge(r_ready, round_before(r).ready("WB1"))
                nc.gpsimd.tensor_copy(st_hot[:].rearrange("e (a i) -> e a i", a=1), onehot[:, bass.ds(i, 1), :]).then_inc(staged, 1)
                pool.wait_ge(r_ready, round_before(r).ready("OC"))
                pool.wait_ge(r_dve, r.d - 2)
                nc.gpsimd.tensor_copy(st_qd[:], qdT[:, :, tok]).then_inc(staged, 1)
            for k in range(2):
                pool.wait_ge(y_done, k + 1)
                nc.gpsimd.tensor_tensor(rows[:, 2 + k, :], rows[:, 2 + k, :], half[:], ALU.pow).then_inc(sums_done, 1)

        @block.scalar
        def _(act):
            def high(names, r):
                for name in names:
                    act.wait_ge(g_ready, r.ready(name))
                    if name in ("F0", "F1"):
                        c = int(name[1])
                        nc.scalar.activation(chunk(h, c), r.bank(name)[:], ACT.Gelu, scale=ngamma[:, 0:1]).then_inc(g_hi, 1)
                        continue
                    dst = place(name)[0]
                    if name[0] == "U":
                        nc.scalar.activation(dst, r.bank(name)[:].bitcast(BF16)[:, 0:CH].rearrange("p (a b) -> p a b", a=2),
                                             ACT.Copy).then_inc(g_hi, 1)
                        continue
                    nc.scalar.activation(dst, as_shape(r.bank(name), dst), ACT.Copy,
                                         scale=SCALE if name[0] == "Q" else 1.0).then_inc(g_hi, 1)

            def exp(u, s):
                act.wait_ge(max_done, 2 * NT * u + s + 1)
                if s >= 4:
                    act.wait_ge(t_ready, NTG * u + TG[s - 3])
                nc.scalar.activation(prob_view(prob[s % 4], TILE[s]), score_view(sc[s % 2], TILE[s]), ACT.Exp,
                                     bias=nmax[:, s % 4:s % 4 + 1], accum_out=rsum[:, s % 4:s % 4 + 1]).then_inc(exp_done, 1)

            def high_p(u, s):
                i = TILE[s]
                for b in range(TG[s + 1] - TG[s]):
                    w = min(4, i + 1 - 4 * b)
                    act.wait_ge(t_ready, NTG * u + TG[s] + b + 1)
                    q = (i % 4) * P
                    nc.scalar.activation(pT[i // 4][0][:, 4 * b:4 * b + w, q:q + P],
                                         tp[(TG[s] + b) % 2][:, 0:w * P].rearrange("p (j q) -> p j q", q=P),
                                         ACT.Copy).then_inc(t_hi, 1)

            def heads(u, r):
                for s in range(2 * NT):
                    if s in EXP_FIRST:
                        exp(u, s)
                    if s >= 1:
                        high(finished(s - 1, r), r)
                    if s >= LAG:
                        high_p(u, s - LAG)
                    if s not in EXP_FIRST:
                        exp(u, s)
                high(finished(2 * NT - 1, r), r)
                for s in range(2 * NT - LAG, 2 * NT):
                    high_p(u, s)
                    high(finished(s + LAG, r), r)

            def make_decays():
                act.wait_ge(l1_in, 16 * L1_LOADS)
                act.wait_ge(consts1, 1)
                act.wait_ge(decay_in, 1)
                for b in range(2):
                    nc.scalar.activation(qdecay[:, b, :], qdecay[:, b, :], ACT.Exp, scale=colw[:, 6 + b:7 + b]).then_inc(decays, 1)
                nc.scalar.activation(kdecay[:], negs_rows[:], ACT.Exp, scale=small[:, 0:1]).then_inc(decays, 1)
                nc.scalar.activation(colw[:, 8:10], colw[:, 6:8], ACT.Exp, scale=float(P)).then_inc(decays, 1)
                for a in range(4):
                    for b in range(2):
                        for c in range(2):
                            hh = HALF * b + 2 * a + c
                            last = nc.scalar.activation(causal[:, 2 * b + c, a, :], dist[:], ACT.Exp, scale=negs_rows[:, hh:hh + 1])
                last.then_inc(masks_done, 1)

            def magnitude(k, t):
                w = t.shape[1] * t.shape[2]
                if k:
                    act.wait_ge(absum_done, k)
                nc.scalar.activation(junk[:, 0:w].rearrange("p (a b) -> p a b", b=t.shape[2]), t, ACT.Abs,
                                     accum_out=absum[:, k:k + 1]).then_inc(absum_done, 1)

            high(XT + ["Wq", "Wk"], start)
            act.wait_ge(fc_in, 16)
            magnitude(0, raw_fc[:])
            high(["Q00"], start)
            act.wait_ge(pr_in, 16)
            magnitude(1, raw_pr[:])
            high(["Q01", "Wv", "K00", "K01"], start)
            act.wait_ge(raws_in, 32)
            magnitude(2, raw_l1[:, 0:6, :])
            magnitude(3, raw_l1[:, 6:8, :])
            high(T8[:4], start)
            act.wait_ge(spill, 32)
            act.wait_ge(tern_done, 2)
            with act.Fori(0, PAIRS - 1) as u:
                r = attention_round(u)
                heads(u, r)
                high([x_ for x_ in AFTER if x_ in ROUND.read_by_act], r)
            u, r = PAIRS - 1, last_round
            heads(u, r)
            high(["F0", "F1", "AV10"], r)
            make_decays()
            high(["H0", "H1", "GT"], r)


            def high1(name, r):
                act.wait_ge(r_ready, r.ready(name))
                src = r.bank(name)
                if name[:2] == "LT":
                    d, scale = logits_T[:, int(name[2]) * CH:(int(name[2]) + 1) * CH], 1.0
                elif name[:2] in ("XA", "XB"):
                    c = int(name[2])
                    k = c // NCH
                    d = (x2T if name[1] == "A" else nT)[0][:, k, (c % NCH) * CH:(c % NCH + 1) * CH]
                    scale = 1.0 if name[1] == "A" else colw[:, k:k + 1]
                elif name[:2] == "QA":
                    d, scale = q1T[:, int(name[2]), int(name[3]) * CH:(int(name[3]) + 1) * CH], ngamma[:, 2:3]
                elif name[:2] == "KA":
                    at = slice(int(name[3]) * CH, (int(name[3]) + 1) * CH)
                    nc.scalar.activation(k1T[1][:, int(name[2]), at], src[:], ACT.Copy, scale=colw[:, 13:14])
                    d, scale = k1T[0][:, int(name[2]), at], colw[:, 12:13]
                elif name[:2] == "SL":
                    d, scale = chunk(selT, int(name[2])), 1.0
                elif name == "WG":
                    d, scale = guT[0][:].rearrange("p k m i -> p k (m i)"), 1.0
                elif name == "WD":
                    d, scale = dnT[0][:], 1.0
                else:
                    c = int(name[2])
                    k = c // NCH
                    d, scale = nT[0][:, k, (c % NCH) * CH:(c % NCH + 1) * CH], colw[:, 2 + k:3 + k]
                nc.scalar.activation(d, as_shape(src, d), ACT.Copy, scale=scale).then_inc(r_act, 1)

            for name in PRE1.names:
                if name == "LG":
                    continue
                if name == "LT0":
                    act.wait_ge(x2_done, NT // 2)
                    act.wait_ge(sums_done, 3)
                    for t in range(NT // 2):
                        nc.scalar.activation(hq[:, t, :], x2[:, t, :], ACT.Copy, scale=rows[:, 1, t:t + 1]).then_inc(hq_done, 1)
                if name[:2] == "QA" and name == "QA00":
                    act.wait_ge(sel_done, 1)
                    nc.scalar.activation(pb[:], lg[:], ACT.Exp).then_inc(pb_done, 1)
                if any(name.startswith(v) for v in ACT1):
                    high1(name, pre1)

            act.wait_ge(consts2, 1)
            with act.Fori(0, G) as i:
                r = round1(i)
                act.wait_ge(r_ready, r.ready("V"))
                nc.scalar.activation(v1[:], r.bank("V")[:, 0:D], ACT.Copy, scale=ngamma[:, 2:3])
                for b in range(2):
                    last_ = nc.scalar.activation(diagonal(v_apart, b), r.bank("V")[:, b * P:(b + 1) * P].rearrange(
                        "p (h d) -> p h d", d=D1), ACT.Copy, scale=ngamma[:, 2:3])
                last_.then_inc(r_act, 1)
                high1("WG", r)
                high1("WD", r)
                for c in range(2):
                    name = f"GA{c}"
                    act.wait_ge(r_ready, r.ready(name))
                    act.wait_ge(r_dve, r.d - ROUND1.nd + ROUND1.dve[f"UP{c}"])
                    nc.scalar.activation(silu[:, c, :], r.bank(name)[0:I, :], ACT.Silu).then_inc(r_act, 1)
                    act.wait_ge(r_dve, r.read(f"WB{c}"))
                    act.wait_ge(ma_done, 2 * i + c + 1)
                    nc.scalar.activation(aT[0][:, c, :], actv[:, c, :], ACT.Copy).then_inc(a_hi, 1)
                act.wait_ge(r_ready, r.ready("OC"))
                nc.scalar.activation(y_square[:, 0, :], r.bank("OC")[:, 0:D], ACT.Square, scale=float(D1) ** -0.5,
                                     accum_out=y_sums[:, 0, :]).then_inc(y_step, 1)
                act.wait_ge(y_step, YSTEPS * i + 1)
                act.sem_inc(r_act, 1)
                act.wait_ge(r_dve, r.read("OC"))
                nc.scalar.activation(y_square[:, 1, :], o1[:, bass.ds(i, 1), :].rearrange("p a d -> p (a d)"), ACT.Square,
                                     accum_out=y_sums[:, 1, :]).then_inc(y_step, 1)
                act.wait_ge(y_step, YSTEPS * i + 2)
                nc.scalar.activation(rows[:, 2:4, bass.ds(i, 1)], y_sums[:], ACT.Copy).then_inc(y_step, 1)
            act.wait_ge(staged, STAGED * G)
            for name in POST1.names[:4]:
                high1(name, post1)

        @block.vector
        def _(dve):
            n = [0]

            def link(ins, wait=True):
                n[0] += 1
                ins.then_inc(dve_step, 1)
                if wait:
                    dve.wait_ge(dve_step, n[0])

            def settle():
                dve.wait_ge(dve_step, n[0])

            def layer_stats(src, tiles=range(NT)):
                for t in tiles:
                    link(nc.vector.bn_stats(stats[:, t, :], src[:, t, :]), False)
                settle()
                for t in tiles:
                    link(nc.vector.bn_aggr(mv[:, t, :], stats[:, t, :]), False)
                settle()

            for c in range(NCH):
                tiles = range(c * NT // NCH, (c + 1) * NT // NCH)
                dve.wait_ge((x_in, x_in2)[c], 16)
                layer_stats(acc, tiles)
                nc.vector.tensor_scalar(rstd[:, tiles[0]:tiles[-1] + 1], mv[:, tiles[0]:tiles[-1] + 1, 1], EPS_LN, None,
                                        ALU.add).then_inc(xvar_done, 1)
            for t in range(NT):
                if t % (NT // NCH) == 0:
                    dve.wait_ge(const_pool, 2 + t // (NT // NCH))
                nc.vector.tensor_scalar(xn[:, t, :], acc[:, t, :], mv[:, t, 0:1], rstd[:, t:t + 1],
                                        ALU.subtract, ALU.mult).then_inc(xn_done, 1)

            def low(names, r):
                for name in names:
                    bank = r.bank(name)
                    if name[:2] in ("TQ", "TP"):
                        dve.wait_ge(g_ready, r.ready(name))
                        nc.vector.tensor_copy(p1T[:] if name == "TP" else qkvT[:, :, int(name[2]) * 2 * P:(int(name[2]) + 1) * 2 * P],
                                              bank[:].bitcast(BF16)[:, 0:CH].rearrange("p (a b) -> p a b", a=2)).then_inc(g_lo, 1)
                    elif name[0] == "T":
                        c = int(name[1])
                        dve.wait_ge(g_ready, r.ready(name))
                        dst = fcT[:, :, 2 * c * P:2 * (c + 1) * P] if c < 4 else prT[:, 2 * (c - 4):2 * (c - 4) + 2, :]
                        nc.vector.tensor_copy(dst, bank[:].bitcast(BF16)[:, 0:CH].rearrange("p (a b) -> p a b", a=2)).then_inc(g_lo, 1)
                    elif name == "GM":
                        dve.wait_ge(g_ready, r.ready(name))
                        nc.vector.tensor_scalar(gamma[:, 0:2], bank[:, 0:2], 1.0 / (F * D), None, ALU.mult).then_inc(g_lo, 1)
                        dve.wait_ge(g_lo, r.read(name))
                        link(nc.vector.tensor_scalar(thr[:, 0:2], gamma[:, 0:2], EPS_BIT, 0.5, ALU.add, ALU.mult))
                        link(nc.vector.tensor_scalar(nthr[:, 0:2], thr[:, 0:2], -1.0, None, ALU.mult))
                        nc.vector.tensor_scalar(ngamma[:, 0:2], gamma[:, 0:2], -1.0, None, ALU.mult).then_inc(scales_done, 1)
                    elif name == "GN":
                        dve.wait_ge(g_ready, r.ready(name))
                        link(nc.vector.tensor_scalar(gamma[:, 2:3], bank[:, 2:3], 1.0 / (3 * D * D), 1e-5, ALU.mult, ALU.max))
                        nc.vector.tensor_scalar(gamma[:, 3:4], bank[:, 3:4], 1.0 / (D * D), 1e-5, ALU.mult, ALU.max).then_inc(g_lo, 1)
                        dve.wait_ge(g_lo, r.read(name))
                        nc.vector.tensor_scalar(ngamma[:, 2:4], gamma[:, 2:4], -1.0, None, ALU.mult).then_inc(scales_done, 1)
                    elif name[0] == "O":
                        c = int(name[1])
                        dve.wait_ge(g_ready, r.ready(name))
                        a = acc[:, 2 * c:2 * c + 2, :]
                        nc.vector.tensor_tensor(a, bank[:].rearrange("p (a b) -> p a b", b=D), a, ALU.add).then_inc(g_lo, 1)
                    else:
                        dve.wait_ge(g_hi, r.acted(name))
                        hi, lo = place(name)
                        if name[0] == "Q":
                            nc.vector.scalar_tensor_tensor(out=lo, in0=as_shape(bank, lo), scalar=SCALE, in1=hi.bitcast(F32),
                                                           op0=ALU.mult, op1=ALU.subtract).then_inc(g_lo, 1)
                        else:
                            nc.vector.tensor_tensor(lo, as_shape(bank, lo), hi.bitcast(F32), ALU.subtract).then_inc(g_lo, 1)

            def tern(k, dst, src, w):
                a = (above_fc, above_pr)[k][:, 0:w].rearrange("p (a b) -> p a b", b=src.shape[2])
                if k == 0:
                    link(nc.vector.tensor_scalar(a, src, thr[:, 0:1], None, ALU.is_gt))
                else:
                    dve.wait_ge(above_done, 1)
                nc.vector.scalar_tensor_tensor(out=dst, in0=src, scalar=nthr[:, k:k + 1], in1=a, op0=ALU.is_lt,
                                               op1=ALU.subtract).then_inc(tern_done, 1)

            low(XT + ["Wq", "Wk", "Q00", "Q01", "Wv", "GM"], start)
            tern(0, tern_fc[:], raw_fc[:], 2 * F)
            low(["K00", "K01"], start)
            tern(1, tern_pr[:], raw_pr[:], 2 * F)
            low(T8[4:] + ["GN"], start)
            dve.wait_ge(spill, 32)

            def quantise_x(u, s):
                def after(k):
                    dve.wait_ge(xq_step, XSTEPS * u + k)

                if s == 0:
                    dve.wait_ge(xq_in, 16 * (u + 1))
                    dve.sem_inc(dve_waits, 1)
                    nc.vector.bn_stats(xstats[:], xq_tile[:]).then_inc(xq_step, 1)
                    after(1)
                    dve.sem_inc(dve_waits, 1)
                    nc.vector.bn_aggr(xmv[:], xstats[:]).then_inc(xq_step, 1)
                    after(2)
                    nc.vector.tensor_scalar(xrow[:, 0:1], xmv[:, 1:2], EPS_BIT, None, ALU.add).then_inc(xq_step, 1)
                elif s == 1:
                    after(4)
                    nc.vector.tensor_scalar(xq_tile[:], xq_tile[:], xmv[:, 0:1], xrow[:, 0:1], ALU.subtract, ALU.mult).then_inc(xq_step, 1)
                elif s == 2:
                    after(5)
                    nc.vector.tensor_reduce(xrow[:, 1:2], xq_tile[:], AX.X, ALU.max, apply_absolute_value=True).then_inc(xq_step, 1)
                    after(6)
                    nc.vector.reciprocal(xrow[:, 2:3], xrow[:, 1:2]).then_inc(xq_step, 1)
                    after(7)
                    nc.vector.tensor_scalar(xrow[:, 3:4], xrow[:, 2:3], QB, None, ALU.mult).then_inc(xq_step, 1)
                    nc.vector.tensor_scalar(xrow[:, 4:5], xrow[:, 1:2], 1.0 / QB, None, ALU.mult).then_inc(xq_step, 1)
                elif s == 3:
                    after(9)
                    nc.vector.tensor_scalar(xq_tile[:], xq_tile[:], xrow[:, 3:4], QB, ALU.mult, ALU.min).then_inc(xq_step, 1)
                    after(10)
                    nc.vector.tensor_scalar(xq_tile[:], xq_tile[:], -QB, xrow[:, 4:5], ALU.max, ALU.mult).then_inc(xq_step, 1)

            def row_max(u, s):
                dve.wait_ge(s_ready, 2 * NT * u + s + 1)
                i = TILE[s]
                nc.vector.tensor_reduce(nmax[:, s % 4:s % 4 + 1], score_view(sc[s % 2], i), AX.X if i < 4 else AX.XY,
                                        ALU.max, negate=True).then_inc(max_done, 1)

            def recip(u, s):
                dve.wait_ge(exp_done, 2 * NT * u + s + 1)
                nc.vector.reciprocal(rinv[:, s % 4:s % 4 + 1], rsum[:, s % 4:s % 4 + 1]).then_inc(rcp_done, 1)

            def low_p(u, s):
                i = TILE[s]
                for b in range(TG[s + 1] - TG[s]):
                    w = min(4, i + 1 - 4 * b)
                    dve.wait_ge(t_hi, NTG * u + TG[s] + b + 1)
                    q = (i % 4) * P
                    nc.vector.tensor_tensor(pT[i // 4][1][:, 4 * b:4 * b + w, q:q + P],
                                            tp[(TG[s] + b) % 2][:, 0:w * P].rearrange("p (j q) -> p j q", q=P),
                                            pT[i // 4][0][:, 4 * b:4 * b + w, q:q + P].bitcast(F32),
                                            ALU.subtract).then_inc(t_lo, 1)

            def heads(u, r):
                for s in range(2 * NT):
                    if s in LOWS_FIRST:
                        low(finished(s - 1, r), r)
                    row_max(u, s)
                    quantise_x(u, s)
                    if s >= 1 and s not in SUMS_LAST:
                        recip(u, s - 1)
                    if s >= 1 and s not in LOWS_FIRST:
                        low(finished(s - 1, r), r)
                    if s >= LAG:
                        low_p(u, s - LAG)
                    if s in SUMS_LAST:
                        recip(u, s - 1)
                recip(u, 2 * NT - 1)
                low(finished(2 * NT - 1, r), r)
                for s in range(2 * NT - LAG, 2 * NT):
                    low_p(u, s)
                    low(finished(s + LAG, r), r)

            def ffn(u, r, k):
                def did(ins, k):
                    ins.then_inc(ffn_step, 1)

                def after(k):
                    dve.wait_ge(ffn_step, FSTEPS * u + k)

                if k == 0:
                    dve.wait_ge(g_hi, r.acted("F1"))
                    for c in range(2):
                        did(nc.vector.bn_stats(hstats[:, c, :], chunk(h, c)), 1 + c)
                    after(2)
                    dve.sem_inc(dve_waits, 1)
                    did(nc.vector.bn_aggr(hmv[:], hstats[:].rearrange("p a b -> p (a b)")), 3)
                    after(3)
                    did(nc.vector.tensor_scalar(hrow[:, 0:1], hmv[:, 1:2], EPS_BIT, None, ALU.add), 4)
                elif k == 1:
                    dve.wait_ge(ffn_pow, u + 1)
                    did(nc.vector.tensor_scalar(h[:], h[:], hmv[:, 0:1], hrow[:, 0:1], ALU.subtract, ALU.mult), 5)
                elif k == 2:
                    after(5)
                    did(nc.vector.tensor_reduce(hrow[:, 1:2], h[:], AX.X, ALU.max, apply_absolute_value=True), 6)
                    after(6)
                    did(nc.vector.reciprocal(hrow[:, 2:3], hrow[:, 1:2]), 7)
                    after(7)
                    did(nc.vector.tensor_scalar(hrow[:, 3:4], hrow[:, 2:3], QB, None, ALU.mult), 8)
                    did(nc.vector.tensor_scalar(hrow[:, 4:5], hrow[:, 1:2], 1.0 / QB, None, ALU.mult), 9)
                elif k == 3:
                    after(9)
                    did(nc.vector.tensor_scalar(h[:], h[:], hrow[:, 3:4], QB, ALU.mult, ALU.min), 10)
                    after(10)
                    did(nc.vector.tensor_scalar(h[:], h[:], -QB, hrow[:, 4:5], ALU.max, ALU.mult), 11)

            def ffn_out(u, r):
                dve.wait_ge(g_ready, r.ready("FP"))
                dve.wait_ge(g_lo, r.read("FP") - 1)
                a = acc[:, bass.ds(u, 1), :].rearrange("p a d -> p (a d)")
                nc.vector.scalar_tensor_tensor(out=a, in0=r.bank("FP")[:, 0:D], scalar=ngamma[:, 1:2], in1=a, op0=ALU.mult,
                                               op1=ALU.add).then_inc(g_lo, 1)
                dve.wait_ge(g_lo, r.read("FP"))

            with dve.Fori(0, PAIRS - 1) as u:
                r = attention_round(u)
                heads(u, r)
                ffn(u, r, 0)
                for name in [x_ for x_ in AFTER if x_ in ROUND.read_by_dve]:
                    if name == "FP":
                        ffn_out(u, r)
                    else:
                        low([name], r)
                    if name in FFN_STEPS:
                        ffn(u, r, FFN_STEPS[name])
            u, r = PAIRS - 1, last_round
            heads(u, r)
            ffn(u, r, 0)
            ffn(u, r, 1)
            low(["O2"], r)
            ffn(u, r, 2)
            low(["AV10"], r)
            dve.wait_ge(l1_in, 16 * L1_LOADS)
            dve.wait_ge(consts1, 1)
            link(nc.vector.tensor_scalar(negs_rows[:], negs_rows[:], -1.0, None, ALU.mult))
            for b in range(2):
                link(nc.vector.scalar_tensor_tensor(out=small[:, 8:8 + HALF], in0=blocks[:].rearrange("p (g d) -> p g d", d=D1)[:, :, 0],
                                                    scalar=1.0, in1=negs_rows[:, b * HALF:(b + 1) * HALF], op0=ALU.mult,
                                                    op1=ALU.mult, accum_out=colw[:, 6 + b:7 + b]))
            nc.vector.memset(small[:, 4:5], 0.0).then_inc(decay_in, 1)
            ffn(u, r, 3)
            pairs = blocks[:].rearrange("p (g c d) -> p c g d", c=2, d=D1)
            for c in range(2):
                link(nc.vector.tensor_reduce(small[:, 1 + c:2 + c], pairs[:, c, :, 0], AX.X, ALU.add))
                link(nc.vector.tensor_scalar(colw[:, 12 + c:13 + c], small[:, 1 + c:2 + c], ngamma[:, 2:3], None, ALU.mult))
            link(nc.vector.tensor_copy(mg_f[:], mg_i[:]))
            link(nc.vector.tensor_scalar(onehot[:], iota_g[:].rearrange("e (g a) -> e g a", a=1).to_broadcast([2 * E, G, I]),
                                         mg_f[:, 0:1], None, ALU.is_equal))
            low(["TQ0", "TQ1", "O3", "O0", "O1", "TQ2", "TP", "H0", "H1"], r)

            def half_stats(c):
                tiles = range(c * NT // NCH, (c + 1) * NT // NCH)
                layer_stats(acc, tiles)
                nc.vector.tensor_scalar(rows[:, 0, tiles[0]:tiles[-1] + 1], mv[:, tiles[0]:tiles[-1] + 1, 1], EPS_LN, None,
                                        ALU.add).then_inc(post_step, 1)

            dve.wait_ge(g_lo, last_round.read("O1"))
            half_stats(0)
            ffn_out(u, r)
            half_stats(1)
            low(["GT"], last_round)
            for t in range(NT):
                if t % (NT // NCH) == 0:
                    dve.wait_ge(sums_done, 1 + t // (NT // NCH))
                nc.vector.tensor_scalar(x2[:, t, :], acc[:, t, :], mv[:, t, 0:1], rows[:, 0, t:t + 1],
                                        ALU.subtract, ALU.mult).then_inc(x2_done, 1)
            link(nc.vector.memset(top[:], 0.0))

            def low1(name, r, i=None):
                src = r.bank(name)
                if name in r.order.read_by_act:
                    dve.wait_ge(r_act, r.acted(name))
                else:
                    dve.wait_ge(r_ready, r.ready(name))
                def minus(hi, lo, scale=None):
                    s_ = as_shape(src, lo)
                    if scale is None:
                        return nc.vector.tensor_tensor(lo, s_, hi.bitcast(F32), ALU.subtract)
                    return nc.vector.scalar_tensor_tensor(out=lo, in0=s_, scalar=scale, in1=hi.bitcast(F32), op0=ALU.mult,
                                                          op1=ALU.subtract)
                if name[:2] in ("XA", "XB", "OT"):
                    c = int(name[2])
                    k = c // NCH
                    hi, lo = [v[:, k, (c % NCH) * CH:(c % NCH + 1) * CH] for v in (x2T if name[1] == "A" else nT)]
                    ins = minus(hi, lo, None if name[1] == "A" else colw[:, k:k + 1] if name[1] == "B" else colw[:, 2 + k:3 + k])
                elif name == "LG":
                    s_ = src[:, 0:NT * E].rearrange("p (t e) -> p t e", e=E)
                    link(nc.vector.tensor_reduce(gs[:, 0, :], s_, AX.X, ALU.max))
                    ins = nc.vector.tensor_tensor(lg[:], s_, gs[:, 0, :].rearrange("p (t a) -> p t a", a=1).to_broadcast([P, NT, E]),
                                                  ALU.subtract)
                elif name[:2] == "QA":
                    b, c = int(name[2]), int(name[3])
                    dve.wait_ge(decays, 4)
                    ins = nc.vector.scalar_tensor_tensor(
                        out=qdT[:, b, c * CH:(c + 1) * CH].rearrange("p (c t) -> p c t", t=P),
                        in0=src[:].rearrange("p (c t) -> p c t", t=P), scalar=ngamma[:, 2:3],
                        in1=qdecay[:, b:b + 1, :].to_broadcast([P, CH // P, P]), op0=ALU.mult, op1=ALU.mult)
                elif name[:2] == "SL":
                    c = int(name[2])
                    ins = nc.vector.tensor_tensor(selT[E:2 * E, c * CH:(c + 1) * CH], src[E:2 * E, :],
                                                  selT[E:2 * E, c * CH:(c + 1) * CH].bitcast(F32), ALU.subtract)
                elif name == "WG":
                    ins = minus(guT[0][:].rearrange("p k m i -> p k (m i)"), guT[1][:].rearrange("p k m i -> p k (m i)"))
                elif name == "WD":
                    ins = minus(dnT[0][:], dnT[1][:])
                elif name[:2] == "UP":
                    c = int(name[2])
                    dve.wait_ge(r_act, r.acted(f"GA{c}"))
                    ins = nc.vector.tensor_tensor(actv[:, c, :], src[0:I, :], silu[:, c, :], ALU.mult)
                elif name[:2] == "WB":
                    c = int(name[2])
                    dve.wait_ge(r_dve, r.read(name) - 1)
                    ins = nc.vector.tensor_tensor(actv[:, c, :], src[0:I, :], actv[:, c, :], ALU.mult)
                elif name == "KV":
                    ins = nc.vector.scalar_tensor_tensor(
                        out=kd[:].rearrange("p (h d) -> p h d", d=D1), in0=src[:, 0:D].rearrange("p (h d) -> p h d", d=D1),
                        scalar=ngamma[:, 2:3], in1=kdecay[:].rearrange("p (h a) -> p h a", a=1).to_broadcast([P, H1, D1]),
                        op0=ALU.mult, op1=ALU.mult)
                elif name[:2] == "SC":
                    k = int(name[2])
                    ins = nc.vector.tensor_tensor(masked[:, k, :, :], src[:].rearrange("p (h t) -> p h t", t=P),
                                                  causal[:, k, :, :], ALU.mult)
                elif name == "OC":
                    ins = nc.vector.scalar_tensor_tensor(out=o1[:, bass.ds(i, 1), :].rearrange("p a d -> p (a d)"), in0=src[:, 0:D],
                                                         scalar=float(D1) ** -0.5, in1=normw[:], op0=ALU.mult, op1=ALU.mult)
                elif name == "ST":
                    ins = nc.vector.tensor_tensor(state_new[:], src[:, 0:2 * P].rearrange("p (b f) -> p b f", b=2),
                                                  blocks[:].rearrange("p (a f) -> p a f", a=1).to_broadcast([P, 2, P]), ALU.mult)
                elif name[:2] == "PO":
                    c = int(name[2])
                    for t in (2 * c, 2 * c + 1):
                        ins = nc.vector.scalar_tensor_tensor(out=acc[:, t, :], in0=src[:, (t % 2) * D:(t % 2 + 1) * D],
                                                             scalar=factor[:, t:t + 1], in1=acc[:, t, :], op0=ALU.mult, op1=ALU.add)
                ins.then_inc(r_dve, 1)

            def over_experts(v):
                return v.rearrange("p (t a) -> p t a", a=1).to_broadcast([P, NT, E])

            for name in PRE1.names:
                if name in PRE1.read_by_dve:
                    low1(name, pre1)
                if name == "XA3":
                    dve.wait_ge(x2_done, NT)
                    dve.wait_ge(sums_done, 3)
                    for t in range(NT // 2, NT):
                        nc.vector.tensor_scalar(hq[:, t, :], x2[:, t, :], rows[:, 1, t:t + 1], None, ALU.mult).then_inc(hq_late, 1)
                if name == "LG":
                    dve.wait_ge(r_dve, pre1.read("LG"))
                    nc.vector.memset(small[:, 5:6], 0.0).then_inc(sel_done, 1)
                if name == "QA00":
                    dve.wait_ge(pb_done, 1)
                    link(nc.vector.tensor_reduce(gs[:, 1, :], pb[:], AX.X, ALU.add), False)
                if name == "QA01":
                    settle()
                    link(nc.vector.reciprocal(gs[:, 2, :], gs[:, 1, :]))
                    link(nc.vector.tensor_tensor(pb[:], pb[:], over_experts(gs[:, 2, :]), ALU.mult), False)
                if name == "QA10":
                    settle()
                    for t in range(NT):
                        link(nc.vector.max(top[:, t, :], pb[:, t, :]), False)
                if name == "QA11":
                    settle()
                    for t in range(NT):
                        link(nc.vector.match_replace(lg[:, t, :], top[:, t, :], pb[:, t, :], 0.0), False)
                    link(nc.vector.tensor_reduce(gs[:, 1, :], top[:], AX.X, ALU.add))
                    link(nc.vector.reciprocal(gs[:, 2, :], gs[:, 1, :]), False)
                    link(nc.vector.tensor_tensor(sel[:, :, 0, :], pb[:], lg[:], ALU.subtract))
                    link(nc.vector.tensor_tensor(sel[:, :, 0, :], sel[:, :, 0, :], over_experts(gs[:, 2, :]), ALU.mult))
                    nc.vector.tensor_copy(sel[:, :, 1, :], sel[:, :, 0, :]).then_inc(sel_done, 1)
            dve.wait_ge(prep_done, 1)
            with dve.Fori(0, G) as i:
                r = round1(i)
                for name in ROUND1.names:
                    if name in ROUND1.read_by_dve:
                        low1(name, r, i)
                    if name in ("SC2", "WB1"):
                        c = 0 if name == "SC2" else 1
                        dve.wait_ge(a_hi, 2 * i + c + 1)
                        nc.vector.tensor_tensor(aT[1][:, c, :], actv[:, c, :], aT[0][:, c, :].bitcast(F32),
                                                ALU.subtract).then_inc(a_lo, 1)
                dve.wait_ge(r_dve, r.read("ST"))
                for b in range(2):
                    nc.vector.scalar_tensor_tensor(out=state[:, b, :], in0=state[:, b, :], scalar=colw[:, 8 + b:9 + b],
                                                   in1=state_new[:, b, :], op0=ALU.mult, op1=ALU.add).then_inc(state_done, 1)
                dve.wait_ge(state_done, 2 * i + 4)

            dve.wait_ge(y_step, YSTEPS * G)
            nc.vector.tensor_scalar(rows[:, 2, :], rows[:, 2, :], 1.0 / D, EPS_OUT, ALU.mult, ALU.add).then_inc(y_done, 1)

            def add_experts(c):
                dve.wait_ge(ma_done, 2 + 2 * G - 1 + c // 2)
                a = acc[:, 2 * c:2 * c + 2, :]
                link(nc.vector.tensor_tensor(a, sc[c // 2][:, c % 2, :].rearrange("p (a d) -> p a d", d=D), a, ALU.add), False)

            for name in POST1.names[:2]:
                low1(name, post1)
            dve.wait_ge(sums_done, 4)
            for _k in range(2):
                link(nc.vector.tensor_tensor(rows[:, 3, :], rows[:, 3, :], rows[:, 2, :], ALU.mult))
            nc.vector.tensor_scalar(rows[:, 3, :], rows[:, 3, :], 1.0 / D, EPS_F32, ALU.mult, ALU.add).then_inc(y_done, 1)
            for name in POST1.names[2:4]:
                low1(name, post1)
            for c in range(4):
                add_experts(c)
            settle()
            dve.wait_ge(sums_done, 5)
            link(nc.vector.scalar_tensor_tensor(out=factor[:], in0=rows[:, 3, :], scalar=ngamma[:, 3:4], in1=rows[:, 2, :],
                                                op0=ALU.mult, op1=ALU.mult))
            for name in POST1.names[4:]:
                low1(name, post1)

        @block.tensor
        def _(pe):
            mm = nc.tensor.matmul

            def free(r, name):
                before = r.order.before[name]
                if before in r.order.read_by_dve:
                    pe.wait_ge(g_lo, r.read(before))
                elif before:
                    pe.wait_ge(g_hi, r.acted(before))
                elif r.order.bank[name] >= 2:
                    pe.wait_ge(t_lo, r.groups + NTG - (3 - r.order.bank[name]))
                elif r is not start:
                    pe.wait_ge(g_lo, r.d - reads_after_bank(r.order.bank[name]))
                return r.bank(name)

            def three(out, lhs, rhs, start, stop, **kw):
                mm(out, lhs[0], rhs[0], start=start, stop=False, **kw)
                mm(out, lhs[0], rhs[1], start=False, stop=False, **kw)
                return mm(out, lhs[1], rhs[0], start=False, stop=stop, **kw)

            def transposes(g, blocks_, idn):
                for k, b in enumerate(blocks_):
                    last = nc.tensor.transpose(g[:, k * P:(k + 1) * P], b, idn)
                return last

            def w_transposes(w, r, pair):
                g = free(r, "W" + w)
                pe.wait_ge(*{"q": (q_in, 16 * (pair + 1)), "o": (o_in, 16 * (pair + 1))}.get(w, (kv_in, 32 * (pair + 1))))
                raw = wraw["q" if w == "o" else w]
                transposes(g, [raw[:, a, k * P:(k + 1) * P] for k in range(2) for a in range(2)], ident[:]).then_inc(g_ready, 1)

            def project(name, r):
                a, c = int(name[1]), int(name[2])
                g = free(r, name)
                w = wT[name[0].lower()]
                if name[1:] == "00":
                    pe.wait_ge(g_lo, r.read("W" + name[0].lower()))
                for k in range(KT):
                    last = three(g[:], [v[:, k, a * P:(a + 1) * P] for v in w],
                                 [v[:, k, c * CH:(c + 1) * CH] for v in xnT], k == 0, k == KT - 1)
                last.then_inc(g_ready, 1)

            def values(name, r):
                c = int(name[1])
                g = free(r, name)
                if name == "V0":
                    pe.wait_ge(g_lo, r.d - reads_after("Wv"))
                for t in range(2):
                    for k in range(KT):
                        last = three(g[:, t * 2 * P:(t + 1) * 2 * P], [v[:, k, (2 * c + t) * P:(2 * c + t + 1) * P] for v in xnT],
                                     [v[:, k, :] for v in wT["v"]], k == 0, k == KT - 1)
                last.then_inc(g_ready, 1)

            def scores(u, s, r):
                a, i = s // NT, TILE[s]
                if s == 0:
                    pe.wait_ge(g_lo, r.d - min(reads_after("Q01"), reads_after("K01")))
                if s == NT:
                    pe.wait_ge(g_lo, r.read("K11"))
                if s >= 2:
                    pe.wait_ge(exp_done, 2 * NT * u + s - 1)
                ql, w = [v[:, i * P:(i + 1) * P] for v in qT[a]], widths(i)
                for b, k0, wd in w:
                    mm(sc[s % 2][:, b, 0:wd], ql[0], kT[a][0][:, k0:k0 + wd], start=True, stop=False)
                    mm(sc[s % 2][:, b, 0:wd], ql[0], kT[a][1][:, k0:k0 + wd], start=False, stop=False)
                b, k0, wd = w[-1]
                mm(sc[s % 2][:, b, i * P - k0:i * P - k0 + P], ident_b[:], mask_b[:], start=False, stop=False)
                for b, k0, wd in w:
                    last = mm(sc[s % 2][:, b, 0:wd], ql[1], kT[a][0][:, k0:k0 + wd], start=False, stop=True)
                last.then_inc(s_ready, 1)

            def p_transposes(u, s, r):
                pe.wait_ge(pn_done, 2 * NT * u + s + 1)
                i = TILE[s]
                for b in range(TG[s + 1] - TG[s]):
                    k = TG[s] + b
                    if k >= 2:
                        pe.wait_ge(t_lo, NTG * u + k - 1)
                    else:
                        pe.wait_ge(g_lo, r.d - reads_after_bank(2 + k))
                    transposes(tp[k % 2], [prob[s % 4][:, j * P:(j + 1) * P] for j in range(4 * b, min(4 * b + 4, i + 1))],
                               ident[:]).then_inc(t_ready, 1)

            def attend(u, name, r, j0, j1):
                a, c = int(name[2]), int(name[3])
                J = 4 * (c + 1)
                if j0 == 0:
                    g = free(r, name)
                    pe.wait_ge(t_lo, NTG * u + (TG[NT * a + 4] if c else TG[NT * a + 8]))
                    if name == "AV01":
                        pe.wait_ge(g_lo, r.read("V2"))
                if name == "AV01" and j0 < 8 and j1 > 6:
                    pe.wait_ge(g_lo, r.read("V3"))
                g = r.bank(name)
                for j in range(j0, j1):
                    q = min(max(0, j - 4 * c) * P, 2 * P)
                    last = three(g[:, q:], [v[:, j, a * P:(a + 1) * P] for v in vv], [v[:, j, q:] for v in pT[c]],
                                 j == 0, j == J - 1)
                if j1 == J:
                    last.then_inc(g_ready, 1)

            def outputs(name, r):
                c = int(name[1])
                g = free(r, name)
                if c in (0, NT // 4):
                    pe.wait_ge(g_lo, r.read("AV10" if c == 0 else "AV11"))
                for t in range(2):
                    for a in range(2):
                        q = (2 * c + t) * P
                        last = three(g[:, t * 2 * P:(t + 1) * 2 * P], [v[:, q:q + P] for v in zT[a]],
                                     [v[:, a, :] for v in wT["o"]], a == 0, a == 1)
                last.then_inc(g_ready, 1)

            def ffn(name, u, r):
                g = free(r, name)
                if name == "FT":
                    pe.wait_ge(xq_step, XSTEPS * (u + 1))
                    last = transposes(g, [xq_tile[:, k * P:(k + 1) * P] for k in range(KT)], ident[:])
                elif name[0] == "F" and name != "FP":
                    c = int(name[1])
                    pe.wait_ge(g_lo, r.read("FT"))
                    for k in range(KT):
                        for n_ in range(2):
                            last = mm(g[:], fxT[n_][:, k, :], fcT[:, k, c * CH:(c + 1) * CH], start=(k == 0 and n_ == 0),
                                      stop=(k == KT - 1 and n_ == 1))
                elif name[0] == "H":
                    c = int(name[1])
                    pe.wait_ge(ffn_step, FSTEPS * u + FSTEPS)
                    last = transposes(g, [h[:, (4 * c + k) * P:(4 * c + k + 1) * P] for k in range(4)], ident[:])
                else:
                    pe.wait_ge(g_lo, r.read("H1"))
                    for k in range(FT_):
                        for n_ in range(2):
                            last = mm(g[:, 0:D], hT[n_][:, k, :], prT[:, k, :], start=(k == 0 and n_ == 0),
                                      stop=(k == FT_ - 1 and n_ == 1))
                last.then_inc(g_ready, 1)

            def beside(u, r, s):
                for x_ in BESIDE.get(s, ()):
                    if not isinstance(x_, str):
                        attend(u, x_[0], r, x_[1], x_[2])
                    elif x_ not in r.order.at:
                        continue
                    elif x_[0] in "QK":
                        project(x_, r)
                    elif x_[0] == "V":
                        values(x_, r)
                    elif x_[0] == "W":
                        w_transposes(x_[1], r, u if x_ == "Wo" else u + 1)
                    else:
                        ffn(x_, u, r)

            def heads(u, r):
                r.groups = NTG * u
                for s in range(2 * NT):
                    scores(u, s, r)
                    if s >= LAG:
                        p_transposes(u, s - LAG, r)
                    beside(u, r, s)
                for k in range(LAG):
                    p_transposes(u, 2 * NT - LAG + k, r)
                    beside(u, r, 2 * NT + k)

            pe.wait_ge(const_pool, 1)
            for name in XT:
                c = int(name[2])
                kt, c = c // NCH, c % NCH
                g = free(start, name)
                pe.wait_ge(xn_done, 4 * c + 4)
                transposes(g, [xn[:, 4 * c + t, kt * P:(kt + 1) * P] for t in range(4)], ident[:]).then_inc(g_ready, 1)
            w_transposes("q", start, 0)
            w_transposes("k", start, 0)
            project("Q00", start)
            project("Q01", start)
            w_transposes("v", start, 0)
            g = free(start, "GM")
            pe.wait_ge(absum_done, 2)
            mm(g[:, 0:2], ones[:], absum[:, 0:2], start=True, stop=True).then_inc(g_ready, 1)
            project("K00", start)
            project("K01", start)
            for c in range(8):
                g = free(start, T8[c])[:].bitcast(BF16)
                pe.wait_ge(tern_done, 1 if c < 4 else 2)
                if c < 4:
                    b = [tern_fc[:, 2 * c + t, k * P:(k + 1) * P] for k in range(KT) for t in range(2)]
                else:
                    b = [tern_pr[:, k, (2 * (c - 4) + t) * P:(2 * (c - 4) + t + 1) * P] for t in range(2) for k in range(KT)]
                transposes(g, b, ident_b[:]).then_inc(g_ready, 1)
            g = free(start, "GN")
            pe.wait_ge(absum_done, 4)
            mm(g[:, 2:4], ones[:], absum[:, 2:4], start=True, stop=True).then_inc(g_ready, 1)

            def after_heads(u, r):
                for name in AFTER_LAST if r is last_round else AFTER:
                    if name[0] in "QK":
                        project(name, r)
                    elif name[0] == "A":
                        attend(u, name, r, 0, 4)
                    elif name[0] == "O":
                        outputs(name, r)
                    elif name[0] == "T":
                        g = free(r, name)[:].bitcast(BF16)
                        pe.wait_ge(tern_in, 16)
                        t0 = 6 if name == "TP" else 2 * int(name[2])
                        transposes(g, [tern1[:, t0 + t, d * P:(d + 1) * P] for d in range(KT) for t in range(2)],
                                   ident_b[:]).then_inc(g_ready, 1)
                    elif name == "GT":
                        g = free(r, name)
                        pe.wait_ge(l1_in, 16 * L1_LOADS)
                        for k in range(KT):
                            last = nc.tensor.transpose(g[:, k * E:(k + 1) * E], graw[:, k * P:(k + 1) * P], ident[0:E, 0:E])
                        last.then_inc(g_ready, 1)
                    else:
                        ffn(name, u, r)

            pe.wait_ge(zero_done, 4)
            with pe.Fori(0, PAIRS - 1) as u:
                r = attention_round(u)
                heads(u, r)
                after_heads(u, r)
            heads(PAIRS - 1, last_round)
            after_heads(PAIRS - 1, last_round)

            def free1(r, name):
                at, o, g, a, d = r.order.at[name], r.order, r.g, r.a, r.d
                if o.before[name]:
                    before = o.before[name]
                elif r is pre1:
                    pe.wait_ge(g_lo, last_round.read(LAST.last[o.bank[name]]))
                    return r.bank(name)
                else:
                    o = ROUND1
                    before = o.names[o.n - 4 + at]
                    a, d = a - o.na, d - o.nd
                if before in o.read_by_dve:
                    pe.wait_ge(r_dve, d + o.dve[before])
                else:
                    pe.wait_ge(r_act, a + o.act[before])
                return r.bank(name)

            pe.wait_ge(exp_done, 2 * NT * PAIRS)
            pe.wait_ge(consts1, 1)
            for c in range(4):
                last = mm(sc[c // 2][:, c % 2, :], zero_b[:, 0:P], zero_b[:], start=True, stop=True)
            last.then_inc(ma_done, 2)

            def token_transposes(name, src, done, r):
                c = int(name[2])
                g = free1(r, name)
                k, c = c // NCH, c % NCH
                pe.wait_ge(*done[c])
                transposes(g, [src[:, 4 * c + t, k * P:(k + 1) * P] for t in range(4)], ident[:]).then_inc(r_ready, 1)

            for name in PRE1.names[:4]:
                token_transposes(name, x2, ((x2_done, NT // 2), (x2_done, NT)), pre1)
            pe.wait_ge(r_dve, pre1.read("XA3"))
            pe.wait_ge(g_lo, last_round.read("GT"))
            for c in range(NCH):
                g = free1(pre1, f"LT{c}")
                for k in range(KT):
                    last = three(g[0:E, :], [v[:, k, :] for v in gT], [v[:, k, c * CH:(c + 1) * CH] for v in x2T],
                                 k == 0, k == KT - 1)
                last.then_inc(r_ready, 1)
            for name in PRE1.names[6:10]:
                token_transposes(name, hq, ((hq_done, NT // 2), (hq_late, NT // 2)), pre1)
            g = free1(pre1, "LG")
            pe.wait_ge(r_act, pre1.acted("LT1"))
            for t in range(NT):
                last = nc.tensor.transpose(g[:, t * E:(t + 1) * E], logits_T[:, t * P:(t + 1) * P], ident[0:E, 0:E])
            last.then_inc(r_ready, 1)
            pe.wait_ge(r_dve, pre1.read("XB3"))
            for name in [x_ for x_ in PRE1.names if x_[:2] in ("QA", "KA")]:
                b, c = int(name[2]), int(name[3])
                g = free1(pre1, name)
                o = (D if name[0] == "K" else 0) + b * P
                for k in range(KT):
                    for n_ in range(2):
                        last = mm(g[:], qkvT[:, k, o:o + P], nT[n_][:, k, c * CH:(c + 1) * CH], start=(k == 0 and n_ == 0),
                                  stop=(k == KT - 1 and n_ == 1))
                last.then_inc(r_ready, 1)
            pe.wait_ge(sel_done, 2)
            for c in range(NCH):
                g = free1(pre1, f"SL{c}")
                for t in range(4):
                    last = nc.tensor.transpose(g[0:2 * E, t * P:(t + 1) * P], sel[:, 4 * c + t, :, :].rearrange("p a e -> p (a e)"), ident[:])
                last.then_inc(r_ready, 1)
            pe.wait_ge(r_dve, PRE1.nd)
            pe.wait_ge(r_act, PRE1.na)

            def expert_weights(i, r):
                g = free1(r, "WG")
                pe.wait_ge(gu_in, 16 * (i + 1))
                for k in range(KT):
                    for m_ in range(2):
                        last = nc.tensor.transpose(g[:, (2 * k + m_) * I:(2 * k + m_ + 1) * I], raw_gu[:, m_, k * P:(k + 1) * P], ident[0:I, 0:I])
                last.then_inc(r_ready, 1)
                g = free1(r, "WD")
                pe.wait_ge(dn_in, 16 * (i + 1))
                for k in range(2):
                    last = nc.tensor.transpose(g[0:I, k * P:(k + 1) * P], raw_dn[:, k, :], ident[:])
                last.then_inc(r_ready, 1)

            def expert_hidden(i, r, c):
                for m_, name in enumerate((f"GA{c}", f"UP{c}")):
                    g = free1(r, name)
                    if c == 0 and m_ == 0:
                        pe.wait_ge(r_dve, r.read("WG"))
                    for k in range(KT):
                        last = three(g[0:I, :], [v[:, k, m_, :] for v in guT], [v[:, k, c * CH:(c + 1) * CH] for v in x2T],
                                     k == 0, k == KT - 1)
                    last.then_inc(r_ready, 1)
                g = free1(r, f"WB{c}")
                pe.wait_ge(staged, STAGED * i + 8)
                mm(g[0:I, :], st_hot[:], selT[:, c * CH:(c + 1) * CH], start=True, stop=True).then_inc(r_ready, 1)

            def expert_out(i, r, c):
                pe.wait_ge(a_lo, 2 * i + c + 1)
                for t in range(4):
                    tt = 4 * c + t
                    last = three(sc[tt // 4][:, (tt // 2) % 2, (tt % 2) * D:(tt % 2 + 1) * D],
                                 [v[:, c, t * P:(t + 1) * P] for v in aT], [v[:] for v in dnT], False, False,
                                 skip_group_check=True)
                last.then_inc(ma_done, 1)

            def keys_values(i, r):
                pe.wait_ge(staged, STAGED * i + 2)
                for m_, name in enumerate(("KV", "V")):
                    g = free1(r, name)
                    for k in range(KT):
                        for n_ in range(2):
                            last = mm(g[:, 0:D], st_n[n_][:, k, :], qkvT[:, k, (m_ + 1) * D:(m_ + 2) * D],
                                      start=(k == 0 and n_ == 0), stop=(k == KT - 1 and n_ == 1))
                    last.then_inc(r_ready, 1)

            def chunk_scores(i, r, k):
                g = free1(r, f"SC{k}")
                if k == 0:
                    pe.wait_ge(staged, STAGED * i + 7)
                mm(g[:], st_k[k % 2][:, k // 2, :], st_q[:, k // 2, :, :], start=True, stop=True).then_inc(r_ready, 1)

            def chunk_out(i, r):
                g = free1(r, "OC")
                pe.wait_ge(staged, STAGED * (i + 1))
                pe.wait_ge(state_done, 2 * i + 2)
                pe.wait_ge(r_act, r.acted("V"))
                for b in range(2):
                    mm(g[:, b * P:(b + 1) * P], st_qd[:, b, :], state[:, b, :], start=(b == 0), stop=False,
                       skip_group_check=True)
                pe.wait_ge(r_dve, r.read("SC3"))
                for k in range(4):
                    for a in range(4):
                        b, h_ = k // 2, 2 * a + k % 2
                        last = mm(g[:, b * P:(b + 1) * P], masked[:, k, a, :], v_apart[:, b, h_ * P:(h_ + 1) * P],
                                  start=False, stop=(k == 3 and a == 3), skip_group_check=True)
                last.then_inc(r_ready, 1)
                g = free1(r, "ST")
                for b in range(2):
                    last = mm(g[:, b * P:(b + 1) * P], kd[:, b * P:(b + 1) * P], v1[:, b * P:(b + 1) * P], start=True, stop=True)
                last.then_inc(r_ready, 1)

            with pe.Fori(0, G) as i:
                r = round1(i)
                keys_values(i, r)
                expert_weights(i, r)
                chunk_scores(i, r, 0)
                chunk_scores(i, r, 1)
                expert_hidden(i, r, 0)
                chunk_scores(i, r, 2)
                chunk_scores(i, r, 3)
                expert_hidden(i, r, 1)
                chunk_out(i, r)
                expert_out(i, r, 0)
                expert_out(i, r, 1)
            for name in POST1.names[:4]:
                k, c = int(name[2]) // NCH, int(name[2]) % NCH
                g = free1(post1, name)
                pe.wait_ge(y_step, YSTEPS * (4 * c + 4))
                transposes(g, [o1[:, 4 * c + t, k * P:(k + 1) * P] for t in range(4)], ident[:]).then_inc(r_ready, 1)
            for c in range(4):
                g = free1(post1, f"PO{c}")
                pe.wait_ge(r_dve, post1.read(f"OT{2 + c // 2}"))
                for t in range(2):
                    q = (2 * c + t) * P
                    for k in range(KT):
                        for n_ in range(2):
                            last = mm(g[:, t * D:(t + 1) * D], nT[n_][:, k, q:q + P], p1T[:, k, :], start=(k == 0 and n_ == 0),
                                      stop=(k == KT - 1 and n_ == 1))
                last.then_inc(r_ready, 1)


_INS = ["L0_attn_x", "L0_attn_W_K", "L0_attn_W_Q", "L0_attn_W_V", "L0_attn_W_O", "L0_ffn_w_fc", "L0_ffn_w_proj",
        "L1_attn_qkv_w", "L1_attn_qkv_norm_w", "L1_attn_proj_w", "L1_attn_proj_norm_w", "L1_attn_norm_w", "L1_attn_s",
        "L1_ffn_gate_weight", "L1_ffn_gate_up_proj", "L1_ffn_down_proj", "L1_ffn_merge_groups", "L1_ffn_dominant_experts"]
_OUTS = [((1, 1024, 256), "float32")]


def kernel(**inputs):
    import numpy as _np
    import concourse.bacc as _bacc
    from concourse import mybir as _mybir
    from concourse.bass_utils import run_bass_kernel_spmd as _run

    nc = _bacc.Bacc("TRN2", target_bir_lowering=False, num_devices=1)
    arrays, args = {}, []
    for name in _INS:
        a = _np.ascontiguousarray(inputs[name])
        arrays[f"in_{name}_dram"] = a
        args.append(nc.dram_tensor(f"in_{name}_dram", a.shape, _mybir.dt.from_np(a.dtype), kind="ExternalInput").ap())
    for i, (shape, dtype) in enumerate(_OUTS):
        dt = _mybir.dt.from_np(_np.dtype(dtype))
        args.append(nc.dram_tensor(f"out_{i}_dram", shape, dt, kind="ExternalOutput").ap())
    transformer_kernel(nc, *args)
    r = _run(nc, [arrays], core_ids=[0])
    return r.results[0]["out_0_dram"]
```
